# Optimizing a Trainium2 kernel written in Bass

```python
import numpy as np
import jax
import jax.numpy as jnp

def _softmax(x, axis=-1):
    return jax.nn.softmax(x, axis=axis)

def _gelu(x):
    return jax.nn.gelu(x, approximate=True)

def _silu(x):
    return jax.nn.silu(x)

def _sigmoid(x):
    return jax.nn.sigmoid(x)

def _layernorm(x, axis=-1, eps=1e-05):
    m = jnp.mean(x, axis=axis, keepdims=True)
    v = jnp.var(x, axis=axis, keepdims=True)
    return (x - m) / jnp.sqrt(v + eps)

def _scatter_add(tgt, idx, src, axis=0):
    return tgt.at[idx].add(src)

def _segment_sum(src, seg, n):
    return jax.ops.segment_sum(src, seg, n)
kernel_name = 'mk_decoder_preln_d1_seqx_r8_af3353'

def setup_inputs(seed: int=0):
    np.random.seed(seed)
    _w = jnp.asarray

    def _rec_inputs():
        import jax
        import jax.numpy as jnp
        _rk = jax.random.key(seed)
        x = -0.0002928 + 1 * jax.random.normal(jax.random.fold_in(_rk, 1), (32, 64, 256), jnp.float32)
        _lenS = 64 - jax.random.randint(jax.random.fold_in(_rk, 7), (32,), 0, max(1, 64 // 4) + 1, jnp.int32)
        _lenS2 = 64 - jax.random.randint(jax.random.fold_in(_rk, 8), (32,), 0, max(1, 64 // 4) + 1, jnp.int32)
        _ctx_512P = jax.random.normal(jax.random.fold_in(_rk, 11), (32, 16, 64), jnp.float32)
        _ctx_512c = jax.random.dirichlet(jax.random.fold_in(_rk, 511), 0.3 * jnp.ones((16,), jnp.float32), (32, 64))
        _ctx_512t = jnp.einsum('bsk,bkd->bsd', _ctx_512c, _ctx_512P)
        _ctx_512t = _ctx_512t * jax.lax.rsqrt(jnp.mean(jnp.square(_ctx_512t)) + 1e-12) * 0.953939
        ctx_512 = 0.000227908 + 0.99994 * (_ctx_512t + 0.3 * jax.random.normal(jax.random.fold_in(_rk, 611), (32, 64, 64), jnp.float32))
        return (x, ctx_512)
    x, ctx_512 = _rec_inputs()

    def _L0_attn_setup():
        import jax, jax.numpy as jnp
        import numpy as np
        import math
        B_, T_, D_INNER, D_STATE, DT_RANK, K_ = (2, 128, 256, 16, 128, 4)
        LOG_EPS = math.log(1e-38)

        def _ssm_core(x, conv_w, conv_b, x_proj_w, dt_proj_w, dt_proj_b, A_log, D_param):
            Bb, T, d_inner = x.shape
            d_state = A_log.shape[1]
            dt_rank = dt_proj_w.shape[1]
            k = conv_w.shape[-1]
            xc = jax.lax.conv_general_dilated(x.transpose(0, 2, 1), conv_w, window_strides=(1,), padding=[(k - 1, 0)], dimension_numbers=('NCH', 'OIH', 'NCH'), feature_group_count=d_inner)
            xc = (xc + conv_b[None, :, None]).transpose(0, 2, 1)
            xc = jax.nn.silu(xc)
            proj = xc @ x_proj_w.T
            dt_raw = proj[..., :dt_rank]
            B_ssm = proj[..., dt_rank:dt_rank + d_state]
            C_ssm = proj[..., dt_rank + d_state:]
            dt = jax.nn.softplus(dt_raw @ dt_proj_w.T + dt_proj_b)
            A = -jnp.exp(A_log)
            log_dA = jnp.maximum(dt[..., None] * A, LOG_EPS)
            dBx = dt[..., None] * B_ssm[:, :, None, :] * xc[..., None]
            log_dBx = jnp.log(jnp.maximum(dBx, 1e-38))
            flat = d_inner * d_state
            a_star = jnp.cumsum(log_dA.reshape(Bb, T, flat), axis=1)
            log_h = a_star + jax.lax.cumlogsumexp(log_dBx.reshape(Bb, T, flat) - a_star, axis=1)
            h = jnp.exp(log_h).reshape(Bb, T, d_inner, d_state)
            y = jnp.einsum('bts,btds->btd', C_ssm, h) + D_param * xc
            return y
        key = jax.random.key(seed)
        ks = jax.random.split(key, 6)
        x = jax.random.normal(ks[0], (B_, T_, D_INNER), dtype=jnp.float32)
        conv_w = jax.random.normal(ks[1], (D_INNER, 1, K_), dtype=jnp.float32) * (1.0 / math.sqrt(K_))
        conv_b = jax.random.normal(ks[2], (D_INNER,), dtype=jnp.float32) * 0.02
        x_proj_w = jax.random.normal(ks[3], (DT_RANK + 2 * D_STATE, D_INNER), dtype=jnp.float32) * 0.02
        dt_proj_w = jax.random.normal(ks[4], (D_INNER, DT_RANK), dtype=jnp.float32) * (1.0 / math.sqrt(DT_RANK))
        dt_proj_b = jax.random.uniform(ks[5], (D_INNER,), dtype=jnp.float32, minval=math.log(0.001), maxval=math.log(0.1))
        A_log = jnp.broadcast_to(jnp.log(jnp.arange(1, D_STATE + 1, dtype=jnp.float32))[None, :], (D_INNER, D_STATE)).copy()
        D_param = jnp.ones((D_INNER,), dtype=jnp.float32)
        return {'x': x, 'conv_w': conv_w, 'conv_b': conv_b, 'x_proj_w': x_proj_w, 'dt_proj_w': dt_proj_w, 'dt_proj_b': dt_proj_b, 'A_log': A_log, 'D_param': D_param}
    _L0_attn_all = _L0_attn_setup()
    _L0_attn_in = {k: v for k, v in _L0_attn_all.items() if k in ('conv_w', 'conv_b', 'x_proj_w', 'dt_proj_w', 'dt_proj_b', 'A_log', 'D_param')}
    del _L0_attn_all

    def _L0_xattn_setup():
        import jax, jax.numpy as jnp
        import numpy as np
        B, S, L = (2, 128, 128)
        DIM_Q, H, K, D_C, D_CQ, R = (256, 16, 128, 64, 192, 64)

        def _rope_tables(length, dim):
            inv = 1.0 / 10000.0 ** (jnp.arange(0, dim, 2, dtype=jnp.float32) / dim)
            f = jnp.arange(length, dtype=jnp.float32)[:, None] * inv[None, :]
            sin = jnp.repeat(jnp.sin(f), 2, axis=-1)
            cos = jnp.repeat(jnp.cos(f), 2, axis=-1)
            return (sin, cos)

        def _rotate_half(x):
            half = x.shape[-1] // 2
            return jnp.concatenate([-x[..., half:], x[..., :half]], axis=-1)

        def _apply_rope(x, sin, cos):
            return x * cos + _rotate_half(x) * sin
        key = jax.random.key(seed)
        ks = jax.random.split(key, 8)
        return {'hidden_q': jax.random.normal(ks[0], (B, S, DIM_Q), jnp.float32), 'kv_c': jax.random.normal(ks[1], (B, L, D_C), jnp.float32), 'Wq': jax.random.normal(ks[2], (H * K, DIM_Q), jnp.float32) / np.sqrt(DIM_Q).astype(np.float32), 'w_kc_q': jax.random.normal(ks[3], (H, K, D_CQ), jnp.float32) / np.sqrt(K).astype(np.float32), 'w_kc_kv': jax.random.normal(ks[4], (H, K, D_C), jnp.float32) / np.sqrt(K).astype(np.float32), 'W_qr': jax.random.normal(ks[5], (H, D_CQ, R), jnp.float32) / np.float32(np.sqrt(D_CQ) * np.sqrt(R)), 'W_kr': jax.random.normal(ks[6], (H, D_C, R), jnp.float32) / np.sqrt(D_C).astype(np.float32), 'Wo': jax.random.normal(ks[7], (DIM_Q, H * K), jnp.float32) / np.sqrt(H * K).astype(np.float32)}
    _L0_xattn_all = _L0_xattn_setup()
    _L0_xattn_in = {k: v for k, v in _L0_xattn_all.items() if k in ('Wq', 'w_kc_q', 'w_kc_kv', 'W_qr', 'W_kr', 'Wo')}
    del _L0_xattn_all

    def _L0_ffn_setup():
        import jax, jax.numpy as jnp
        import numpy as np
        B, S, D = (2, 256, 256)
        E, H, TOP_K = (8, 176, 2)
        SH = 176
        ROUTED_SCALE = 2.5
        key = jax.random.key(seed)
        ks = jax.random.split(key, 8)
        std = 0.02
        return {'x': jax.random.normal(ks[0], (B, S, D), jnp.float32), 'gate_w': jax.random.normal(ks[1], (E, D), jnp.float32) * std, 'w1': jax.random.normal(ks[2], (E, D, H), jnp.float32) * std, 'w3': jax.random.normal(ks[3], (E, D, H), jnp.float32) * std, 'w2': jax.random.normal(ks[4], (E, H, D), jnp.float32) * std, 'sw1': jax.random.normal(ks[5], (D, SH), jnp.float32) * std, 'sw3': jax.random.normal(ks[6], (D, SH), jnp.float32) * std, 'sw2': jax.random.normal(ks[7], (SH, D), jnp.float32) * std}
    _L0_ffn_all = _L0_ffn_setup()
    _L0_ffn_in = {k: v for k, v in _L0_ffn_all.items() if k in ('gate_w', 'w1', 'w2', 'w3', 'sw1', 'sw2', 'sw3')}
    del _L0_ffn_all
    return {'x': x, 'ctx_512': ctx_512, 'L0_attn_conv_w': _L0_attn_in['conv_w'], 'L0_attn_conv_b': _L0_attn_in['conv_b'], 'L0_attn_x_proj_w': _L0_attn_in['x_proj_w'], 'L0_attn_dt_proj_w': _L0_attn_in['dt_proj_w'], 'L0_attn_dt_proj_b': _L0_attn_in['dt_proj_b'], 'L0_attn_A_log': _L0_attn_in['A_log'], 'L0_attn_D_param': _L0_attn_in['D_param'], 'L0_xattn_Wq': _L0_xattn_in['Wq'], 'L0_xattn_w_kc_q': _L0_xattn_in['w_kc_q'], 'L0_xattn_w_kc_kv': _L0_xattn_in['w_kc_kv'], 'L0_xattn_W_qr': _L0_xattn_in['W_qr'], 'L0_xattn_W_kr': _L0_xattn_in['W_kr'], 'L0_xattn_Wo': _L0_xattn_in['Wo'], 'L0_ffn_gate_w': _L0_ffn_in['gate_w'], 'L0_ffn_w1': _L0_ffn_in['w1'], 'L0_ffn_w2': _L0_ffn_in['w2'], 'L0_ffn_w3': _L0_ffn_in['w3'], 'L0_ffn_sw1': _L0_ffn_in['sw1'], 'L0_ffn_sw2': _L0_ffn_in['sw2'], 'L0_ffn_sw3': _L0_ffn_in['sw3']}

def reference(x, ctx_512, L0_attn_conv_w, L0_attn_conv_b, L0_attn_x_proj_w, L0_attn_dt_proj_w, L0_attn_dt_proj_b, L0_attn_A_log, L0_attn_D_param, L0_xattn_Wq, L0_xattn_w_kc_q, L0_xattn_w_kc_kv, L0_xattn_W_qr, L0_xattn_W_kr, L0_xattn_Wo, L0_ffn_gate_w, L0_ffn_w1, L0_ffn_w2, L0_ffn_w3, L0_ffn_sw1, L0_ffn_sw2, L0_ffn_sw3):
    import jax
    import jax.numpy as jnp

    def _L0_attn_ref(x, conv_w, conv_b, x_proj_w, dt_proj_w, dt_proj_b, A_log, D_param):
        import jax, jax.numpy as jnp
        import numpy as np
        import math
        B_, T_, D_INNER, D_STATE, DT_RANK, K_ = (2, 128, 256, 16, 128, 4)
        LOG_EPS = math.log(1e-38)

        def _ssm_core(x, conv_w, conv_b, x_proj_w, dt_proj_w, dt_proj_b, A_log, D_param):
            Bb, T, d_inner = x.shape
            d_state = A_log.shape[1]
            dt_rank = dt_proj_w.shape[1]
            k = conv_w.shape[-1]
            xc = jax.lax.conv_general_dilated(x.transpose(0, 2, 1), conv_w, window_strides=(1,), padding=[(k - 1, 0)], dimension_numbers=('NCH', 'OIH', 'NCH'), feature_group_count=d_inner)
            xc = (xc + conv_b[None, :, None]).transpose(0, 2, 1)
            xc = jax.nn.silu(xc)
            proj = xc @ x_proj_w.T
            dt_raw = proj[..., :dt_rank]
            B_ssm = proj[..., dt_rank:dt_rank + d_state]
            C_ssm = proj[..., dt_rank + d_state:]
            dt = jax.nn.softplus(dt_raw @ dt_proj_w.T + dt_proj_b)
            A = -jnp.exp(A_log)
            log_dA = jnp.maximum(dt[..., None] * A, LOG_EPS)
            dBx = dt[..., None] * B_ssm[:, :, None, :] * xc[..., None]
            log_dBx = jnp.log(jnp.maximum(dBx, 1e-38))
            flat = d_inner * d_state
            a_star = jnp.cumsum(log_dA.reshape(Bb, T, flat), axis=1)
            log_h = a_star + jax.lax.cumlogsumexp(log_dBx.reshape(Bb, T, flat) - a_star, axis=1)
            h = jnp.exp(log_h).reshape(Bb, T, d_inner, d_state)
            y = jnp.einsum('bts,btds->btd', C_ssm, h) + D_param * xc
            return y
        return _ssm_core(x, conv_w, conv_b, x_proj_w, dt_proj_w, dt_proj_b, A_log, D_param)

    def _L0_xattn_ref(hidden_q, kv_c, Wq, w_kc_q, w_kc_kv, W_qr, W_kr, Wo):
        import jax, jax.numpy as jnp
        import numpy as np
        B, S, L = (2, 128, 128)
        DIM_Q, H, K, D_C, D_CQ, R = (256, 16, 128, 64, 192, 64)

        def _rope_tables(length, dim):
            inv = 1.0 / 10000.0 ** (jnp.arange(0, dim, 2, dtype=jnp.float32) / dim)
            f = jnp.arange(length, dtype=jnp.float32)[:, None] * inv[None, :]
            sin = jnp.repeat(jnp.sin(f), 2, axis=-1)
            cos = jnp.repeat(jnp.cos(f), 2, axis=-1)
            return (sin, cos)

        def _rotate_half(x):
            half = x.shape[-1] // 2
            return jnp.concatenate([-x[..., half:], x[..., :half]], axis=-1)

        def _apply_rope(x, sin, cos):
            return x * cos + _rotate_half(x) * sin
        Bv, Sv, _ = hidden_q.shape
        _, Lv, _ = kv_c.shape
        q_hk = (hidden_q @ Wq.T).reshape(Bv, Sv, H, K)
        q_big = jnp.einsum('bshk,hkq->bshq', q_hk, w_kc_q)
        sin_q, cos_q = _rope_tables(Sv, D_CQ)
        q_big = _apply_rope(q_big, sin_q[None, :, None, :], cos_q[None, :, None, :])
        sin_k, cos_k = _rope_tables(Lv, D_C)
        kv_r = _apply_rope(kv_c, sin_k[None], cos_k[None])
        q_r = jnp.einsum('bshq,hqr->bhsr', q_big, W_qr)
        k_r = jnp.einsum('bld,hdr->bhlr', kv_r, W_kr)
        scores = jnp.einsum('bhsr,bhlr->bhsl', q_r, k_r)
        attn = jax.nn.softmax(scores, axis=-1)
        ctx_c = jnp.einsum('bhsl,bld->bhsd', attn, kv_r)
        ctx_lat = jnp.einsum('bhsd,hkd->bhsk', ctx_c, w_kc_kv)
        ctx = ctx_lat.transpose(0, 2, 1, 3).reshape(Bv, Sv, H * K)
        return ctx @ Wo.T

    def _L0_ffn_ref(x, gate_w, w1, w2, w3, sw1, sw2, sw3):
        import jax, jax.numpy as jnp
        import numpy as np
        B, S, D = (2, 256, 256)
        E, H, TOP_K = (8, 176, 2)
        SH = 176
        ROUTED_SCALE = 2.5
        b, s, d = x.shape
        xt = x.reshape(b * s, d)
        scores = jax.nn.sigmoid(xt @ gate_w.T)
        top_scores, top_idx = jax.lax.top_k(scores, TOP_K)
        top_scores = top_scores / (jnp.sum(top_scores, axis=-1, keepdims=True) + 1e-20)
        top_scores = top_scores * ROUTED_SCALE
        combine = jnp.sum(jax.nn.one_hot(top_idx, E, dtype=xt.dtype) * top_scores[..., None], axis=1)
        h = jnp.einsum('td,edh->eth', xt, w1)
        u = jnp.einsum('td,edh->eth', xt, w3)
        y = jnp.einsum('eth,ehd->etd', jax.nn.silu(h) * u, w2)
        routed = jnp.einsum('etd,te->td', y, combine)
        shared = jax.nn.silu(xt @ sw1) * (xt @ sw3) @ sw2
        return (routed + shared).reshape(b, s, d)
    x = x + _L0_attn_ref(_layernorm(x, axis=-1), L0_attn_conv_w, L0_attn_conv_b, L0_attn_x_proj_w, L0_attn_dt_proj_w, L0_attn_dt_proj_b, L0_attn_A_log, L0_attn_D_param)
    x = x + _L0_xattn_ref(_layernorm(x, axis=-1), ctx_512, L0_xattn_Wq, L0_xattn_w_kc_q, L0_xattn_w_kc_kv, L0_xattn_W_qr, L0_xattn_W_kr, L0_xattn_Wo)
    x = x + _L0_ffn_ref(_layernorm(x, axis=-1), L0_ffn_gate_w, L0_ffn_w1, L0_ffn_w2, L0_ffn_w3, L0_ffn_sw1, L0_ffn_sw2, L0_ffn_sw3)
    return x

_drawn_inputs = setup_inputs


def setup_inputs(seed=0):
    import zlib

    import numpy as np

    out = dict(_drawn_inputs(seed))
    spreads = {'L0_attn_D_param': (1.0, 0.6)}
    factors = {'L0_attn_conv_b': 5.163,
     'L0_attn_x_proj_w': 8.0,
     'L0_attn_dt_proj_w': 8.0,
     'L0_attn_dt_proj_b': 8.0,
     'L0_attn_A_log': 8.0,
     'L0_ffn_gate_w': 3.344,
     'L0_ffn_w1': 2.922,
     'L0_ffn_w2': 2.887,
     'L0_ffn_w3': 2.884,
     'L0_ffn_sw1': 5.174,
     'L0_ffn_sw2': 5.125,
     'L0_ffn_sw3': 5.135}
    for name, (base, spread) in spreads.items():
        noise = np.random.default_rng([zlib.crc32(name.encode()), seed]).standard_normal(out[name].shape)
        drawn = base * np.exp(spread * noise) if base else spread * noise
        out[name] = jnp.asarray(drawn.astype(out[name].dtype))
    for name, factor in factors.items():
        out[name] = (out[name] * factor).astype(out[name].dtype)
    return out
```

```python
import numpy as np
import concourse.bass as bass
import concourse.mybir as mybir
from contextlib import ExitStack

P = 128
D = 256
KD = D // P
T_ALL, SEQ = 2048, 64
GT = 512
NG = T_ALL // GT
TT = GT // P
NB = GT // SEQ
NBP = NB // 2
NS, RANK, TAPS = 16, 128, 4
H, DC, DQ, R = 16, 64, 192, 64
HP = H // 2
QT = 2 * DQ // P
E, HID = 8, 176
MT = -(-((E + 1) * HID) // P)
RING = 3
LOG_FLOOR = 1e-38
EPS = 1e-5

UNITS_AFTER_PAIR = [0, 0, 1, 1, 1, 1, 2, 2]
UNITS_AFTER_TILE = [1, 0, 1, 0, 1, 0, 1, 1, 0, 1, 0, 1, 1]
assert sum(UNITS_AFTER_PAIR) + sum(UNITS_AFTER_TILE) == NS

LN_VAR, LN_OUT = 10, 18
CONV_N = KD * TAPS
SP_M, SP_DT, SP_N = 1, 12, 13
SMALL = 1 / 64
SPLIT_N = 4
UNIT_N = 4
TAIL_YT, TAIL_X1, TAIL_N = 2, 4, 4
KV_N = 5
PROD_N = 2 * QT
SM_SUB, SM_N = 2, 4
GATE_N = 29
FFN_N = 2


def before(g, per, s, depth):
    return g * per + max(0, s + 1 - depth)


CREDIT = {"sync": {"out_done": 16},
          "tensor": dict.fromkeys(["pe_hu", "pe_ctx", "pe_sc", "pe_w2", "pe_qp", "pe_at", "pe_comb", "pe_y",
                                   "pe_qb"], 1),
          "scalar": dict.fromkeys(["act_g", "act_hq", "act_b"], 1),
          "gpsimd": dict.fromkeys(["pool_at", "pool_act", "pool_hc", "kv"], 1),
          "vector": dict.fromkeys(["x2_ready", "ffn", "unit", "tail"], 1)}
CREDIT_OF = {name: c for names in CREDIT.values() for name, c in names.items()}


class Sems(dict):

    def at(self, name, n):
        return self[name], n + CREDIT_OF.get(name, 0)


class Steps:

    def __init__(self, eng, s, name, per):
        self.eng, self.s, self.name, self.per, self.k, self.base = eng, s, name, per, 0, 0

    def start(self, round_):
        assert self.k in (0, self.per), (self.k, self.per)
        self.base, self.k = round_ * self.per, 0
        return self

    def mark(self, instruction):
        self.k += 1
        instruction.then_inc(self.s[self.name], 1)

    def at(self, k):
        return self.s.at(self.name, self.base + k)

    def link(self, instruction):
        self.mark(instruction)
        self.eng.wait_ge(*self.at(self.k))


def build(nc, a, out):
    f32, bf16 = mybir.dt.float32, mybir.dt.bfloat16
    ALU, ACT, AX = mybir.AluOpType, mybir.ActivationFunctionType, mybir.AxisListType
    ctx = ExitStack()
    with ctx:
        def sb(name, shape, dt=f32):
            return ctx.enter_context(nc.sbuf_tensor(name, shape, dt))

        def sem(name):
            return ctx.enter_context(nc.semaphore(name))

        ident = sb("ident", [P, P])
        sel_bc = sb("sel_bc", [96, 2 * NS, P], bf16)
        sel_comb = sb("sel_comb", [96, MT, P], bf16)
        rope_q = sb("rope_q", [P, 2, QT, SEQ])
        rope_k = sb("rope_k", [P, 2, DC])
        conv_w = sb("conv_w", [P, KD, TAPS])
        vecs = sb("vecs", [P, 3, KD])
        conv_b, dt_b, d_par = vecs[:, 0, :], vecs[:, 1, :], vecs[:, 2, :]
        a_neg = sb("a_neg", [P, KD, NS])
        xp_dt = sb("xp_dt", [P, KD, RANK])
        xp_bc = sb("xp_bc", [P, KD, 96])
        dtw = sb("dtw", [RANK, D])
        gate_w = sb("gate_w", [P, KD, E])
        prio = sb("prio", [P, E])
        minus_half = sb("minus_half", [P, TT])
        wf = sb("wf", [P, KD, H * DQ])
        n_mat = sb("n_mat", [P, HP, 2, 4, DC])
        u_mat = sb("u_mat", [P, HP, D])
        w2 = sb("w2", [P, MT, D])
        w13 = sb("w13", [P, RING, 2, KD, P])

        x_raw = sb("x_raw", [P, TT, D])
        x1 = sb("x1", [P, TT, D])
        x2 = sb("x2", [P, TT, D])
        ln_stats = [sb(f"ln_stats{k}", [P, TT, 6]) for k in range(3)]
        ln_mv = [sb(f"ln_mv{k}", [P, TT, 2]) for k in range(3)]
        ln_s = [sb(f"ln_s{k}", [P, 3, TT]) for k in range(3)]

        conv_in = sb("conv_in", [P, KD, NB, SEQ + TAPS - 1])
        xc = sb("xc", [P, KD, GT])
        dt_ = sb("dt", [P, KD, GT])
        u = sb("u", [P, KD, GT])
        da = sb("da", [P, 2, KD, GT])
        v = sb("v", [P, KD, GT])
        h = sb("h", [P, KD, GT])
        hc = sb("hc", [P, 2, KD, GT])
        b_sb = sb("b_sb", [P, 2, GT])
        c_sb = sb("c_sb", [P, 2, GT])
        bc_parts = sb("bc_parts", [96, GT], bf16)
        xn1 = h[:, :, :].rearrange("p k t -> p (k t)").rearrange("p (t d) -> p t d", t=TT)
        acc = v
        th_c = hc[:, 0]
        dt_raw = b_sb[:, 0, :]
        bc_hi = sb("bc_hi", [96, GT], bf16)
        bc_r = b_sb[0:96, 1, :]
        zs = hc[:, 1]
        sp_e = h
        sp_ln = v
        sp_c = hc[:, 0]
        yt = v
        xn2 = h[:, :, :].rearrange("p k t -> p (k t)").rearrange("p (t d) -> p t d", t=TT)

        hq = sb("hq", [P, KD, GT])
        kr = sb("kr", [P, NB, DC])
        kr_t = sb("kr_t", [P, NB, DC])
        bd = sb("bd", [P, NB, P])
        kb = sb("kb", [P, NB, P])

        region = sb("region", [P, 9728])
        at = [0]

        def part(n, start=None):
            if start is not None:
                at[0] = start
            s = region[:, at[0]:at[0] + n]
            at[0] += n
            assert at[0] <= 9728, at[0]
            return s

        wq_in = part(H * D, 0).rearrange("p (h d) -> p h d", h=H)
        wkq_in = part(H * DQ).rearrange("p (h d) -> p h d", h=H)
        wo_in = part(H * D, 0).rearrange("p (h d) -> p h d", h=H)
        wkv_in = part(H * DC).rearrange("p (h d) -> p h d", h=H)
        wkr_in = part(H * DC).rearrange("p (h d) -> p h d", h=H)
        wqr_in = part(H * DQ).rearrange("p (h d) -> p h d", h=H)
        prod = part(QT * 2 * GT, 0).rearrange("p (t c n) -> p t c n", t=QT, c=2)
        ctx_t = part(HP * GT).rearrange("p (h n) -> p h n", h=HP)
        qp = part(GT)
        sh = part(GT).rearrange("p (g l) -> p g l", l=SEQ)
        ex = part(GT).rearrange("p (g l) -> p g l", l=SEQ)
        at_t = part(GT).rearrange("p (b s) -> p b s", b=NBP)
        sm_s = sb("sm_s", [P, 3, NB])
        act_h = part(MT * GT, 0).rearrange("p (m n) -> p m n", m=MT)
        x3t = part(KD * GT).rearrange("p (k n) -> p k n", k=KD)
        th_f = part(2 * GT).rearrange("p (k n) -> p k n", k=2)
        xn3 = region[:, 11 * GT:13 * GT].rearrange("p (t d) -> p t d", t=TT)
        gw = part(2 * GT).rearrange("p (k n) -> p k n", k=2)
        gt = [sb(f"gt{k}", [P, TT, E]) for k in range(7)]
        g_s = sb("g_s", [P, 8, TT])
        g_bf = sb("g_bf", [P, 2, TT, E], bf16)
        comb = sb("comb", [P, TT, 96])
        comb_t = sb("comb_t", [96, GT], bf16)

        bank = [ctx.enter_context(nc.psum_tensor(f"bank{i}", [P, GT], f32)) for i in range(8)]
        px, y_ps = bank[0], [bank[1], bank[2]]
        q_ps, r2, r3 = [bank[3], bank[4], bank[5]], bank[6], bank[7]
        hu_ps = [(bank[3], bank[4]), (bank[5], bank[6])]

        names = """ld_const ld_mix ld_prep1 ld_prep2 ld_w2 ld_x ld_c ld_w13_0 ld_w13_1 ld_w13_2 out_done
            mem_set a_ready conv_scaled ln1 ln2 ln3 pow1 pow2 pow3
            pe_x1t act_conv_in conv act_tanh xc_ready pe_proj act_dt_raw act_bc_hi act_bc_part bc_split
            pe_z act_z softplus act_e act_ln pe_bc act_c act_b act_da unit pool_hc pe_y
            tail pe_yt pe_x2t act_hq
            kv pe_kv act_kb pe_qb prod_done pe_qp act_qp pe_sc softmax act_ex pool_at pe_at act_at pe_ctx
            act_ctx pe_wo x2_ready pe_x3t act_x3t pe_logit act_ge gate pe_comb act_comb pe_hu pe_g act_tf
            ffn act_g pool_act pe_w2 pe_prep1 pe_prep2 pe_prep3 prep1_out prep2_out prep3_out""".split()
        s = Sems((n, sem(n)) for n in names)

        block = ctx.enter_context(nc.Block())

        LN_SEM = [("ln1", "pow1"), ("ln2", "pow2"), ("ln3", "pow3")]

        @block.sync
        def _(sp):
            for name, c in CREDIT["sync"].items():
                sp.sem_inc(s[name], c)
            def load(name, dst, src):
                sp.dma_start(dst, src).then_inc(s[name], 16)

            def load_x(g):
                sp.wait_ge(*s.at("tail", g * TAIL_N))
                load("ld_x", x_raw[:, :, :], a["x"][bass.ds(g * GT, GT), :].rearrange("(n p) d -> p n d", p=P))

            def load_ctx(g):
                sp.wait_ge(*s.at("kv", g * KV_N))
                src = a["ctx"][bass.ds(g * GT, GT), :].rearrange("(b l) d -> l b d", l=SEQ)
                for dup in range(2):
                    load("ld_c", kr[dup * SEQ:(dup + 1) * SEQ, :, :], src)

            def stream_w13(g):
                for m in range(MT):
                    sp.wait_ge(*s.at("pe_hu", before(g, MT, m, RING)))
                    load(f"ld_w13_{m % RING}", w13[:, m % RING], a["w13"][m])

            load_x(0)
            load("ld_const", ident[:, :], a["ident"])
            load("ld_mix", conv_w[:, :, :], a["conv_w"])
            load("ld_mix", vecs[:, :, :], a["vecs"])
            load("ld_mix", a_neg[:, :, :], a["a_log"])
            load("ld_mix", xp_dt[:, :, :], a["xp_dt"])
            load("ld_mix", xp_bc[:, :, :], a["xp_bc"])
            load("ld_mix", dtw[:, :], a["dtw"])
            load("ld_mix", sel_bc[:, :, :], a["sel_bc"])
            load("ld_const", rope_k[:, :, :], a["rope_k"])
            load("ld_const", rope_q[:, :, :, :], a["rope_q"])
            load("ld_const", sel_comb[:, :, :], a["sel_comb"])
            load("ld_const", gate_w[:, :, :], a["gate_w"])
            load("ld_const", prio[:, :], a["prio"])
            load_ctx(0)
            load("ld_prep1", wq_in, a["wq"])
            load("ld_prep1", wkq_in, a["wkq"])
            load("ld_w2", w2[:, :, :], a["w2"])
            sp.wait_ge(*s.at("pe_prep1", H))
            load("ld_prep2", wo_in, a["wo"])
            load("ld_prep2", wkv_in, a["wkv"])
            load("ld_prep2", wkr_in[0:R], a["wkr"])
            load("ld_prep2", wkr_in[R:2 * R], a["wkr"])
            load("ld_prep2", wqr_in, a["wqr"])

            def store(g):
                sp.wait_ge(*s.at("x2_ready", (g + 1) * 4))
                sp.dma_start(out[bass.ds(g * GT, GT), :].rearrange("(n p) d -> p n d", p=P),
                             x2[:, :, :]).then_inc(s["out_done"], 16)

            with sp.Fori(0, NG - 1) as i:
                load_x(i + 1)
                stream_w13(i)
                load_ctx(i + 1)
                store(i)
            stream_w13(NG - 1)
            store(NG - 1)
            sp.wait_ge(*s.at("out_done", 16 * NG))

        @block.gpsimd
        def _(pool):
            for name, c in CREDIT["gpsimd"].items():
                pool.sem_inc(s[name], c)
            for k, (t, val) in enumerate([
                    (conv_in[:, :, :, 0:TAPS - 1], 0.0),
                    (minus_half[:, :], -0.5),
                    (bd[0:SEQ, :, SEQ:], 0.0), (bd[SEQ:, :, 0:SEQ], 0.0),
                    (da[:, :, :, 0:GT:SEQ], 0.0),
                    (n_mat[:, :, :, 1:3, :], 0.0),
                    (comb[:, :, :], 0.0)]):
                nc.gpsimd.memset(t, val).then_inc(s["mem_set"], 1)
                pool.wait_ge(*s.at("mem_set", k + 1))
            nc.gpsimd.memset(comb[:, :, E:E + 1], 0.5).then_inc(s["mem_set"], 1)
            pool.wait_ge(*s.at("mem_set", 8))

            def rstd(k, g):
                dve_sem, pool_sem = LN_SEM[k]
                pool.wait_ge(*s.at(dve_sem, g * LN_OUT + LN_VAR))
                nc.gpsimd.tensor_tensor(ln_s[k][:, 1, :], ln_s[k][:, 0, :], minus_half[:, :],
                                        ALU.pow).then_inc(s[pool_sem], 1)

            kv = Steps(pool, s, "kv", KV_N)

            def rope_keys(g):
                kv.start(g)
                pool.wait_ge(*s.at("ld_c", (g + 1) * 32))
                pool.wait_ge(*s.at("pe_ctx", g * HP))
                cos = rope_k[:, 0:1, :].to_broadcast([P, NB, DC])
                for lo in (0, DC // 2):
                    hi = DC // 2 - lo
                    kv.mark(nc.gpsimd.tensor_tensor(
                        kr_t[:, :, lo:lo + DC // 2], kr[:, :, hi:hi + DC // 2],
                        rope_k[:, 1:2, lo:lo + DC // 2].to_broadcast([P, NB, DC // 2]), ALU.mult))
                pool.wait_ge(*kv.at(2))
                kv.link(nc.gpsimd.tensor_tensor(kr[:, :, :], kr[:, :, :], cos, ALU.mult))
                for rows, cols in ((slice(0, SEQ), slice(0, DC)), (slice(SEQ, P), slice(DC, P))):
                    kv.link(nc.gpsimd.tensor_tensor(bd[rows, :, cols], kr[rows], kr_t[rows], ALU.add))

            def unit(g, n):
                pool.wait_ge(*s.at("unit", (g * NS + n) * UNIT_N + 4))
                pool.wait_ge(*s.at("act_c", g * NS + n + 1))
                pool.wait_ge(*s.at("pe_y", before(g, NS, n, 2)))
                c = c_sb[:, n % 2:n % 2 + 1, :].to_broadcast([P, KD, GT])
                nc.gpsimd.tensor_tensor(hc[:, n % 2], h[:, :, :], c, ALU.mult).then_inc(s["pool_hc"], 1)

            def norm(g, p):
                n = g * HP + p
                pool.wait_ge(*s.at("softmax", n * SM_N + SM_N))
                inv = sm_s[:, 2, :].unsqueeze(2).to_broadcast([P, NB, SEQ])
                nc.gpsimd.tensor_tensor(sh, ex, inv, ALU.mult).then_inc(s["pool_at"], 1)

            def ffn_tile(g, m):
                n = g * MT + m
                pool.wait_ge(*s.at("ffn", (n + 1) * FFN_N))
                pool.wait_ge(*s.at("act_g", n + 1))
                nc.gpsimd.tensor_tensor(act_h[:, m, :], th_f[:, m % 2, :], gw[:, m % 2, :],
                                        ALU.mult).then_inc(s["pool_act"], 1)

            pool.wait_ge(*s.at("ld_const", 96))
            rstd(0, 0)
            rope_keys(0)
            for n in range(NS):
                unit(0, n)
            rstd(1, 0)

            def body(g, ahead):
                n = 0
                if ahead:
                    rstd(0, g + 1)
                for p in range(HP):
                    norm(g, p)
                    for _ in range(UNITS_AFTER_PAIR[p] if ahead else 0):
                        unit(g + 1, n)
                        n += 1
                rstd(2, g)
                for m in range(MT):
                    ffn_tile(g, m)
                    for _ in range(UNITS_AFTER_TILE[m] if ahead else 0):
                        unit(g + 1, n)
                        n += 1
                if ahead:
                    rstd(1, g + 1)
                    rope_keys(g + 1)

            with pool.Fori(0, NG - 1) as i:
                body(i, True)
            body(NG - 1, False)

        @block.scalar
        def _(act):
            for name, c in CREDIT["scalar"].items():
                act.sem_inc(s[name], c)
            def evict(dst, src, name):
                nc.scalar.activation(dst, src, ACT.Copy).then_inc(s[name], 1)

            act.wait_ge(*s.at("ld_mix", 7 * 16))
            nc.scalar.activation(a_neg[:, :, :], a_neg[:, :, :], ACT.Exp).then_inc(s["a_ready"], 1)

            def front_conv_in(g):
                act.wait_ge(*s.at("pe_x1t", g + 1))
                for k in range(KD):
                    evict(conv_in[:, k, :, TAPS - 1:], y_ps[k][:, :].rearrange("p (b t) -> p b t", b=NB),
                          "act_conv_in")

            def front_tanh(g):
                act.wait_ge(*s.at("conv", (g + 1) * CONV_N))
                nc.scalar.activation(th_c, acc[:, :, :], ACT.Tanh).then_inc(s["act_tanh"], 1)

            def front_proj(g):
                act.wait_ge(*s.at("pe_proj", 2 * g + 1))
                evict(dt_raw, px[:, :], "act_dt_raw")
                act.wait_ge(*s.at("pe_proj", 2 * g + 2))
                evict(bc_hi[:, :], y_ps[0][0:96, :], "act_bc_hi")
                evict(bc_parts[0:32, :], y_ps[0][0:32, :], "act_bc_part")

            def front_z(g):
                act.wait_ge(*s.at("pe_z", g + 1))
                for k in range(KD):
                    nc.scalar.activation(zs[:, k, :], y_ps[k][:, :], ACT.Identity,
                                         bias=dt_b[:, k:k + 1]).then_inc(s["act_z"], 1)

            def front_log(g):
                act.wait_ge(*s.at("softplus", g * SP_N + SP_M))
                nc.scalar.activation(sp_e[:, :, :], sp_e[:, :, :], ACT.Exp).then_inc(s["act_e"], 1)
                act.wait_ge(*s.at("act_e", g + 1))
                nc.scalar.activation(sp_ln[:, :, :], sp_e[:, :, :], ACT.Ln, bias=1.0).then_inc(s["act_ln"], 1)

            def unit(g, n):
                act.wait_ge(*s.at("unit", before(g, NS, n, 2) * UNIT_N))
                if n == 0:
                    act.wait_ge(*s.at("softplus", g * SP_N + SP_DT))
                for k in range(KD):
                    dst = da[:, n % 2, k, :].rearrange("p (b t) -> p b t", b=NB)[:, :, 1:]
                    src = dt_[:, k, :].rearrange("p (b t) -> p b t", b=NB)[:, :, 1:]
                    nc.scalar.activation(dst, src, ACT.Exp, scale=a_neg[:, k, n:n + 1]).then_inc(s["act_da"], 1)
                act.wait_ge(*s.at("pe_bc", (g * NS + n) * 2 + 1))
                act.wait_ge(*s.at("pool_hc", before(g, NS, n, 2)))
                evict(c_sb[:, n % 2, :], px[:, :], "act_c")
                act.wait_ge(*s.at("pe_bc", (g * NS + n) * 2 + 2))
                evict(b_sb[:, n % 2, :], px[:, :], "act_b")

            def tail_hq(g):
                act.wait_ge(*s.at("pe_x2t", g + 1))
                act.wait_ge(*s.at("pe_qb", g * HP * QT))
                for k in range(KD):
                    evict(hq[:, k, :], y_ps[k][:, :], "act_hq")

            def keys(g):
                act.wait_ge(*s.at("pe_kv", g + 1))
                act.wait_ge(*s.at("pe_sc", g * HP))
                for k, b in enumerate((r2, r3)):
                    evict(kb[:, 4 * k:4 * k + 4, :], b[:, :].rearrange("p (b c) -> p b c", c=P), "act_kb")

            def pair_qp(g, p):
                n = g * HP + p
                act.wait_ge(*s.at("pe_qp", n + 1))
                act.wait_ge(*s.at("pe_sc", n))
                evict(qp, r2[:, :], "act_qp")

            def pair_at(g, p):
                n = g * HP + p
                act.wait_ge(*s.at("pe_at", n + 1))
                act.wait_ge(*s.at("pe_ctx", n))
                evict(at_t, r3[:, :].rearrange("p (b s) -> p b s", b=NBP), "act_at")

            def pair_exp(g, p):
                n = g * HP + p
                act.wait_ge(*s.at("softmax", n * SM_N + SM_SUB))
                act.wait_ge(*s.at("pool_at", n))
                nc.scalar.activation(ex, sh, ACT.Exp).then_inc(s["act_ex"], 1)

            def pair_ctx(g, p):
                n = g * HP + p
                act.wait_ge(*s.at("pe_ctx", n + 1))
                if p == 0:
                    act.wait_ge(*s.at("pe_w2", g))
                evict(ctx_t[:, p, :], r3[:, :], "act_ctx")

            def ffn_tile(g, m):
                n = g * MT + m
                act.wait_ge(*s.at("pe_hu", n + 1))
                act.wait_ge(*s.at("pool_act", before(g, MT, m, 2)))
                nc.scalar.activation(th_f[:, m % 2, :], hu_ps[m % 2][0][:, :], ACT.Tanh,
                                     scale=0.5).then_inc(s["act_tf"], 1)

            def ffn_gate(g, m):
                n = g * MT + m
                act.wait_ge(*s.at("pe_g", n + 1))
                act.wait_ge(*s.at("pool_act", before(g, MT, m, 2)))
                evict(gw[:, m % 2, :], r3[:, :], "act_g")

            act.wait_ge(*s.at("a_ready", 1))
            nc.scalar.mul(a_neg[:, :, :], a_neg[:, :, :], -1.0).then_inc(s["a_ready"], 1)
            act.wait_ge(*s.at("a_ready", 2))
            front_conv_in(0)
            front_tanh(0)
            front_proj(0)
            front_z(0)
            front_log(0)
            for hd in range(H):
                act.wait_ge(*s.at("pe_prep1", hd + 1))
                for k in range(KD):
                    evict(wf[:, k, hd * DQ:(hd + 1) * DQ], bank[3 + hd % 2][:, k * DQ:(k + 1) * DQ], "prep1_out")
            for p in range(HP):
                act.wait_ge(*s.at("pe_prep2", p + 1))
                if p == 0:
                    act.wait_ge(*s.at("mem_set", 8))
                for c in range(2):
                    src = bank[3 + 2 * c + p % 2][:, 0:4 * DC].rearrange("p (b d) -> p b d", b=4)
                    evict(n_mat[:, p, c, 0:4:3, :], src[:, 0:4:3, :], "prep2_out")
                    for b, rows in ((1, slice(0, SEQ)), (2, slice(SEQ, P))):
                        evict(n_mat[rows, p, c, b, :], src[rows, b, :], "prep2_out")
            for p in range(HP):
                act.wait_ge(*s.at("pe_prep3", p + 1))
                evict(u_mat[:, p, :], bank[5 + p % 2][:, 0:D], "prep3_out")

            act.wait_ge(*s.at("mem_set", 8))
            for n in range(NS):
                unit(0, n)
            tail_hq(0)

            def body(g, ahead):
                n = 0
                keys(g)
                for p in range(HP):
                    pair_qp(g, p)
                    if p:
                        pair_at(g, p - 1)
                    if ahead and p == 0:
                        front_conv_in(g + 1)
                    pair_exp(g, p)
                    if ahead and p == 0:
                        front_tanh(g + 1)
                    if ahead and p == 1:
                        front_proj(g + 1)
                    if p:
                        pair_ctx(g, p - 1)
                    if ahead and p == 1:
                        front_z(g + 1)
                        front_log(g + 1)
                    for _ in range(UNITS_AFTER_PAIR[p] if ahead else 0):
                        unit(g + 1, n)
                        n += 1
                pair_at(g, HP - 1)
                pair_ctx(g, HP - 1)
                act.wait_ge(*s.at("pe_x3t", g + 1))
                for k in range(KD):
                    evict(x3t[:, k, :], q_ps[k][:, :], "act_x3t")
                act.wait_ge(*s.at("pe_logit", g + 1))
                nc.scalar.activation(gt[0][:, :, :], r3[:, 0:TT * E].rearrange("p (t e) -> p t e", e=E),
                                     ACT.Exp, scale=-1.0).then_inc(s["act_ge"], 1)
                for m in range(MT):
                    ffn_tile(g, m)
                    if m == 1:
                        act.wait_ge(*s.at("pe_comb", g + 1))
                        evict(comb_t[:, :], r3[0:96, :], "act_comb")
                    if m:
                        ffn_gate(g, m - 1)
                    for _ in range(UNITS_AFTER_TILE[m] if ahead else 0):
                        unit(g + 1, n)
                        n += 1
                ffn_gate(g, MT - 1)
                if ahead:
                    tail_hq(g + 1)

            with act.Fori(0, NG - 1) as i:
                body(i, True)
            body(NG - 1, False)

        @block.vector
        def _(dve):
            for name, c in CREDIT["vector"].items():
                dve.sem_inc(s[name], c)
            V = nc.vector

            dve.wait_ge(*s.at("ld_mix", 7 * 16))
            V.tensor_scalar(conv_w[:, :, :], conv_w[:, :, :], 0.5, None, ALU.mult).then_inc(s["conv_scaled"], 1)
            V.tensor_scalar(conv_b, conv_b, 0.5, None, ALU.mult).then_inc(s["conv_scaled"], 1)
            dve.wait_ge(*s.at("conv_scaled", 2))
            dve.wait_ge(*s.at("mem_set", 8))

            ln = [Steps(dve, s, LN_SEM[k][0], LN_OUT) for k in range(3)]

            def layernorm(k, g, x, xn):
                st, mv, w = ln_stats[k], ln_mv[k], ln_s[k]
                step = ln[k].start(g)
                for t in range(TT):
                    step.mark(V.bn_stats(st[:, t, :], x[:, t, :]))
                dve.wait_ge(*step.at(TT))
                step.mark(V.memset(w[:, 2, :], 0.0))
                for t in range(TT):
                    step.mark(V.bn_aggr(mv[:, t, :], st[:, t, :]))
                dve.wait_ge(*step.at(2 * TT + 1))
                step.mark(V.tensor_scalar(w[:, 0, :], mv[:, :, 1], EPS, None, ALU.add))
                dve.wait_ge(*s.at(LN_SEM[k][1], g + 1))
                step.link(V.tensor_tensor(w[:, 2, :], w[:, 1, :], w[:, 1, :], ALU.mult))
                step.link(V.tensor_tensor(w[:, 2, :], w[:, 2, :], w[:, 0, :], ALU.mult))
                step.link(V.tensor_scalar(w[:, 2, :], w[:, 2, :], -0.5, 1.5, ALU.mult, ALU.add))
                step.link(V.tensor_tensor(w[:, 1, :], w[:, 2, :], w[:, 1, :], ALU.mult))
                for t in range(TT):
                    step.mark(V.tensor_scalar(xn[:, t, :], x[:, t, :], mv[:, t, 0:1], w[:, 1, t:t + 1],
                                              ALU.subtract, ALU.mult))

            def front_ln(g):
                dve.wait_ge(*s.at("ld_x", (g + 1) * 16))
                layernorm(0, g, x_raw, xn1)

            conv = Steps(dve, s, "conv", CONV_N)

            def front_conv(g):
                conv.start(g)
                dve.wait_ge(*s.at("act_conv_in", (g + 1) * KD))
                for j in range(TAPS):
                    for k in range(KD):
                        o = acc[:, k, :].rearrange("p (b t) -> p b t", b=NB)
                        i_ = conv_in[:, k, :, j:j + SEQ]
                        if j:
                            dve.wait_ge(*conv.at(KD * (j - 1) + k + 1))
                            conv.mark(V.scalar_tensor_tensor(out=o, in0=i_, scalar=conv_w[:, k, j:j + 1], in1=o,
                                                             op0=ALU.mult, op1=ALU.add))
                        else:
                            conv.mark(V.tensor_scalar(o, i_, conv_w[:, k, 0:1], conv_b[:, k:k + 1],
                                                      ALU.mult, ALU.add))
                dve.wait_ge(*s.at("act_tanh", g + 1))
                V.scalar_tensor_tensor(out=xc[:, :, :], in0=th_c, scalar=1.0, in1=acc[:, :, :],
                                       op0=ALU.add, op1=ALU.mult).then_inc(s["xc_ready"], 1)

            split = Steps(dve, s, "bc_split", SPLIT_N)
            soft = Steps(dve, s, "softplus", SP_N)

            def front_split(g):
                split.start(g)
                dve.wait_ge(*s.at("act_bc_hi", g + 1))
                dve.wait_ge(*s.at("act_bc_part", g + 1))
                split.link(V.tensor_tensor(bc_r, y_ps[0][0:96, :], bc_hi[:, :], ALU.subtract))
                split.mark(V.tensor_copy(bc_parts[32:64, :], bc_r[32:64, :]))
                split.link(V.tensor_copy(bc_hi[64:96, :], bc_r[64:96, :]))
                split.mark(V.tensor_tensor(bc_parts[64:96, :], bc_r[64:96, :], bc_hi[64:96, :], ALU.subtract))

            def front_abs(g):
                soft.start(g)
                dve.wait_ge(*s.at("act_z", (g + 1) * KD))
                soft.mark(V.scalar_tensor_tensor(out=sp_e[:, :, :], in0=zs, scalar=-1.0, in1=zs,
                                                 op0=ALU.mult, op1=ALU.min))

            def front_dt(g):
                dve.wait_ge(*s.at("act_e", g + 1))
                soft.link(V.tensor_scalar(sp_c, sp_e[:, :, :], 1.0, -1.0, ALU.add, ALU.add))
                soft.link(V.tensor_tensor(sp_c, sp_e[:, :, :], sp_c, ALU.subtract))
                dve.wait_ge(*s.at("act_ln", g + 1))
                soft.link(V.tensor_tensor(sp_c, sp_ln[:, :, :], sp_c, ALU.add))
                e, series = sp_e[:, :, :], u[:, :, :]
                soft.link(V.tensor_scalar(series, e, -1 / 4, 1 / 3, ALU.mult, ALU.add))
                soft.link(V.tensor_tensor(series, series, e, ALU.mult))
                for c in (-1 / 2, 1.0):
                    soft.link(V.scalar_tensor_tensor(out=series, in0=series, scalar=c, in1=e,
                                                     op0=ALU.add, op1=ALU.mult))
                soft.mark(V.scalar_tensor_tensor(out=series, in0=e, scalar=SMALL, in1=series,
                                                 op0=ALU.is_lt, op1=ALU.mult))
                soft.link(V.scalar_tensor_tensor(out=sp_c, in0=e, scalar=SMALL, in1=sp_c,
                                                 op0=ALU.is_ge, op1=ALU.mult))
                soft.link(V.tensor_tensor(sp_c, sp_c, series, ALU.add))
                soft.link(V.scalar_tensor_tensor(out=dt_[:, :, :], in0=zs, scalar=0.0, in1=sp_c,
                                                 op0=ALU.max, op1=ALU.add))
                soft.link(V.tensor_tensor(u[:, :, :], dt_[:, :, :], xc[:, :, :], ALU.mult))

            steps = Steps(dve, s, "unit", UNIT_N)

            def unit(g, n):
                steps.start(g * NS + n)
                dve.wait_ge(*s.at("act_b", g * NS + n + 1))
                b = b_sb[:, n % 2:n % 2 + 1, :].to_broadcast([P, KD, GT])
                steps.mark(V.tensor_tensor(v[:, :, :], u[:, :, :], b, ALU.mult))
                dve.wait_ge(*s.at("act_da", (g * NS + n + 1) * KD))
                d3 = da[:, n % 2].rearrange("p k (b t) -> p (k b) t", b=NB)[:, :, 1:]
                steps.mark(V.tensor_scalar(d3, d3, LOG_FLOOR, None, ALU.max))
                dve.wait_ge(*steps.at(1))
                steps.mark(V.tensor_scalar(v[:, :, :], v[:, :, :], LOG_FLOOR, None, ALU.max))
                dve.wait_ge(*steps.at(3))
                dve.wait_ge(*s.at("pool_hc", before(g, NS, n, 1)))
                steps.link(V.tensor_tensor_scan(h[:, :, :].rearrange("p k t -> p (k t)"),
                                                da[:, n % 2].rearrange("p k t -> p (k t)"),
                                                v[:, :, :].rearrange("p k t -> p (k t)"),
                                                0.0, ALU.mult, ALU.add))

            tail_s = Steps(dve, s, "tail", TAIL_N)

            def tail(g):
                tail_s.start(g)
                dve.wait_ge(*s.at("pe_y", (g + 1) * NS))
                for k in range(KD):
                    tail_s.mark(V.scalar_tensor_tensor(out=yt[:, k, :], in0=xc[:, k, :], scalar=d_par[:, k:k + 1],
                                                       in1=y_ps[k][:, :], op0=ALU.mult, op1=ALU.add))
                dve.wait_ge(*s.at("pe_yt", g + 1))
                for j in range(2):
                    tail_s.mark(V.tensor_tensor(x1[:, 2 * j:2 * j + 2, :], x_raw[:, 2 * j:2 * j + 2, :],
                                                y_ps[j][:, :].rearrange("p (t d) -> p t d", t=2), ALU.add))
                dve.wait_ge(*tail_s.at(TAIL_X1))
                layernorm(1, g, x1, xn2)

            def products(g, p):
                n = g * HP + p
                if p == 0:
                    dve.wait_ge(*s.at("pe_w2", g))
                dve.wait_ge(*s.at("pe_qp", n))
                for t in range(QT):
                    dve.wait_ge(*s.at("pe_qb", n * QT + t + 1))
                    for c in range(2):
                        tab = rope_q[:, c, t, :].unsqueeze(1).to_broadcast([P, NB, SEQ])
                        V.tensor_tensor(prod[:, t, c, :].rearrange("p (b s) -> p b s", b=NB),
                                        q_ps[t][:, :].rearrange("p (b s) -> p b s", b=NB), tab,
                                        ALU.mult).then_inc(s["prod_done"], 1)

            sm = Steps(dve, s, "softmax", SM_N)

            def softmax_shift(g, p):
                n = g * HP + p
                sm.start(n)
                dve.wait_ge(*s.at("pe_sc", n + 1))
                sc = r2[:, :].rearrange("p (g l) -> p g l", l=SEQ)
                sm.link(V.tensor_reduce(sm_s[:, 0, :], sc, axis=AX.X, op=ALU.max))
                dve.wait_ge(*s.at("pe_at", n))
                mx = sm_s[:, 0, :].unsqueeze(2).to_broadcast([P, NB, SEQ])
                sm.mark(V.tensor_tensor(sh, sc, mx, ALU.subtract))

            def softmax_sum(g, p):
                n = g * HP + p
                dve.wait_ge(*s.at("act_ex", n + 1))
                sm.link(V.tensor_reduce(sm_s[:, 1, :], ex, axis=AX.X, op=ALU.add))
                dve.wait_ge(*s.at("pool_at", n))
                sm.link(V.reciprocal(sm_s[:, 2, :], sm_s[:, 1, :]))

            gate = Steps(dve, s, "gate", GATE_N)

            def route(g):
                gate.start(g)
                tiny = lambda k: g_s[:, k, :]
                wide = lambda k: g_s[:, k, :].unsqueeze(2).to_broadcast([P, TT, E])
                pr = prio[:, :].unsqueeze(1).to_broadcast([P, TT, E])
                step, tt = gate.link, V.tensor_tensor
                dve.wait_ge(*s.at("act_ge", g + 1))
                step(V.tensor_scalar(gt[1][:, :, :], gt[0][:, :, :], 1.0, None, ALU.add))
                step(V.reciprocal(gt[2][:, :, :], gt[1][:, :, :]))
                left = gt[2]
                for k, hot in ((0, gt[3]), (1, gt[4])):
                    step(V.tensor_reduce(tiny(k), left[:, :, :], axis=AX.X, op=ALU.max))
                    step(tt(hot[:, :, :], left[:, :, :], wide(k), ALU.is_equal))
                    step(tt(hot[:, :, :], hot[:, :, :], pr, ALU.mult))
                    step(V.tensor_reduce(tiny(2), hot[:, :, :], axis=AX.X, op=ALU.max))
                    step(tt(hot[:, :, :], hot[:, :, :], wide(2), ALU.is_equal))
                    if k == 0:
                        step(V.scalar_tensor_tensor(out=gt[5][:, :, :], in0=hot[:, :, :], scalar=-2.0,
                                                    in1=left[:, :, :], op0=ALU.mult, op1=ALU.add))
                        left = gt[5]
                step(tt(tiny(3), tiny(0), tiny(1), ALU.add))
                step(V.tensor_scalar(tiny(3), tiny(3), 1e-20, None, ALU.add))
                step(V.reciprocal(tiny(4), tiny(3)))
                for k in range(2):
                    step(tt(tiny(5 + k), tiny(k), tiny(4), ALU.mult))
                    step(V.tensor_scalar(tiny(5 + k), tiny(5 + k), 1.25, None, ALU.mult))
                    step(tt(gt[3 + k][:, :, :], gt[3 + k][:, :, :], wide(5 + k), ALU.mult))
                step(tt(gt[6][:, :, :], gt[3][:, :, :], gt[4][:, :, :], ALU.add))
                step(V.tensor_copy(g_bf[:, 0], gt[6][:, :, :]))
                step(tt(gt[1][:, :, :], gt[6][:, :, :], g_bf[:, 0], ALU.subtract))
                dve.wait_ge(*s.at("pe_comb", g))
                gate_hi = V.tensor_copy(comb[:, :, 0:E], g_bf[:, 0])
                gate.mark(gate_hi)
                gate.link(V.tensor_copy(g_bf[:, 1], gt[1][:, :, :]))
                return tt

            def route_parts(g):
                gate.mark(V.tensor_copy(comb[:, :, 32:32 + E], g_bf[:, 1]))
                gate.mark(V.tensor_tensor(comb[:, :, 64:64 + E], gt[1][:, :, :], g_bf[:, 1], ALU.subtract))

            f = Steps(dve, s, "ffn", FFN_N)

            def ffn_tile(g, m):
                f.start(g * MT + m)
                dve.wait_ge(*s.at("act_tf", g * MT + m + 1))
                hb, ub = hu_ps[m % 2]
                th = th_f[:, m % 2, :]
                f.link(V.scalar_tensor_tensor(out=th, in0=th, scalar=1.0, in1=hb[:, :], op0=ALU.add, op1=ALU.mult))
                f.mark(V.tensor_tensor(th, th, ub[:, :], ALU.mult))

            front_ln(0)
            front_conv(0)
            front_split(0)
            front_abs(0)
            front_dt(0)
            for n in range(NS):
                unit(0, n)
            tail(0)

            def body(g, ahead):
                n = 0
                products(g, 0)
                if ahead:
                    front_ln(g + 1)
                for p in range(HP):
                    softmax_shift(g, p)
                    if p + 1 < HP:
                        products(g, p + 1)
                    if ahead and p == 2:
                        front_dt(g + 1)
                    softmax_sum(g, p)
                    if ahead and p == 0:
                        front_conv(g + 1)
                    if ahead and p == 1:
                        front_split(g + 1)
                        front_abs(g + 1)
                    for _ in range(UNITS_AFTER_PAIR[p] if ahead else 0):
                        unit(g + 1, n)
                        n += 1
                dve.wait_ge(*s.at("pe_wo", g + 1))
                dve.wait_ge(*s.at("out_done", g * 16))
                for j in range(2):
                    V.tensor_tensor(x2[:, 2 * j:2 * j + 2, :], x1[:, 2 * j:2 * j + 2, :],
                                    q_ps[j][:, :].rearrange("p (t d) -> p t d", t=2),
                                    ALU.add).then_inc(s["x2_ready"], 1)
                dve.wait_ge(*s.at("x2_ready", g * 4 + 2))
                layernorm(2, g, x2, xn3)
                route(g)
                route_parts(g)
                for m in range(MT):
                    ffn_tile(g, m)
                    for _ in range(UNITS_AFTER_TILE[m] if ahead else 0):
                        unit(g + 1, n)
                        n += 1
                if ahead:
                    tail(g + 1)
                dve.wait_ge(*s.at("pe_w2", g + 1))
                for j, b in enumerate((q_ps[2], r2)):
                    V.tensor_tensor(x2[:, 2 * j:2 * j + 2, :], x2[:, 2 * j:2 * j + 2, :],
                                    b[:, :].rearrange("p (t d) -> p t d", t=2), ALU.add).then_inc(s["x2_ready"], 1)

            with dve.Fori(0, NG - 1) as i:
                body(i, True)
            body(NG - 1, False)

        @block.tensor
        def _(pe):
            for name, c in CREDIT["tensor"].items():
                pe.sem_inc(s[name], c)
            mm = nc.tensor.matmul

            def group(b, pairs, name=None):
                for i_, (l, r) in enumerate(pairs):
                    last = mm(b, l, r, start=i_ == 0, stop=i_ == len(pairs) - 1)
                if name:
                    last.then_inc(s[name], 1)

            def to_channels(xn, banks, name):
                for k in range(KD):
                    for t in range(TT):
                        last = nc.tensor.transpose(banks[k][:, t * P:(t + 1) * P], xn[:, t, k * P:(k + 1) * P],
                                                   ident[:, :])
                last.then_inc(s[name], 1)

            def front_x1t(g):
                pe.wait_ge(*s.at("ln1", (g + 1) * LN_OUT))
                pe.wait_ge(*s.at("act_hq", g * KD))
                to_channels(xn1, y_ps, "pe_x1t")

            def front_proj(g):
                pe.wait_ge(*s.at("xc_ready", g + 1))
                pe.wait_ge(*s.at("act_conv_in", (g + 1) * KD))
                pe.wait_ge(*s.at("act_b", g * NS))
                group(px[:, :], [(xp_dt[:, k, :], xc[:, k, :]) for k in range(KD)], "pe_proj")
                group(y_ps[0][0:96, :], [(xp_bc[:, k, :], xc[:, k, :]) for k in range(KD)], "pe_proj")

            def front_z(g):
                pe.wait_ge(*s.at("act_dt_raw", g + 1))
                pe.wait_ge(*s.at("act_bc_part", g + 1))
                pe.wait_ge(*s.at("bc_split", g * SPLIT_N + 1))
                for k in range(KD):
                    group(y_ps[k][:, :], [(dtw[:, k * P:(k + 1) * P], dt_raw)], "pe_z" if k == KD - 1 else None)

            def y_sum(g, n):
                pe.wait_ge(*s.at("pool_hc", g * NS + n + 1))
                if n == 0:
                    pe.wait_ge(*s.at("act_z", (g + 1) * KD))
                for k in range(KD):
                    last = mm(y_ps[k][:, :], ident[:, :], hc[:, n % 2, k, :], start=n == 0, stop=n == NS - 1)
                last.then_inc(s["pe_y"], 1)

            def unit(g, n):
                if n == 0:
                    pe.wait_ge(*s.at("bc_split", (g + 1) * SPLIT_N))
                    pe.wait_ge(*s.at("act_dt_raw", g + 1))
                pe.wait_ge(*s.at("act_b", before(g, NS, n, 1)))
                group(px[:, :], [(sel_bc[:, NS + n, :], bc_parts[:, :])], "pe_bc")
                if n:
                    y_sum(g, n - 1)
                pe.wait_ge(*s.at("act_c", g * NS + n + 1))
                group(px[:, :], [(sel_bc[:, n, :], bc_parts[:, :])], "pe_bc")

            def tail_yt(g):
                pe.wait_ge(*s.at("tail", g * TAIL_N + TAIL_YT))
                for t in range(TT):
                    for k in range(KD):
                        at_ = (t % 2) * D + k * P
                        last = nc.tensor.transpose(y_ps[t // 2][:, at_:at_ + P], yt[:, k, t * P:(t + 1) * P],
                                                   ident[:, :])
                last.then_inc(s["pe_yt"], 1)

            def tail_x2t(g):
                pe.wait_ge(*s.at("ln2", (g + 1) * LN_OUT))
                to_channels(xn2, y_ps, "pe_x2t")

            def keys(g):
                pe.wait_ge(*s.at("kv", (g + 1) * KV_N))
                pe.wait_ge(*s.at("x2_ready", g * 4))
                pe.wait_ge(*s.at("act_g", g * MT))
                for b in range(NB):
                    last = nc.tensor.transpose((r2, r3)[b // 4][:, (b % 4) * P:(b % 4 + 1) * P], bd[:, b, :],
                                               ident[:, :])
                last.then_inc(s["pe_kv"], 1)

            def query(g, p):
                n = g * HP + p
                if p == 0:
                    pe.wait_ge(*s.at("act_hq", (g + 1) * KD))
                    pe.wait_ge(*s.at("x2_ready", g * 4))
                    pe.wait_ge(*s.at("ffn", g * MT * FFN_N))
                for t in range(QT):
                    if p:
                        pe.wait_ge(*s.at("prod_done", (n - 1) * PROD_N + 2 * t + 2))
                    c = (p * QT + t) * P
                    group(q_ps[t][:, :], [(wf[:, k, c:c + P], hq[:, k, :]) for k in range(KD)], "pe_qb")

            def latent_query(g, p):
                n = g * HP + p
                pe.wait_ge(*s.at("prod_done", (n + 1) * PROD_N))
                if p:
                    pe.wait_ge(*s.at("softmax", (n - 1) * SM_N + SM_SUB))
                else:
                    pe.wait_ge(*s.at("act_kb", (g + 1) * 2))
                todo = [(t, c) for t in range(2) for c in range(2)]
                for i_, (t, c) in enumerate(todo):
                    for hd in range(2):
                        blk, tile = (t, t) if hd == 0 else (2 + t, 1 + t)
                        last = mm(r2[hd * DC:(hd + 1) * DC, :], n_mat[:, p, c, blk, :], prod[:, tile, c, :],
                                  start=i_ == 0, stop=i_ == len(todo) - 1)
                last.then_inc(s["pe_qp"], 1)

            def scores(g, p):
                n = g * HP + p
                pe.wait_ge(*s.at("act_qp", n + 1))
                if p == 0:
                    pe.wait_ge(*s.at("act_kb", (g + 1) * 2))
                for bp in range(NBP):
                    for o in range(2):
                        b = 2 * bp + o
                        last = mm(r2[o * SEQ:(o + 1) * SEQ, bp * P:(bp + 1) * P], qp[:, b * SEQ:(b + 1) * SEQ],
                                  kb[:, b, :], start=bp == 0, stop=bp == NBP - 1, skip_group_check=True)
                last.then_inc(s["pe_sc"], 1)

            def weights_t(g, p):
                n = g * HP + p
                pe.wait_ge(*s.at("pool_at", n + 1))
                if p:
                    pe.wait_ge(*s.at("act_ctx", n))
                w = sh.rearrange("p (b h) l -> p b (h l)", b=NBP)
                for bp in range(NBP):
                    last = nc.tensor.transpose(r3[:, bp * P:(bp + 1) * P], w[:, bp, :], ident[:, :])
                last.then_inc(s["pe_at"], 1)

            def context(g, p):
                n = g * HP + p
                pe.wait_ge(*s.at("act_at", n + 1))
                for b in range(NB):
                    last = mm(r3[:, b * SEQ:(b + 1) * SEQ], bd[:, b, :],
                              at_t[:, b // 2, (b % 2) * SEQ:(b % 2 + 1) * SEQ],
                              start=b == 0, stop=b == NB - 1, skip_group_check=True)
                last.then_inc(s["pe_ctx"], 1)

            def project(g, p):
                pe.wait_ge(*s.at("act_ctx", g * HP + p + 1))
                if p == 0:
                    pe.wait_ge(*s.at("prod_done", (g + 1) * HP * PROD_N))
                for t in range(TT):
                    last = mm(q_ps[t // 2][:, (t % 2) * D:(t % 2 + 1) * D], ctx_t[:, p, t * P:(t + 1) * P],
                              u_mat[:, p, :], start=p == 0 and t % 2 == 0, stop=p == HP - 1,
                              skip_group_check=True)
                if p == HP - 1:
                    last.then_inc(s["pe_wo"], 1)

            def ffn_up(g, m):
                n = g * MT + m
                slot = m % RING
                pe.wait_ge(*s.at(f"ld_w13_{slot}", (g * len(range(slot, MT, RING)) + m // RING + 1) * 16))
                if m == 0:
                    pe.wait_ge(*s.at("act_x3t", (g + 1) * KD))
                if m >= 2:
                    pe.wait_ge(*s.at("ffn", (n - 1) * FFN_N))
                for w, b in enumerate(hu_ps[m % 2]):
                    group(b[:, :], [(w13[:, m % RING, w, k, :], x3t[:, k, :]) for k in range(KD)],
                          "pe_hu" if w else None)

            def ffn_gate(g, m):
                n = g * MT + m
                if m:
                    pe.wait_ge(*s.at("act_g", n))
                else:
                    pe.wait_ge(*s.at("act_comb", g + 1))
                group(r3[:, :], [(sel_comb[:, m, :], comb_t[:, :])], "pe_g")

            def ffn_down(g, m):
                n = g * MT + m
                pe.wait_ge(*s.at("pool_act", n + 1))
                if m == 0:
                    pe.wait_ge(*s.at("ffn", (g + 1) * MT * FFN_N))
                for t in range(TT):
                    last = mm((q_ps[2], r2)[t // 2][:, (t % 2) * D:(t % 2 + 1) * D], act_h[:, m, t * P:(t + 1) * P],
                              w2[:, m, :], start=m == 0 and t % 2 == 0, stop=m == MT - 1, skip_group_check=True)
                if m == MT - 1:
                    last.then_inc(s["pe_w2"], 1)

            pe.wait_ge(*s.at("ld_const", 96))
            pe.wait_ge(*s.at("ld_mix", 7 * 16))
            front_x1t(0)
            front_proj(0)
            front_z(0)

            pe.wait_ge(*s.at("ld_prep1", 32))
            for hd in range(H):
                if hd >= 2:
                    pe.wait_ge(*s.at("prep1_out", (hd - 1) * KD))
                for k in range(KD):
                    last = mm(bank[3 + hd % 2][:, k * DQ:(k + 1) * DQ], wq_in[:, hd, k * P:(k + 1) * P],
                              wkq_in[:, hd, :], start=k == 0, stop=k == KD - 1, skip_group_check=True)
                last.then_inc(s["pe_prep1"], 1)
            pe.wait_ge(*s.at("ld_prep2", 5 * 16))
            pe.wait_ge(*s.at("prep1_out", H * KD))
            for p in range(HP):
                if p >= 2:
                    pe.wait_ge(*s.at("prep2_out", (p - 1) * 6))
                for c in range(2):
                    rows = slice(c * R, (c + 1) * R)
                    wqr = wqr_in[rows, 2 * p:2 * p + 2, :].rearrange("p h q -> p (h q)")
                    for blk, (tile, hd) in enumerate(((0, 0), (1, 0), (1, 1), (2, 1))):
                        last = mm(bank[3 + 2 * c + p % 2][:, blk * DC:(blk + 1) * DC],
                                  wqr[:, tile * P:(tile + 1) * P], wkr_in[rows, 2 * p + hd, :],
                                  start=blk == 0, stop=blk == 3, skip_group_check=True)
                last.then_inc(s["pe_prep2"], 1)
            pe.wait_ge(*s.at("prep2_out", HP * 6))
            for p in range(HP):
                if p >= 2:
                    pe.wait_ge(*s.at("prep3_out", p - 1))
                for hd in range(2):
                    last = mm(bank[5 + p % 2][hd * DC:(hd + 1) * DC, 0:D], wkv_in[:, 2 * p + hd, :],
                              wo_in[:, 2 * p + hd, :], start=True, stop=True)
                last.then_inc(s["pe_prep3"], 1)
            for n in range(NS):
                unit(0, n)
            y_sum(0, NS - 1)
            tail_yt(0)
            tail_x2t(0)
            pe.wait_ge(*s.at("prep2_out", HP * 6))
            pe.wait_ge(*s.at("prep3_out", HP))
            pe.wait_ge(*s.at("ld_w2", 16))

            def body(g, ahead):
                n = 0
                query(g, 0)
                keys(g)
                for p in range(HP):
                    latent_query(g, p)
                    if p:
                        weights_t(g, p - 1)
                    scores(g, p)
                    if ahead and p == 0:
                        front_x1t(g + 1)
                    if ahead and p == 1:
                        front_proj(g + 1)
                    if p + 1 < HP:
                        query(g, p + 1)
                    if p:
                        context(g, p - 1)
                    if ahead and p == 1:
                        front_z(g + 1)
                    for _ in range(UNITS_AFTER_PAIR[p] if ahead else 0):
                        unit(g + 1, n)
                        n += 1
                for p in range(HP - 1):
                    project(g, p)
                weights_t(g, HP - 1)
                context(g, HP - 1)
                project(g, HP - 1)
                pe.wait_ge(*s.at("ln3", (g + 1) * LN_OUT))
                to_channels(xn3, q_ps, "pe_x3t")
                pe.wait_ge(*s.at("act_x3t", (g + 1) * KD))
                for t in range(TT):
                    for k in range(KD):
                        last = mm(r3[:, t * E:(t + 1) * E], x3t[:, k, t * P:(t + 1) * P], gate_w[:, k, :],
                                  start=(t, k) == (0, 0), stop=(t, k) == (TT - 1, KD - 1), skip_group_check=True)
                last.then_inc(s["pe_logit"], 1)
                for m in range(MT):
                    ffn_up(g, m)
                    if m == 1:
                        pe.wait_ge(*s.at("gate", (g + 1) * GATE_N))
                        for t in range(TT):
                            last = nc.tensor.transpose(r3[0:96, t * P:(t + 1) * P], comb[:, t, :], ident[:, :])
                        last.then_inc(s["pe_comb"], 1)
                    if m:
                        ffn_gate(g, m - 1)
                    for _ in range(UNITS_AFTER_TILE[m] if ahead else 0):
                        unit(g + 1, n)
                        n += 1
                ffn_gate(g, MT - 1)
                if ahead:
                    y_sum(g + 1, NS - 1)
                for m in range(MT):
                    ffn_down(g, m)
                    if ahead and m == 3:
                        tail_yt(g + 1)
                    if ahead and m == 9:
                        tail_x2t(g + 1)

            with pe.Fori(0, NG - 1) as i:
                body(i, True)
            body(NG - 1, False)


def rope_table(length, dim):
    inv = (1.0 / 10000.0 ** (np.arange(0, dim, 2, dtype=np.float32) / dim)).astype(np.float32)
    f = np.arange(length, dtype=np.float32)[:, None] * inv[None, :]
    return np.repeat(np.sin(f), 2, axis=-1), np.repeat(np.cos(f), 2, axis=-1)


def constants():
    sin_q, cos_q = rope_table(SEQ, DQ)
    sin_k, cos_k = rope_table(SEQ, DC)
    j = np.arange(QT * P) % DQ
    half = DQ // 2
    sin_t = (sin_q[:, (j + half) % DQ] * np.where(j < half, 1.0, -1.0)).T
    rope_q = np.stack([cos_q[:, j].T, sin_t]).reshape(2, QT, P, SEQ).transpose(2, 0, 1, 3)
    sign = np.where(np.arange(DC) < DC // 2, -1.0, 1.0)
    rope_k = np.tile(np.stack([cos_k, sin_k * sign], axis=1), (2, 1, 1))
    sel_bc = np.zeros((96, 2 * NS, P))
    sel_comb = np.zeros((96, MT * P))
    for part in range(3):
        for r in range(2 * NS):
            sel_bc[32 * part + r, r, :] = 1
        for e in range(E + 1):
            sel_comb[32 * part + e, e * HID:(e + 1) * HID] = 1
    f32 = np.float32
    return {"ident": np.eye(P, dtype=f32), "rope_q": rope_q.astype(f32), "rope_k": rope_k.astype(f32),
            "sel_bc": sel_bc.astype(np.dtype("bfloat16")),
            "sel_comb": sel_comb.reshape(96, MT, P).astype(np.dtype("bfloat16")),
            "prio": np.tile(np.arange(E, 0, -1, dtype=f32), (P, 1))}


def laid_out(x, ctx_512, L0_attn_conv_w, L0_attn_conv_b, L0_attn_x_proj_w, L0_attn_dt_proj_w, L0_attn_dt_proj_b,
             L0_attn_A_log, L0_attn_D_param, L0_xattn_Wq, L0_xattn_w_kc_q, L0_xattn_w_kc_kv, L0_xattn_W_qr,
             L0_xattn_W_kr, L0_xattn_Wo, L0_ffn_gate_w, L0_ffn_w1, L0_ffn_w2, L0_ffn_w3, L0_ffn_sw1, L0_ffn_sw2,
             L0_ffn_sw3):
    n = np.asarray

    def halves(w):
        return n(w).reshape(KD, P, -1).transpose(1, 0, 2)

    xp = halves(n(L0_attn_x_proj_w).T)
    bc = xp[:, :, RANK:]
    pad = MT * P - (E + 1) * HID

    def packed(w, sw):
        cols = np.concatenate([n(w).transpose(1, 0, 2).reshape(D, E * HID), n(sw),
                               np.zeros((D, pad), np.float32)], axis=1)
        return cols.reshape(KD, P, MT, P).transpose(2, 1, 0, 3)

    w2 = np.concatenate([n(L0_ffn_w2).reshape(E * HID, D), n(L0_ffn_sw2), np.zeros((pad, D), np.float32)])
    qr = n(L0_xattn_W_qr).transpose(2, 0, 1)
    return {
        "x": n(x).reshape(T_ALL, D), "ctx": n(ctx_512).reshape(T_ALL, DC),
        "conv_w": halves(n(L0_attn_conv_w).reshape(D, TAPS)),
        "vecs": np.stack([halves(L0_attn_conv_b)[:, :, 0], halves(L0_attn_dt_proj_b)[:, :, 0],
                          halves(L0_attn_D_param)[:, :, 0]], axis=1),
        "a_log": halves(L0_attn_A_log), "xp_dt": xp[:, :, :RANK], "xp_bc": np.concatenate([bc, bc, bc], axis=2),
        "dtw": n(L0_attn_dt_proj_w).T,
        "wq": n(L0_xattn_Wq).reshape(H, P, D).transpose(1, 0, 2), "wkq": n(L0_xattn_w_kc_q).transpose(1, 0, 2),
        "wo": n(L0_xattn_Wo).reshape(D, H, P).transpose(2, 1, 0), "wkv": n(L0_xattn_w_kc_kv).transpose(1, 0, 2),
        "wkr": n(L0_xattn_W_kr).transpose(2, 0, 1),
        "wqr": np.concatenate([qr, np.roll(qr, -(DQ // 2), axis=2)]),
        "gate_w": halves(n(L0_ffn_gate_w).T), "w2": w2.reshape(MT, P, D).transpose(1, 0, 2),
        "w13": np.stack([packed(L0_ffn_w1, L0_ffn_sw1), packed(L0_ffn_w3, L0_ffn_sw3)], axis=2),
    }


def kernel(**inputs):
    import concourse.bacc as bacc
    from concourse.bass_utils import run_bass_kernel_spmd

    arrays = {f"in_{k}": np.ascontiguousarray(v) for k, v in {**constants(), **laid_out(**inputs)}.items()}
    nc = bacc.Bacc("TRN2", target_bir_lowering=False, num_devices=1)
    aps = {k[3:]: nc.dram_tensor(k, v.shape, mybir.dt.from_np(v.dtype), kind="ExternalInput").ap()
           for k, v in arrays.items()}
    out = nc.dram_tensor("out", (T_ALL, D), mybir.dt.float32, kind="ExternalOutput").ap()
    build(nc, aps, out)
    r = run_bass_kernel_spmd(nc, [arrays], core_ids=[0])
    return r.results[0]["out"].reshape(T_ALL // SEQ, SEQ, D)
```

```python
import numpy as np
import concourse.bass as bass
import concourse.mybir as mybir
from contextlib import ExitStack

P = 128
D = 256
KD = D // P
T_ALL, SEQ = 2048, 64
GT = 512
NG = T_ALL // GT
TT = GT // P
NB = GT // SEQ
NBP = NB // 2
NS, RANK, TAPS = 16, 128, 4
H, DC, DQ, R = 16, 64, 192, 64
HP = H // 2
QT = 2 * DQ // P
E, HID = 8, 176
MT = -(-((E + 1) * HID) // P)
RING = 3
LOG_FLOOR = 1e-38
EPS = 1e-5

UNITS = [0, 0, 0, 0, 0, 2, 2, 2] + [1, 1, 1, 0, 1, 1, 0, 1, 1, 0, 1, 1, 1]
assert len(UNITS) == HP + MT and sum(UNITS) == NS


def states(step, ahead):
    first = sum(UNITS[:step])
    return range(first, first + UNITS[step]) if ahead else range(0)

LN_PARTS = (1, 1, 2)


def ln_var(k):
    return 2 * TT // LN_PARTS[k] + 2


def ln_out(k):
    return 3 * TT // LN_PARTS[k] + 6


CONV_N = KD * TAPS
SP_M, SP_DT, SP_N = 1, 12, 13
SMALL = 1 / 64
SPLIT_N = 4
UNIT_N = 4
TAIL_YT, TAIL_X1, TAIL_N = 2, 4, 4
KV_N = 5
PROD_N = 2 * QT
SM_SUB, SM_N = 2, 4
GATE_N = 29
FFN_N = 2


def before(g, per, s, depth):
    return g * per + max(0, s + 1 - depth)


CREDIT = {"sync": {"out_done": 16},
          "tensor": dict.fromkeys(["pe_hu", "pe_ctx", "pe_sc", "pe_w2", "pe_qp", "pe_at", "pe_comb", "pe_y",
                                   "pe_qb"], 1),
          "scalar": dict.fromkeys(["act_g", "act_hq", "act_c"], 1),
          "gpsimd": dict.fromkeys(["pool_at", "pool_act", "pool_hc", "kv"], 1),
          "vector": dict.fromkeys(["x2_ready", "ffn", "unit", "tail"], 1)}
CREDIT_OF = {name: c for names in CREDIT.values() for name, c in names.items()}


class Sems(dict):

    def at(self, name, n):
        return self[name], n + CREDIT_OF.get(name, 0)


class Steps:

    def __init__(self, eng, s, name, per):
        self.eng, self.s, self.name, self.per, self.k, self.base = eng, s, name, per, 0, 0

    def start(self, round_):
        assert self.k in (0, self.per), (self.k, self.per)
        self.base, self.k = round_ * self.per, 0
        return self

    def mark(self, instruction):
        self.k += 1
        instruction.then_inc(self.s[self.name], 1)

    def at(self, k):
        return self.s.at(self.name, self.base + k)

    def link(self, instruction):
        self.mark(instruction)
        self.eng.wait_ge(*self.at(self.k))


def build(nc, a, out):
    f32, bf16 = mybir.dt.float32, mybir.dt.bfloat16
    ALU, ACT, AX = mybir.AluOpType, mybir.ActivationFunctionType, mybir.AxisListType
    ctx = ExitStack()
    with ctx:
        def sb(name, shape, dt=f32):
            return ctx.enter_context(nc.sbuf_tensor(name, shape, dt))

        def sem(name):
            return ctx.enter_context(nc.semaphore(name))

        ident = sb("ident", [P, P])
        sel_bc = sb("sel_bc", [96, 2 * NS, P], bf16)
        sel_comb = sb("sel_comb", [96, MT, P], bf16)
        rope_q = sb("rope_q", [P, 2, QT, SEQ])
        rope_k = sb("rope_k", [P, 2, DC])
        conv_w = sb("conv_w", [P, KD, TAPS])
        vecs = sb("vecs", [P, 3, KD])
        conv_b, dt_b, d_par = vecs[:, 0, :], vecs[:, 1, :], vecs[:, 2, :]
        a_neg = sb("a_neg", [P, KD, NS])
        xp_dt = sb("xp_dt", [P, KD, RANK])
        xp_bc = sb("xp_bc", [P, KD, 96])
        dtw = sb("dtw", [RANK, D])
        gate_w = sb("gate_w", [P, KD, E])
        prio = sb("prio", [P, E])
        minus_half = sb("minus_half", [P, TT])
        wf = sb("wf", [P, KD, H * DQ])
        n_mat = sb("n_mat", [P, HP, 2, 4, DC])
        u_mat = sb("u_mat", [P, HP, D])
        w2 = sb("w2", [P, MT, D])
        w13 = sb("w13", [P, RING, 2, KD, P])

        x_raw = sb("x_raw", [P, TT, D])
        x1 = sb("x1", [P, TT, D])
        x2 = sb("x2", [P, TT, D])
        ln_stats = [sb(f"ln_stats{k}", [P, TT, 6]) for k in range(3)]
        ln_mv = [sb(f"ln_mv{k}", [P, TT, 2]) for k in range(3)]
        ln_s = [sb(f"ln_s{k}", [P, 3, TT]) for k in range(3)]

        conv_in = sb("conv_in", [P, KD, NB, SEQ + TAPS - 1])
        xc = sb("xc", [P, KD, GT])
        dt_ = sb("dt", [P, KD, GT])
        u = sb("u", [P, KD, GT])
        da = sb("da", [P, 2, KD, GT])
        v = sb("v", [P, KD, GT])
        h = sb("h", [P, KD, GT])
        hc = sb("hc", [P, 2, KD, GT])
        b_sb = sb("b_sb", [P, 2, GT])
        c_sb = sb("c_sb", [P, 2, GT])
        bc_parts = sb("bc_parts", [96, GT], bf16)
        xn1 = h[:, :, :].rearrange("p k t -> p (k t)").rearrange("p (t d) -> p t d", t=TT)
        acc = v
        th_c = hc[:, 0]
        dt_raw = b_sb[:, 0, :]
        bc_hi = sb("bc_hi", [96, GT], bf16)
        bc_r = b_sb[0:96, 1, :]
        zs = hc[:, 1]
        sp_e = h
        sp_ln = v
        sp_c = hc[:, 0]
        yt = v
        xn2 = h[:, :, :].rearrange("p k t -> p (k t)").rearrange("p (t d) -> p t d", t=TT)

        hq = sb("hq", [P, KD, GT])
        kr = sb("kr", [P, NB, DC])
        kr_t = sb("kr_t", [P, NB, DC])
        bd = sb("bd", [P, NB, P])
        kb = sb("kb", [P, NB, P])

        region = sb("region", [P, 9728])
        at = [0]

        def part(n, start=None):
            if start is not None:
                at[0] = start
            s = region[:, at[0]:at[0] + n]
            at[0] += n
            assert at[0] <= 9728, at[0]
            return s

        wq_in = part(H * D, 0).rearrange("p (h d) -> p h d", h=H)
        wkq_in = part(H * DQ).rearrange("p (h d) -> p h d", h=H)
        wo_in = part(H * D, 0).rearrange("p (h d) -> p h d", h=H)
        wkv_in = part(H * DC).rearrange("p (h d) -> p h d", h=H)
        wkr_in = part(H * DC).rearrange("p (h d) -> p h d", h=H)
        wqr_in = part(H * DQ).rearrange("p (h d) -> p h d", h=H)
        prod = part(QT * 2 * GT, 0).rearrange("p (t c n) -> p t c n", t=QT, c=2)
        ctx_t = part(HP * GT).rearrange("p (h n) -> p h n", h=HP)
        qp = part(GT)
        sh = part(GT).rearrange("p (g l) -> p g l", l=SEQ)
        ex = part(GT).rearrange("p (g l) -> p g l", l=SEQ)
        at_t = part(GT).rearrange("p (b s) -> p b s", b=NBP)
        sm_s = sb("sm_s", [P, 3, NB])
        act_h = part(MT * GT, 0).rearrange("p (m n) -> p m n", m=MT)
        x3t = part(KD * GT).rearrange("p (k n) -> p k n", k=KD)
        th_f = part(2 * GT).rearrange("p (k n) -> p k n", k=2)
        xn3 = region[:, 0:TT * D].rearrange("p (t d) -> p t d", t=TT)
        gw = part(2 * GT).rearrange("p (k n) -> p k n", k=2)
        gt = [sb(f"gt{k}", [P, TT, E]) for k in range(7)]
        g_s = sb("g_s", [P, 8, TT])
        g_bf = sb("g_bf", [P, 2, TT, E], bf16)
        comb = sb("comb", [P, TT, 96])
        comb_t = sb("comb_t", [96, GT], bf16)

        bank = [ctx.enter_context(nc.psum_tensor(f"bank{i}", [P, GT], f32)) for i in range(8)]
        px, y_ps = bank[0], [bank[1], bank[2]]
        q_ps, r2, r3 = [bank[3], bank[4], bank[5]], bank[6], bank[7]
        hu_ps = [(bank[3], bank[4]), (bank[5], bank[6])]
        x3_ps = w2_ps = hu_ps[1]

        names = """ld_const ld_mix ld_prep1 ld_prep2 ld_w2 ld_x ld_c ld_w13_0 ld_w13_1 ld_w13_2 out_done
            mem_set a_ready conv_scaled ln1 ln2 ln3 pow1 pow2 pow3
            pe_x1t act_conv_in conv act_tanh xc_ready pe_proj act_dt_raw act_bc_hi act_bc_part bc_split
            pe_z act_z softplus act_e act_ln pe_bc act_c act_b act_da unit pool_hc pe_y
            tail pe_yt pe_x2t act_hq
            kv pe_kv act_kb pe_qb prod_done pe_qp act_qp pe_sc softmax act_ex pool_at pe_at act_at pe_ctx
            act_ctx pe_wo x2_ready pe_x3t act_x3t pe_logit act_ge gate pe_comb act_comb pe_hu pe_g act_tf
            ffn act_g pool_act pe_w2 pe_prep1 pe_prep2 pe_prep3 prep1_out prep2_out prep3_out""".split()
        s = Sems((n, sem(n)) for n in names)

        block = ctx.enter_context(nc.Block())

        LN_SEM = [("ln1", "pow1"), ("ln2", "pow2"), ("ln3", "pow3")]

        @block.sync
        def _(sp):
            for name, c in CREDIT["sync"].items():
                sp.sem_inc(s[name], c)
            def load(name, dst, src):
                sp.dma_start(dst, src).then_inc(s[name], 16)

            def load_x(g):
                sp.wait_ge(*s.at("tail", g * TAIL_N))
                load("ld_x", x_raw[:, :, :], a["x"][bass.ds(g * GT, GT), :].rearrange("(n p) d -> p n d", p=P))

            def load_ctx(g):
                sp.wait_ge(*s.at("kv", g * KV_N))
                src = a["ctx"][bass.ds(g * GT, GT), :].rearrange("(b l) d -> l b d", l=SEQ)
                for dup in range(2):
                    load("ld_c", kr[dup * SEQ:(dup + 1) * SEQ, :, :], src)

            def stream_w13(g):
                for m in range(MT):
                    sp.wait_ge(*s.at("pe_hu", before(g, MT, m, RING)))
                    load(f"ld_w13_{m % RING}", w13[:, m % RING], a["w13"][m])

            load_x(0)
            load("ld_const", ident[:, :], a["ident"])
            load("ld_mix", conv_w[:, :, :], a["conv_w"])
            load("ld_mix", vecs[:, :, :], a["vecs"])
            load("ld_mix", a_neg[:, :, :], a["a_log"])
            load("ld_mix", xp_dt[:, :, :], a["xp_dt"])
            load("ld_mix", xp_bc[:, :, :], a["xp_bc"])
            load("ld_mix", dtw[:, :], a["dtw"])
            load("ld_mix", sel_bc[:, :, :], a["sel_bc"])
            load("ld_const", rope_k[:, :, :], a["rope_k"])
            load("ld_const", rope_q[:, :, :, :], a["rope_q"])
            load("ld_const", sel_comb[:, :, :], a["sel_comb"])
            load("ld_const", gate_w[:, :, :], a["gate_w"])
            load("ld_const", prio[:, :], a["prio"])
            load_ctx(0)
            load("ld_prep1", wq_in, a["wq"])
            load("ld_prep1", wkq_in, a["wkq"])
            load("ld_w2", w2[:, :, :], a["w2"])
            sp.wait_ge(*s.at("pe_prep1", H))
            load("ld_prep2", wo_in, a["wo"])
            load("ld_prep2", wkv_in, a["wkv"])
            load("ld_prep2", wkr_in[0:R], a["wkr"])
            load("ld_prep2", wkr_in[R:2 * R], a["wkr"])
            load("ld_prep2", wqr_in, a["wqr"])

            def store(g):
                sp.wait_ge(*s.at("x2_ready", (g + 1) * 4))
                sp.dma_start(out[bass.ds(g * GT, GT), :].rearrange("(n p) d -> p n d", p=P),
                             x2[:, :, :]).then_inc(s["out_done"], 16)

            with sp.Fori(0, NG - 1) as i:
                load_x(i + 1)
                stream_w13(i)
                load_ctx(i + 1)
                store(i)
            stream_w13(NG - 1)
            store(NG - 1)
            sp.wait_ge(*s.at("out_done", 16 * NG))

        @block.gpsimd
        def _(pool):
            for name, c in CREDIT["gpsimd"].items():
                pool.sem_inc(s[name], c)
            for k, (t, val) in enumerate([
                    (conv_in[:, :, :, 0:TAPS - 1], 0.0),
                    (minus_half[:, :], -0.5),
                    (bd[0:SEQ, :, SEQ:], 0.0), (bd[SEQ:, :, 0:SEQ], 0.0),
                    (da[:, :, :, 0:GT:SEQ], 0.0),
                    (n_mat[:, :, :, 1:3, :], 0.0),
                    (comb[:, :, :], 0.0)]):
                nc.gpsimd.memset(t, val).then_inc(s["mem_set"], 1)
                pool.wait_ge(*s.at("mem_set", k + 1))
            nc.gpsimd.memset(comb[:, :, E:E + 1], 0.5).then_inc(s["mem_set"], 1)
            pool.wait_ge(*s.at("mem_set", 8))

            def rstd(k, g):
                dve_sem, pool_sem = LN_SEM[k]
                for part_ in range(LN_PARTS[k]):
                    ts = slice(part_ * TT // LN_PARTS[k], (part_ + 1) * TT // LN_PARTS[k])
                    pool.wait_ge(*s.at(dve_sem, (g * LN_PARTS[k] + part_) * ln_out(k) + ln_var(k)))
                    nc.gpsimd.tensor_tensor(ln_s[k][:, 1, ts], ln_s[k][:, 0, ts], minus_half[:, ts],
                                            ALU.pow).then_inc(s[pool_sem], 1)

            kv = Steps(pool, s, "kv", KV_N)

            def rope_keys(g):
                kv.start(g)
                pool.wait_ge(*s.at("ld_c", (g + 1) * 32))
                pool.wait_ge(*s.at("pe_ctx", g * HP))
                cos = rope_k[:, 0:1, :].to_broadcast([P, NB, DC])
                for lo in (0, DC // 2):
                    hi = DC // 2 - lo
                    kv.mark(nc.gpsimd.tensor_tensor(
                        kr_t[:, :, lo:lo + DC // 2], kr[:, :, hi:hi + DC // 2],
                        rope_k[:, 1:2, lo:lo + DC // 2].to_broadcast([P, NB, DC // 2]), ALU.mult))
                pool.wait_ge(*kv.at(2))
                kv.link(nc.gpsimd.tensor_tensor(kr[:, :, :], kr[:, :, :], cos, ALU.mult))
                for rows, cols in ((slice(0, SEQ), slice(0, DC)), (slice(SEQ, P), slice(DC, P))):
                    kv.link(nc.gpsimd.tensor_tensor(bd[rows, :, cols], kr[rows], kr_t[rows], ALU.add))

            def unit(g, n):
                pool.wait_ge(*s.at("unit", (g * NS + n) * UNIT_N + 4))
                pool.wait_ge(*s.at("act_c", g * NS + n + 1))
                pool.wait_ge(*s.at("pe_y", before(g, NS, n, 2)))
                c = c_sb[:, n % 2:n % 2 + 1, :].to_broadcast([P, KD, GT])
                nc.gpsimd.tensor_tensor(hc[:, n % 2], h[:, :, :], c, ALU.mult).then_inc(s["pool_hc"], 1)

            def norm(g, p):
                n = g * HP + p
                pool.wait_ge(*s.at("softmax", n * SM_N + SM_N))
                inv = sm_s[:, 2, :].unsqueeze(2).to_broadcast([P, NB, SEQ])
                nc.gpsimd.tensor_tensor(sh, ex, inv, ALU.mult).then_inc(s["pool_at"], 1)

            def ffn_tile(g, m):
                n = g * MT + m
                pool.wait_ge(*s.at("ffn", (n + 1) * FFN_N))
                pool.wait_ge(*s.at("act_g", n + 1))
                nc.gpsimd.tensor_tensor(act_h[:, m, :], th_f[:, m % 2, :], gw[:, m % 2, :],
                                        ALU.mult).then_inc(s["pool_act"], 1)

            pool.wait_ge(*s.at("ld_const", 96))
            rstd(0, 0)
            rope_keys(0)
            for n in range(NS):
                unit(0, n)
            rstd(1, 0)

            def body(g, ahead):
                if ahead:
                    rstd(0, g + 1)
                for p in range(HP):
                    norm(g, p)
                    for n in states(p, ahead):
                        unit(g + 1, n)
                rstd(2, g)
                for m in range(MT):
                    ffn_tile(g, m)
                    for n in states(HP + m, ahead):
                        unit(g + 1, n)
                if ahead:
                    rstd(1, g + 1)
                    rope_keys(g + 1)

            with pool.Fori(0, NG - 1) as i:
                body(i, True)
            body(NG - 1, False)

        @block.scalar
        def _(act):
            for name, c in CREDIT["scalar"].items():
                act.sem_inc(s[name], c)
            def evict(dst, src, name):
                nc.scalar.activation(dst, src, ACT.Copy).then_inc(s[name], 1)

            act.wait_ge(*s.at("ld_mix", 7 * 16))
            nc.scalar.activation(a_neg[:, :, :], a_neg[:, :, :], ACT.Exp).then_inc(s["a_ready"], 1)

            def front_conv_in(g):
                act.wait_ge(*s.at("pe_x1t", g + 1))
                for k in range(KD):
                    evict(conv_in[:, k, :, TAPS - 1:], y_ps[k][:, :].rearrange("p (b t) -> p b t", b=NB),
                          "act_conv_in")

            def front_tanh(g):
                act.wait_ge(*s.at("conv", (g + 1) * CONV_N))
                nc.scalar.activation(th_c, acc[:, :, :], ACT.Tanh).then_inc(s["act_tanh"], 1)

            def front_proj(g):
                act.wait_ge(*s.at("pe_proj", 2 * g + 1))
                evict(dt_raw, px[:, :], "act_dt_raw")
                act.wait_ge(*s.at("pe_proj", 2 * g + 2))
                evict(bc_hi[:, :], y_ps[0][0:96, :], "act_bc_hi")
                evict(bc_parts[0:32, :], y_ps[0][0:32, :], "act_bc_part")

            def front_z(g):
                act.wait_ge(*s.at("pe_z", g + 1))
                for k in range(KD):
                    nc.scalar.activation(zs[:, k, :], y_ps[k][:, :], ACT.Identity,
                                         bias=dt_b[:, k:k + 1]).then_inc(s["act_z"], 1)

            def front_log(g):
                act.wait_ge(*s.at("softplus", g * SP_N + SP_M))
                nc.scalar.activation(sp_e[:, :, :], sp_e[:, :, :], ACT.Exp).then_inc(s["act_e"], 1)
                act.wait_ge(*s.at("act_e", g + 1))
                nc.scalar.activation(sp_ln[:, :, :], sp_e[:, :, :], ACT.Ln, bias=1.0).then_inc(s["act_ln"], 1)

            def decay(g, n):
                act.wait_ge(*s.at("unit", before(g, NS, n, 2) * UNIT_N))
                act.wait_ge(*s.at("softplus", g * SP_N + SP_DT))
                for k in range(KD):
                    dst = da[:, n % 2, k, :].rearrange("p (b t) -> p b t", b=NB)[:, :, 1:]
                    src = dt_[:, k, :].rearrange("p (b t) -> p b t", b=NB)[:, :, 1:]
                    nc.scalar.activation(dst, src, ACT.Exp, scale=a_neg[:, k, n:n + 1]).then_inc(s["act_da"], 1)

            def take_b(g, n):
                act.wait_ge(*s.at("pe_bc", (g * NS + n) * 2 + 1))
                act.wait_ge(*s.at("unit", before(g, NS, n, 2) * UNIT_N))
                evict(b_sb[:, n % 2, :], px[:, :], "act_b")

            def take_c(g, n):
                act.wait_ge(*s.at("pe_bc", (g * NS + n) * 2 + 2))
                act.wait_ge(*s.at("pool_hc", before(g, NS, n, 2)))
                evict(c_sb[:, n % 2, :], px[:, :], "act_c")

            def fetch(g, n):
                take_b(g, n)
                decay(g, n)
                take_c(g, n)

            def tail_hq(g):
                act.wait_ge(*s.at("pe_x2t", g + 1))
                act.wait_ge(*s.at("pe_qb", g * HP * QT))
                for k in range(KD):
                    evict(hq[:, k, :], y_ps[k][:, :], "act_hq")

            def keys(g):
                act.wait_ge(*s.at("pe_kv", g + 1))
                act.wait_ge(*s.at("pe_sc", g * HP))
                for k, b in enumerate((q_ps[1], r3)):
                    evict(kb[:, 4 * k:4 * k + 4, :], b[:, :].rearrange("p (b c) -> p b c", c=P), "act_kb")

            def pair_qp(g, p):
                n = g * HP + p
                act.wait_ge(*s.at("pe_qp", n + 1))
                act.wait_ge(*s.at("pe_sc", n))
                evict(qp, r2[:, :], "act_qp")

            def pair_at(g, p):
                n = g * HP + p
                act.wait_ge(*s.at("pe_at", n + 1))
                act.wait_ge(*s.at("pe_ctx", n))
                evict(at_t, r3[:, :].rearrange("p (b s) -> p b s", b=NBP), "act_at")

            def pair_exp(g, p):
                n = g * HP + p
                act.wait_ge(*s.at("softmax", n * SM_N + SM_SUB))
                act.wait_ge(*s.at("pool_at", n))
                nc.scalar.activation(ex, sh, ACT.Exp).then_inc(s["act_ex"], 1)

            def pair_ctx(g, p):
                n = g * HP + p
                act.wait_ge(*s.at("pe_ctx", n + 1))
                if p == 0:
                    act.wait_ge(*s.at("pe_w2", g))
                evict(ctx_t[:, p, :], r3[:, :], "act_ctx")

            def ffn_tile(g, m):
                n = g * MT + m
                act.wait_ge(*s.at("pe_hu", n + 1))
                act.wait_ge(*s.at("pool_act", before(g, MT, m, 2)))
                nc.scalar.activation(th_f[:, m % 2, :], hu_ps[m % 2][0][:, :], ACT.Tanh,
                                     scale=0.5).then_inc(s["act_tf"], 1)

            def ffn_gate(g, m):
                n = g * MT + m
                act.wait_ge(*s.at("pe_g", n + 1))
                act.wait_ge(*s.at("pool_act", before(g, MT, m, 2)))
                evict(gw[:, m % 2, :], r3[:, :], "act_g")

            act.wait_ge(*s.at("a_ready", 1))
            nc.scalar.mul(a_neg[:, :, :], a_neg[:, :, :], -1.0).then_inc(s["a_ready"], 1)
            act.wait_ge(*s.at("a_ready", 2))
            front_conv_in(0)
            front_tanh(0)
            front_proj(0)
            front_z(0)
            front_log(0)
            def fold_query(hd):
                act.wait_ge(*s.at("pe_prep1", hd + 1))
                for k in range(KD):
                    evict(wf[:, k, hd * DQ:(hd + 1) * DQ], bank[3 + hd % 2][:, k * DQ:(k + 1) * DQ], "prep1_out")

            def fold_pair(p):
                act.wait_ge(*s.at("pe_prep2", p + 1))
                for c in range(2):
                    src = bank[3 + 2 * c + p % 2][:, 0:4 * DC].rearrange("p (b d) -> p b d", b=4)
                    evict(n_mat[:, p, c, 0:4:3, :], src[:, 0:4:3, :], "prep2_out")
                    for b, rows in ((1, slice(0, SEQ)), (2, slice(SEQ, P))):
                        evict(n_mat[rows, p, c, b, :], src[rows, b, :], "prep2_out")
                act.wait_ge(*s.at("pe_prep3", p + 1))
                evict(u_mat[:, p, :], bank[7][:, 0:D], "prep3_out")

            act.wait_ge(*s.at("mem_set", 8))
            fetch(0, 0)
            for n in range(NS):
                if n < NS // 4:
                    for hd in range(4 * n, 4 * n + 4):
                        fold_query(hd)
                if n >= NS // 2:
                    fold_pair(n - NS // 2)
                if n + 1 < NS:
                    fetch(0, n + 1)
            tail_hq(0)
            keys(0)

            def body(g, ahead):
                for p in range(HP):
                    now = states(p, ahead)
                    pair_qp(g, p)
                    if ahead and p == 1:
                        front_tanh(g + 1)
                    if ahead and p == 2:
                        front_proj(g + 1)
                    if ahead and p == 3:
                        front_z(g + 1)
                    for n in now[:1]:
                        take_b(g + 1, n)
                    if p:
                        pair_at(g, p - 1)
                    for n in now[:1]:
                        take_c(g + 1, n)
                    pair_exp(g, p)
                    if ahead and p == 0:
                        front_conv_in(g + 1)
                    for n in now[:1]:
                        decay(g + 1, n)
                    for n in now[1:]:
                        take_b(g + 1, n)
                    if p:
                        pair_ctx(g, p - 1)
                    for n in now[1:]:
                        take_c(g + 1, n)
                        decay(g + 1, n)
                    if ahead and p == 3:
                        front_log(g + 1)
                pair_at(g, HP - 1)
                pair_ctx(g, HP - 1)
                act.wait_ge(*s.at("pe_x3t", 2 * g + 2))
                for k in range(KD):
                    evict(x3t[:, k, :], x3_ps[k][:, :], "act_x3t")
                act.wait_ge(*s.at("pe_logit", g + 1))
                nc.scalar.activation(gt[0][:, :, :], r3[:, 0:TT * E].rearrange("p (t e) -> p t e", e=E),
                                     ACT.Exp, scale=-1.0).then_inc(s["act_ge"], 1)
                for m in range(MT):
                    now = states(HP + m, ahead)
                    for n in now:
                        take_b(g + 1, n)
                    ffn_tile(g, m)
                    if m == 1:
                        act.wait_ge(*s.at("pe_comb", g + 1))
                        evict(comb_t[:, :], r3[0:96, :], "act_comb")
                    if m:
                        ffn_gate(g, m - 1)
                    for n in now:
                        take_c(g + 1, n)
                        decay(g + 1, n)
                ffn_gate(g, MT - 1)
                if ahead:
                    tail_hq(g + 1)
                    keys(g + 1)

            with act.Fori(0, NG - 1) as i:
                body(i, True)
            body(NG - 1, False)

        @block.vector
        def _(dve):
            for name, c in CREDIT["vector"].items():
                dve.sem_inc(s[name], c)
            V = nc.vector

            dve.wait_ge(*s.at("ld_mix", 7 * 16))
            V.tensor_scalar(conv_w[:, :, :], conv_w[:, :, :], 0.5, None, ALU.mult).then_inc(s["conv_scaled"], 1)
            V.tensor_scalar(conv_b, conv_b, 0.5, None, ALU.mult).then_inc(s["conv_scaled"], 1)
            dve.wait_ge(*s.at("conv_scaled", 2))
            dve.wait_ge(*s.at("mem_set", 8))

            ln = [Steps(dve, s, LN_SEM[k][0], ln_out(k)) for k in range(3)]

            def layernorm(k, g, x, xn, part_=0):
                st, mv, w = ln_stats[k], ln_mv[k], ln_s[k]
                n = g * LN_PARTS[k] + part_
                tiles = range(part_ * TT // LN_PARTS[k], (part_ + 1) * TT // LN_PARTS[k])
                ts = slice(tiles[0], tiles[-1] + 1)
                step = ln[k].start(n)
                for t in tiles:
                    step.mark(V.bn_stats(st[:, t, :], x[:, t, :]))
                dve.wait_ge(*step.at(len(tiles)))
                step.mark(V.memset(w[:, 2, ts], 0.0))
                for t in tiles:
                    step.mark(V.bn_aggr(mv[:, t, :], st[:, t, :]))
                dve.wait_ge(*step.at(2 * len(tiles) + 1))
                step.mark(V.tensor_scalar(w[:, 0, ts], mv[:, ts, 1], EPS, None, ALU.add))
                dve.wait_ge(*s.at(LN_SEM[k][1], n + 1))
                step.link(V.tensor_tensor(w[:, 2, ts], w[:, 1, ts], w[:, 1, ts], ALU.mult))
                step.link(V.tensor_tensor(w[:, 2, ts], w[:, 2, ts], w[:, 0, ts], ALU.mult))
                step.link(V.tensor_scalar(w[:, 2, ts], w[:, 2, ts], -0.5, 1.5, ALU.mult, ALU.add))
                step.link(V.tensor_tensor(w[:, 1, ts], w[:, 2, ts], w[:, 1, ts], ALU.mult))
                for t in tiles:
                    step.mark(V.tensor_scalar(xn[:, t, :], x[:, t, :], mv[:, t, 0:1], w[:, 1, t:t + 1],
                                              ALU.subtract, ALU.mult))

            def front_ln(g):
                dve.wait_ge(*s.at("ld_x", (g + 1) * 16))
                layernorm(0, g, x_raw, xn1)

            conv = Steps(dve, s, "conv", CONV_N)

            def front_conv(g):
                conv.start(g)
                dve.wait_ge(*s.at("act_conv_in", (g + 1) * KD))
                for j in range(TAPS):
                    for k in range(KD):
                        o = acc[:, k, :].rearrange("p (b t) -> p b t", b=NB)
                        i_ = conv_in[:, k, :, j:j + SEQ]
                        if j:
                            dve.wait_ge(*conv.at(KD * (j - 1) + k + 1))
                            conv.mark(V.scalar_tensor_tensor(out=o, in0=i_, scalar=conv_w[:, k, j:j + 1], in1=o,
                                                             op0=ALU.mult, op1=ALU.add))
                        else:
                            conv.mark(V.tensor_scalar(o, i_, conv_w[:, k, 0:1], conv_b[:, k:k + 1],
                                                      ALU.mult, ALU.add))

            def front_silu(g):
                dve.wait_ge(*s.at("act_tanh", g + 1))
                V.scalar_tensor_tensor(out=xc[:, :, :], in0=th_c, scalar=1.0, in1=acc[:, :, :],
                                       op0=ALU.add, op1=ALU.mult).then_inc(s["xc_ready"], 1)

            split = Steps(dve, s, "bc_split", SPLIT_N)
            soft = Steps(dve, s, "softplus", SP_N)

            def front_split(g):
                split.start(g)
                dve.wait_ge(*s.at("act_bc_hi", g + 1))
                dve.wait_ge(*s.at("act_bc_part", g + 1))
                split.link(V.tensor_tensor(bc_r, y_ps[0][0:96, :], bc_hi[:, :], ALU.subtract))
                split.mark(V.tensor_copy(bc_parts[32:64, :], bc_r[32:64, :]))
                split.link(V.tensor_copy(bc_hi[64:96, :], bc_r[64:96, :]))
                split.mark(V.tensor_tensor(bc_parts[64:96, :], bc_r[64:96, :], bc_hi[64:96, :], ALU.subtract))

            def front_abs(g):
                soft.start(g)
                dve.wait_ge(*s.at("act_z", (g + 1) * KD))
                soft.mark(V.scalar_tensor_tensor(out=sp_e[:, :, :], in0=zs, scalar=-1.0, in1=zs,
                                                 op0=ALU.mult, op1=ALU.min))

            def front_log1p(g):
                dve.wait_ge(*s.at("act_e", g + 1))
                soft.link(V.tensor_scalar(sp_c, sp_e[:, :, :], 1.0, -1.0, ALU.add, ALU.add))
                soft.link(V.tensor_tensor(sp_c, sp_e[:, :, :], sp_c, ALU.subtract))
                dve.wait_ge(*s.at("act_ln", g + 1))
                soft.link(V.tensor_tensor(sp_c, sp_ln[:, :, :], sp_c, ALU.add))
                e, series = sp_e[:, :, :], u[:, :, :]
                soft.link(V.tensor_scalar(series, e, -1 / 4, 1 / 3, ALU.mult, ALU.add))
                soft.link(V.tensor_tensor(series, series, e, ALU.mult))

            def front_dt(g):
                e, series = sp_e[:, :, :], u[:, :, :]
                for c in (-1 / 2, 1.0):
                    soft.link(V.scalar_tensor_tensor(out=series, in0=series, scalar=c, in1=e,
                                                     op0=ALU.add, op1=ALU.mult))
                soft.mark(V.scalar_tensor_tensor(out=series, in0=e, scalar=SMALL, in1=series,
                                                 op0=ALU.is_lt, op1=ALU.mult))
                soft.link(V.scalar_tensor_tensor(out=sp_c, in0=e, scalar=SMALL, in1=sp_c,
                                                 op0=ALU.is_ge, op1=ALU.mult))
                soft.link(V.tensor_tensor(sp_c, sp_c, series, ALU.add))
                soft.link(V.scalar_tensor_tensor(out=dt_[:, :, :], in0=zs, scalar=0.0, in1=sp_c,
                                                 op0=ALU.max, op1=ALU.add))
                soft.link(V.tensor_tensor(u[:, :, :], dt_[:, :, :], xc[:, :, :], ALU.mult))

            steps = Steps(dve, s, "unit", UNIT_N)

            def unit(g, n):
                steps.start(g * NS + n)
                dve.wait_ge(*s.at("act_b", g * NS + n + 1))
                b = b_sb[:, n % 2:n % 2 + 1, :].to_broadcast([P, KD, GT])
                steps.mark(V.tensor_tensor(v[:, :, :], u[:, :, :], b, ALU.mult))
                dve.wait_ge(*s.at("act_da", (g * NS + n + 1) * KD))
                d3 = da[:, n % 2].rearrange("p k (b t) -> p (k b) t", b=NB)[:, :, 1:]
                steps.mark(V.tensor_scalar(d3, d3, LOG_FLOOR, None, ALU.max))
                dve.wait_ge(*steps.at(1))
                steps.mark(V.tensor_scalar(v[:, :, :], v[:, :, :], LOG_FLOOR, None, ALU.max))
                dve.wait_ge(*steps.at(3))
                dve.wait_ge(*s.at("pool_hc", before(g, NS, n, 1)))
                steps.link(V.tensor_tensor_scan(h[:, :, :].rearrange("p k t -> p (k t)"),
                                                da[:, n % 2].rearrange("p k t -> p (k t)"),
                                                v[:, :, :].rearrange("p k t -> p (k t)"),
                                                0.0, ALU.mult, ALU.add))

            tail_s = Steps(dve, s, "tail", TAIL_N)

            def tail(g):
                tail_s.start(g)
                dve.wait_ge(*s.at("pe_y", (g + 1) * NS))
                for k in range(KD):
                    tail_s.mark(V.scalar_tensor_tensor(out=yt[:, k, :], in0=xc[:, k, :], scalar=d_par[:, k:k + 1],
                                                       in1=y_ps[k][:, :], op0=ALU.mult, op1=ALU.add))
                dve.wait_ge(*s.at("pe_yt", g + 1))
                for j in range(2):
                    tail_s.mark(V.tensor_tensor(x1[:, 2 * j:2 * j + 2, :], x_raw[:, 2 * j:2 * j + 2, :],
                                                y_ps[j][:, :].rearrange("p (t d) -> p t d", t=2), ALU.add))
                dve.wait_ge(*tail_s.at(TAIL_X1))
                layernorm(1, g, x1, xn2)

            def products(g, p):
                n = g * HP + p
                if p == 0:
                    dve.wait_ge(*s.at("pe_w2", g))
                dve.wait_ge(*s.at("pe_qp", n))
                for t in range(QT):
                    dve.wait_ge(*s.at("pe_qb", n * QT + t + 1))
                    for c in range(2):
                        tab = rope_q[:, c, t, :].unsqueeze(1).to_broadcast([P, NB, SEQ])
                        V.tensor_tensor(prod[:, t, c, :].rearrange("p (b s) -> p b s", b=NB),
                                        q_ps[t][:, :].rearrange("p (b s) -> p b s", b=NB), tab,
                                        ALU.mult).then_inc(s["prod_done"], 1)

            sm = Steps(dve, s, "softmax", SM_N)

            def softmax_shift(g, p):
                n = g * HP + p
                sm.start(n)
                dve.wait_ge(*s.at("pe_sc", n + 1))
                sc = r2[:, :].rearrange("p (g l) -> p g l", l=SEQ)
                sm.link(V.tensor_reduce(sm_s[:, 0, :], sc, axis=AX.X, op=ALU.max))
                dve.wait_ge(*s.at("pe_at", n))
                mx = sm_s[:, 0, :].unsqueeze(2).to_broadcast([P, NB, SEQ])
                sm.mark(V.tensor_tensor(sh, sc, mx, ALU.subtract))

            def softmax_sum(g, p):
                n = g * HP + p
                dve.wait_ge(*s.at("act_ex", n + 1))
                sm.link(V.tensor_reduce(sm_s[:, 1, :], ex, axis=AX.X, op=ALU.add))
                dve.wait_ge(*s.at("pool_at", n))
                sm.link(V.reciprocal(sm_s[:, 2, :], sm_s[:, 1, :]))

            gate = Steps(dve, s, "gate", GATE_N)

            def route(g):
                gate.start(g)
                tiny = lambda k: g_s[:, k, :]
                wide = lambda k: g_s[:, k, :].unsqueeze(2).to_broadcast([P, TT, E])
                pr = prio[:, :].unsqueeze(1).to_broadcast([P, TT, E])
                step, tt = gate.link, V.tensor_tensor
                dve.wait_ge(*s.at("act_ge", g + 1))
                step(V.tensor_scalar(gt[1][:, :, :], gt[0][:, :, :], 1.0, None, ALU.add))
                step(V.reciprocal(gt[2][:, :, :], gt[1][:, :, :]))
                left = gt[2]
                for k, hot in ((0, gt[3]), (1, gt[4])):
                    step(V.tensor_reduce(tiny(k), left[:, :, :], axis=AX.X, op=ALU.max))
                    step(tt(hot[:, :, :], left[:, :, :], wide(k), ALU.is_equal))
                    step(tt(hot[:, :, :], hot[:, :, :], pr, ALU.mult))
                    step(V.tensor_reduce(tiny(2), hot[:, :, :], axis=AX.X, op=ALU.max))
                    step(tt(hot[:, :, :], hot[:, :, :], wide(2), ALU.is_equal))
                    if k == 0:
                        step(V.scalar_tensor_tensor(out=gt[5][:, :, :], in0=hot[:, :, :], scalar=-2.0,
                                                    in1=left[:, :, :], op0=ALU.mult, op1=ALU.add))
                        left = gt[5]
                step(tt(tiny(3), tiny(0), tiny(1), ALU.add))
                step(V.tensor_scalar(tiny(3), tiny(3), 1e-20, None, ALU.add))
                step(V.reciprocal(tiny(4), tiny(3)))
                for k in range(2):
                    step(tt(tiny(5 + k), tiny(k), tiny(4), ALU.mult))
                    step(V.tensor_scalar(tiny(5 + k), tiny(5 + k), 1.25, None, ALU.mult))
                    step(tt(gt[3 + k][:, :, :], gt[3 + k][:, :, :], wide(5 + k), ALU.mult))
                step(tt(gt[6][:, :, :], gt[3][:, :, :], gt[4][:, :, :], ALU.add))
                step(V.tensor_copy(g_bf[:, 0], gt[6][:, :, :]))
                step(tt(gt[1][:, :, :], gt[6][:, :, :], g_bf[:, 0], ALU.subtract))
                dve.wait_ge(*s.at("pe_comb", g))
                gate_hi = V.tensor_copy(comb[:, :, 0:E], g_bf[:, 0])
                gate.mark(gate_hi)
                gate.link(V.tensor_copy(g_bf[:, 1], gt[1][:, :, :]))
                return tt

            def route_parts(g):
                gate.mark(V.tensor_copy(comb[:, :, 32:32 + E], g_bf[:, 1]))
                gate.mark(V.tensor_tensor(comb[:, :, 64:64 + E], gt[1][:, :, :], g_bf[:, 1], ALU.subtract))

            f = Steps(dve, s, "ffn", FFN_N)

            def ffn_tile(g, m):
                f.start(g * MT + m)
                dve.wait_ge(*s.at("act_tf", g * MT + m + 1))
                hb, ub = hu_ps[m % 2]
                th = th_f[:, m % 2, :]
                f.link(V.scalar_tensor_tensor(out=th, in0=th, scalar=1.0, in1=hb[:, :], op0=ALU.add, op1=ALU.mult))
                f.mark(V.tensor_tensor(th, th, ub[:, :], ALU.mult))

            front_ln(0)
            front_conv(0)
            front_silu(0)
            front_split(0)
            front_abs(0)
            front_log1p(0)
            front_dt(0)
            for n in range(NS):
                unit(0, n)
            tail(0)

            def body(g, ahead):
                products(g, 0)
                if ahead:
                    front_ln(g + 1)
                for p in range(HP):
                    softmax_shift(g, p)
                    if p + 1 < HP:
                        products(g, p + 1)
                    if ahead and p == 1:
                        front_silu(g + 1)
                    if ahead and p == 2:
                        front_split(g + 1)
                    if ahead and p == 3:
                        front_abs(g + 1)
                    if ahead and p == 4:
                        front_log1p(g + 1)
                    softmax_sum(g, p)
                    if ahead and p == 0:
                        front_conv(g + 1)
                    if ahead and p == 4:
                        front_dt(g + 1)
                    for n in states(p, ahead):
                        unit(g + 1, n)
                dve.wait_ge(*s.at("out_done", g * 16))
                for j in range(2):
                    dve.wait_ge(*s.at("pe_wo", 2 * g + j + 1))
                    V.tensor_tensor(x2[:, 2 * j:2 * j + 2, :], x1[:, 2 * j:2 * j + 2, :],
                                    q_ps[j][:, :].rearrange("p (t d) -> p t d", t=2),
                                    ALU.add).then_inc(s["x2_ready"], 1)
                    dve.wait_ge(*s.at("x2_ready", g * 4 + j + 1))
                    layernorm(2, g, x2, xn3, j)
                route(g)
                route_parts(g)
                for m in range(MT):
                    ffn_tile(g, m)
                    for n in states(HP + m, ahead):
                        unit(g + 1, n)
                if ahead:
                    tail(g + 1)
                dve.wait_ge(*s.at("pe_w2", g + 1))
                for j, b in enumerate(w2_ps):
                    V.tensor_tensor(x2[:, 2 * j:2 * j + 2, :], x2[:, 2 * j:2 * j + 2, :],
                                    b[:, :].rearrange("p (t d) -> p t d", t=2), ALU.add).then_inc(s["x2_ready"], 1)

            with dve.Fori(0, NG - 1) as i:
                body(i, True)
            body(NG - 1, False)

        @block.tensor
        def _(pe):
            for name, c in CREDIT["tensor"].items():
                pe.sem_inc(s[name], c)
            mm = nc.tensor.matmul

            def group(b, pairs, name=None):
                for i_, (l, r) in enumerate(pairs):
                    last = mm(b, l, r, start=i_ == 0, stop=i_ == len(pairs) - 1)
                if name:
                    last.then_inc(s[name], 1)

            def to_channels(xn, banks, name, tiles=range(TT)):
                for k in range(KD):
                    for t in tiles:
                        last = nc.tensor.transpose(banks[k][:, t * P:(t + 1) * P], xn[:, t, k * P:(k + 1) * P],
                                                   ident[:, :])
                last.then_inc(s[name], 1)

            def front_x1t(g):
                pe.wait_ge(*s.at("ln1", (g + 1) * ln_out(0)))
                pe.wait_ge(*s.at("act_hq", g * KD))
                to_channels(xn1, y_ps, "pe_x1t")

            def front_proj(g):
                pe.wait_ge(*s.at("xc_ready", g + 1))
                pe.wait_ge(*s.at("act_conv_in", (g + 1) * KD))
                pe.wait_ge(*s.at("act_c", g * NS))
                group(px[:, :], [(xp_dt[:, k, :], xc[:, k, :]) for k in range(KD)], "pe_proj")
                group(y_ps[0][0:96, :], [(xp_bc[:, k, :], xc[:, k, :]) for k in range(KD)], "pe_proj")

            def front_z(g):
                pe.wait_ge(*s.at("act_dt_raw", g + 1))
                pe.wait_ge(*s.at("act_bc_part", g + 1))
                pe.wait_ge(*s.at("bc_split", g * SPLIT_N + 1))
                for k in range(KD):
                    group(y_ps[k][:, :], [(dtw[:, k * P:(k + 1) * P], dt_raw)], "pe_z" if k == KD - 1 else None)

            def y_sum(g, n):
                pe.wait_ge(*s.at("pool_hc", g * NS + n + 1))
                if n == 0:
                    pe.wait_ge(*s.at("act_z", (g + 1) * KD))
                for k in range(KD):
                    last = mm(y_ps[k][:, :], ident[:, :], hc[:, n % 2, k, :], start=n == 0, stop=n == NS - 1)
                last.then_inc(s["pe_y"], 1)

            def send_b(g, n):
                if n == 0:
                    pe.wait_ge(*s.at("bc_split", (g + 1) * SPLIT_N))
                    pe.wait_ge(*s.at("act_dt_raw", g + 1))
                pe.wait_ge(*s.at("act_c", g * NS + n))
                group(px[:, :], [(sel_bc[:, n, :], bc_parts[:, :])], "pe_bc")

            def send_c(g, n):
                pe.wait_ge(*s.at("act_b", g * NS + n + 1))
                group(px[:, :], [(sel_bc[:, NS + n, :], bc_parts[:, :])], "pe_bc")

            def tail_yt(g):
                pe.wait_ge(*s.at("tail", g * TAIL_N + TAIL_YT))
                for t in range(TT):
                    for k in range(KD):
                        at_ = (t % 2) * D + k * P
                        last = nc.tensor.transpose(y_ps[t // 2][:, at_:at_ + P], yt[:, k, t * P:(t + 1) * P],
                                                   ident[:, :])
                last.then_inc(s["pe_yt"], 1)

            def tail_x2t(g):
                pe.wait_ge(*s.at("ln2", (g + 1) * ln_out(1)))
                to_channels(xn2, y_ps, "pe_x2t")

            def keys(g):
                pe.wait_ge(*s.at("kv", (g + 1) * KV_N))
                pe.wait_ge(*s.at("ffn", g * MT * FFN_N))
                pe.wait_ge(*s.at("act_g", g * MT))
                for b in range(NB):
                    last = nc.tensor.transpose((q_ps[1], r3)[b // 4][:, (b % 4) * P:(b % 4 + 1) * P], bd[:, b, :],
                                               ident[:, :])
                last.then_inc(s["pe_kv"], 1)

            def query(g, p):
                n = g * HP + p
                if p == 0:
                    pe.wait_ge(*s.at("act_hq", (g + 1) * KD))
                for t in range(QT):
                    if p == 0 and t == 1:
                        pe.wait_ge(*s.at("act_kb", 2 * g + 1))
                    if p == 0 and t == 2:
                        pe.wait_ge(*s.at("x2_ready", g * 4))
                    if p:
                        pe.wait_ge(*s.at("prod_done", (n - 1) * PROD_N + 2 * t + 2))
                    c = (p * QT + t) * P
                    group(q_ps[t][:, :], [(wf[:, k, c:c + P], hq[:, k, :]) for k in range(KD)], "pe_qb")

            def latent_query(g, p):
                n = g * HP + p
                pe.wait_ge(*s.at("prod_done", (n + 1) * PROD_N))
                if p:
                    pe.wait_ge(*s.at("softmax", (n - 1) * SM_N + SM_SUB))
                else:
                    pe.wait_ge(*s.at("act_kb", (g + 1) * 2))
                todo = [(t, c) for t in range(2) for c in range(2)]
                for i_, (t, c) in enumerate(todo):
                    for hd in range(2):
                        blk, tile = (t, t) if hd == 0 else (2 + t, 1 + t)
                        last = mm(r2[hd * DC:(hd + 1) * DC, :], n_mat[:, p, c, blk, :], prod[:, tile, c, :],
                                  start=i_ == 0, stop=i_ == len(todo) - 1)
                last.then_inc(s["pe_qp"], 1)

            def scores(g, p):
                n = g * HP + p
                pe.wait_ge(*s.at("act_qp", n + 1))
                if p == 0:
                    pe.wait_ge(*s.at("act_kb", (g + 1) * 2))
                for bp in range(NBP):
                    for o in range(2):
                        b = 2 * bp + o
                        last = mm(r2[o * SEQ:(o + 1) * SEQ, bp * P:(bp + 1) * P], qp[:, b * SEQ:(b + 1) * SEQ],
                                  kb[:, b, :], start=bp == 0, stop=bp == NBP - 1, skip_group_check=True)
                last.then_inc(s["pe_sc"], 1)

            def weights_t(g, p):
                n = g * HP + p
                pe.wait_ge(*s.at("pool_at", n + 1))
                if p:
                    pe.wait_ge(*s.at("act_ctx", n))
                w = sh.rearrange("p (b h) l -> p b (h l)", b=NBP)
                for bp in range(NBP):
                    last = nc.tensor.transpose(r3[:, bp * P:(bp + 1) * P], w[:, bp, :], ident[:, :])
                last.then_inc(s["pe_at"], 1)

            def context(g, p):
                n = g * HP + p
                pe.wait_ge(*s.at("act_at", n + 1))
                for b in range(NB):
                    last = mm(r3[:, b * SEQ:(b + 1) * SEQ], bd[:, b, :],
                              at_t[:, b // 2, (b % 2) * SEQ:(b % 2 + 1) * SEQ],
                              start=b == 0, stop=b == NB - 1, skip_group_check=True)
                last.then_inc(s["pe_ctx"], 1)

            def project(g, p, j):
                pe.wait_ge(*s.at("act_ctx", g * HP + p + 1))
                if p == 0:
                    pe.wait_ge(*s.at("prod_done", (g + 1) * HP * PROD_N))
                for t in (2 * j, 2 * j + 1):
                    last = mm(q_ps[j][:, (t % 2) * D:(t % 2 + 1) * D], ctx_t[:, p, t * P:(t + 1) * P],
                              u_mat[:, p, :], start=p == 0 and t % 2 == 0, stop=p == HP - 1,
                              skip_group_check=True)
                if p == HP - 1:
                    last.then_inc(s["pe_wo"], 1)

            def ffn_up(g, m, w):
                n = g * MT + m
                slot = m % RING
                pe.wait_ge(*s.at(f"ld_w13_{slot}", (g * len(range(slot, MT, RING)) + m // RING + 1) * 16))
                if m == 0:
                    pe.wait_ge(*s.at("act_x3t", (g + 1) * KD))
                if m >= 2:
                    pe.wait_ge(*s.at("ffn", (n - 1) * FFN_N))
                group(hu_ps[m % 2][w][:, :], [(w13[:, m % RING, w, k, :], x3t[:, k, :]) for k in range(KD)],
                      "pe_hu" if w else None)

            def ffn_gate(g, m):
                n = g * MT + m
                if m:
                    pe.wait_ge(*s.at("act_g", n))
                else:
                    pe.wait_ge(*s.at("act_comb", g + 1))
                group(r3[:, :], [(sel_comb[:, m, :], comb_t[:, :])], "pe_g")

            def ffn_down(g, m):
                n = g * MT + m
                pe.wait_ge(*s.at("pool_act", n + 1))
                if m == 0:
                    pe.wait_ge(*s.at("ffn", (g + 1) * MT * FFN_N))
                for t in range(TT):
                    last = mm(w2_ps[t // 2][:, (t % 2) * D:(t % 2 + 1) * D], act_h[:, m, t * P:(t + 1) * P],
                              w2[:, m, :], start=m == 0 and t % 2 == 0, stop=m == MT - 1, skip_group_check=True)
                if m == MT - 1:
                    last.then_inc(s["pe_w2"], 1)

            pe.wait_ge(*s.at("ld_const", 96))
            pe.wait_ge(*s.at("ld_mix", 7 * 16))
            front_x1t(0)
            front_proj(0)
            front_z(0)

            def fold_query(hd):
                if hd >= 2:
                    pe.wait_ge(*s.at("prep1_out", (hd - 1) * KD))
                for k in range(KD):
                    last = mm(bank[3 + hd % 2][:, k * DQ:(k + 1) * DQ], wq_in[:, hd, k * P:(k + 1) * P],
                              wkq_in[:, hd, :], start=k == 0, stop=k == KD - 1, skip_group_check=True)
                last.then_inc(s["pe_prep1"], 1)

            def fold_pair(p):
                pe.wait_ge(*s.at("prep1_out", H * KD))
                if p >= 2:
                    pe.wait_ge(*s.at("prep2_out", (p - 1) * 6))
                for c in range(2):
                    rows = slice(c * R, (c + 1) * R)
                    wqr = wqr_in[rows, 2 * p:2 * p + 2, :].rearrange("p h q -> p (h q)")
                    for blk, (tile, hd) in enumerate(((0, 0), (1, 0), (1, 1), (2, 1))):
                        last = mm(bank[3 + 2 * c + p % 2][:, blk * DC:(blk + 1) * DC],
                                  wqr[:, tile * P:(tile + 1) * P], wkr_in[rows, 2 * p + hd, :],
                                  start=blk == 0, stop=blk == 3, skip_group_check=True)
                last.then_inc(s["pe_prep2"], 1)
                if p >= 1:
                    pe.wait_ge(*s.at("prep3_out", p))
                for hd in range(2):
                    last = mm(bank[7][hd * DC:(hd + 1) * DC, 0:D], wkv_in[:, 2 * p + hd, :],
                              wo_in[:, 2 * p + hd, :], start=True, stop=True)
                last.then_inc(s["pe_prep3"], 1)

            send_b(0, 0)
            send_c(0, 0)
            pe.wait_ge(*s.at("ld_prep1", 32))
            for n in range(NS):
                if n < NS // 4:
                    for hd in range(4 * n, 4 * n + 4):
                        fold_query(hd)
                if n == NS // 2:
                    pe.wait_ge(*s.at("ld_prep2", 5 * 16))
                if n >= NS // 2:
                    fold_pair(n - NS // 2)
                if n + 1 < NS:
                    send_b(0, n + 1)
                if n >= 2:
                    y_sum(0, n - 2)
                if n + 1 < NS:
                    send_c(0, n + 1)
            for n in (NS - 2, NS - 1):
                y_sum(0, n)
            tail_yt(0)
            tail_x2t(0)
            pe.wait_ge(*s.at("prep2_out", HP * 6))
            pe.wait_ge(*s.at("prep3_out", HP))
            pe.wait_ge(*s.at("ld_w2", 16))
            keys(0)

            def body(g, ahead):
                query(g, 0)
                for p in range(HP):
                    now = states(p, ahead)
                    latent_query(g, p)
                    for n in now[:1]:
                        send_b(g + 1, n)
                    if p:
                        weights_t(g, p - 1)
                    scores(g, p)
                    for n in now[:1]:
                        send_c(g + 1, n)
                        if n >= 2:
                            y_sum(g + 1, n - 2)
                    if ahead and p == 0:
                        front_x1t(g + 1)
                    if p + 1 < HP:
                        query(g, p + 1)
                    if ahead and p == 1:
                        front_proj(g + 1)
                    if ahead and p == 2:
                        front_z(g + 1)
                    for n in now[1:]:
                        send_b(g + 1, n)
                    if p:
                        context(g, p - 1)
                    for n in now[1:]:
                        send_c(g + 1, n)
                        if n >= 2:
                            y_sum(g + 1, n - 2)
                for p in range(HP - 1):
                    project(g, p, 0)
                weights_t(g, HP - 1)
                context(g, HP - 1)
                project(g, HP - 1, 0)
                for p in range(HP):
                    project(g, p, 1)
                for j in range(2):
                    pe.wait_ge(*s.at("ln3", (g * 2 + j + 1) * ln_out(2)))
                    to_channels(xn3, x3_ps, "pe_x3t", (2 * j, 2 * j + 1))
                pe.wait_ge(*s.at("act_x3t", (g + 1) * KD))
                for t in range(TT):
                    for k in range(KD):
                        last = mm(r3[:, t * E:(t + 1) * E], x3t[:, k, t * P:(t + 1) * P], gate_w[:, k, :],
                                  start=(t, k) == (0, 0), stop=(t, k) == (TT - 1, KD - 1), skip_group_check=True)
                last.then_inc(s["pe_logit"], 1)
                for m in range(MT):
                    now = states(HP + m, ahead)
                    ffn_up(g, m, 0)
                    for n in now:
                        send_b(g + 1, n)
                    ffn_up(g, m, 1)
                    if m == 1:
                        pe.wait_ge(*s.at("gate", (g + 1) * GATE_N))
                        for t in range(TT):
                            last = nc.tensor.transpose(r3[0:96, t * P:(t + 1) * P], comb[:, t, :], ident[:, :])
                        last.then_inc(s["pe_comb"], 1)
                    if m:
                        ffn_gate(g, m - 1)
                    for n in now:
                        send_c(g + 1, n)
                        y_sum(g + 1, n - 2)
                ffn_gate(g, MT - 1)
                for m in range(MT):
                    ffn_down(g, m)
                    if ahead and m in (0, 2):
                        y_sum(g + 1, NS - 2 + m // 2)
                    if ahead and m == 5:
                        tail_yt(g + 1)
                    if ahead and m == 11:
                        tail_x2t(g + 1)
                if ahead:
                    keys(g + 1)

            with pe.Fori(0, NG - 1) as i:
                body(i, True)
            body(NG - 1, False)


def rope_table(length, dim):
    inv = (1.0 / 10000.0 ** (np.arange(0, dim, 2, dtype=np.float32) / dim)).astype(np.float32)
    f = np.arange(length, dtype=np.float32)[:, None] * inv[None, :]
    return np.repeat(np.sin(f), 2, axis=-1), np.repeat(np.cos(f), 2, axis=-1)


def constants():
    sin_q, cos_q = rope_table(SEQ, DQ)
    sin_k, cos_k = rope_table(SEQ, DC)
    j = np.arange(QT * P) % DQ
    half = DQ // 2
    sin_t = (sin_q[:, (j + half) % DQ] * np.where(j < half, 1.0, -1.0)).T
    rope_q = np.stack([cos_q[:, j].T, sin_t]).reshape(2, QT, P, SEQ).transpose(2, 0, 1, 3)
    sign = np.where(np.arange(DC) < DC // 2, -1.0, 1.0)
    rope_k = np.tile(np.stack([cos_k, sin_k * sign], axis=1), (2, 1, 1))
    sel_bc = np.zeros((96, 2 * NS, P))
    sel_comb = np.zeros((96, MT * P))
    for part in range(3):
        for r in range(2 * NS):
            sel_bc[32 * part + r, r, :] = 1
        for e in range(E + 1):
            sel_comb[32 * part + e, e * HID:(e + 1) * HID] = 1
    f32 = np.float32
    return {"ident": np.eye(P, dtype=f32), "rope_q": rope_q.astype(f32), "rope_k": rope_k.astype(f32),
            "sel_bc": sel_bc.astype(np.dtype("bfloat16")),
            "sel_comb": sel_comb.reshape(96, MT, P).astype(np.dtype("bfloat16")),
            "prio": np.tile(np.arange(E, 0, -1, dtype=f32), (P, 1))}


def laid_out(x, ctx_512, L0_attn_conv_w, L0_attn_conv_b, L0_attn_x_proj_w, L0_attn_dt_proj_w, L0_attn_dt_proj_b,
             L0_attn_A_log, L0_attn_D_param, L0_xattn_Wq, L0_xattn_w_kc_q, L0_xattn_w_kc_kv, L0_xattn_W_qr,
             L0_xattn_W_kr, L0_xattn_Wo, L0_ffn_gate_w, L0_ffn_w1, L0_ffn_w2, L0_ffn_w3, L0_ffn_sw1, L0_ffn_sw2,
             L0_ffn_sw3):
    n = np.asarray

    def halves(w):
        return n(w).reshape(KD, P, -1).transpose(1, 0, 2)

    xp = halves(n(L0_attn_x_proj_w).T)
    bc = xp[:, :, RANK:]
    pad = MT * P - (E + 1) * HID

    def packed(w, sw):
        cols = np.concatenate([n(w).transpose(1, 0, 2).reshape(D, E * HID), n(sw),
                               np.zeros((D, pad), np.float32)], axis=1)
        return cols.reshape(KD, P, MT, P).transpose(2, 1, 0, 3)

    w2 = np.concatenate([n(L0_ffn_w2).reshape(E * HID, D), n(L0_ffn_sw2), np.zeros((pad, D), np.float32)])
    qr = n(L0_xattn_W_qr).transpose(2, 0, 1)
    return {
        "x": n(x).reshape(T_ALL, D), "ctx": n(ctx_512).reshape(T_ALL, DC),
        "conv_w": halves(n(L0_attn_conv_w).reshape(D, TAPS)),
        "vecs": np.stack([halves(L0_attn_conv_b)[:, :, 0], halves(L0_attn_dt_proj_b)[:, :, 0],
                          halves(L0_attn_D_param)[:, :, 0]], axis=1),
        "a_log": halves(L0_attn_A_log), "xp_dt": xp[:, :, :RANK], "xp_bc": np.concatenate([bc, bc, bc], axis=2),
        "dtw": n(L0_attn_dt_proj_w).T,
        "wq": n(L0_xattn_Wq).reshape(H, P, D).transpose(1, 0, 2), "wkq": n(L0_xattn_w_kc_q).transpose(1, 0, 2),
        "wo": n(L0_xattn_Wo).reshape(D, H, P).transpose(2, 1, 0), "wkv": n(L0_xattn_w_kc_kv).transpose(1, 0, 2),
        "wkr": n(L0_xattn_W_kr).transpose(2, 0, 1),
        "wqr": np.concatenate([qr, np.roll(qr, -(DQ // 2), axis=2)]),
        "gate_w": halves(n(L0_ffn_gate_w).T), "w2": w2.reshape(MT, P, D).transpose(1, 0, 2),
        "w13": np.stack([packed(L0_ffn_w1, L0_ffn_sw1), packed(L0_ffn_w3, L0_ffn_sw3)], axis=2),
    }


def kernel(**inputs):
    import concourse.bacc as bacc
    from concourse.bass_utils import run_bass_kernel_spmd

    arrays = {f"in_{k}": np.ascontiguousarray(v) for k, v in {**constants(), **laid_out(**inputs)}.items()}
    nc = bacc.Bacc("TRN2", target_bir_lowering=False, num_devices=1)
    aps = {k[3:]: nc.dram_tensor(k, v.shape, mybir.dt.from_np(v.dtype), kind="ExternalInput").ap()
           for k, v in arrays.items()}
    out = nc.dram_tensor("out", (T_ALL, D), mybir.dt.float32, kind="ExternalOutput").ap()
    build(nc, aps, out)
    r = run_bass_kernel_spmd(nc, [arrays], core_ids=[0])
    return r.results[0]["out"].reshape(T_ALL // SEQ, SEQ, D)
```

```python
import numpy as np
import concourse.bass as bass
import concourse.mybir as mybir
from contextlib import ExitStack

P = 128
D = 256
KD = D // P
T_ALL, SEQ = 2048, 64
GT = 512
NG = T_ALL // GT
TT = GT // P
NB = GT // SEQ
NBP = NB // 2
NS, RANK, TAPS = 16, 128, 4
H, DC, DQ, R = 16, 64, 192, 64
HP = H // 2
QT = 2 * DQ // P
E, HID = 8, 176
MT = -(-((E + 1) * HID) // P)
RING, RING2 = 2, 3
REGION = 18 * GT
LOG_FLOOR = 1e-38
EPS = 1e-5

UNITS = [0, 0, 0, 0, 1, 2, 2, 2, 1, 0, 1, 1, 1, 1, 0, 1, 1, 0, 1, 1, 0, 0]
TAIL_AT = (3, 6)
FRONT = [[], ["split", "abs"], ["log1p"], ["series"], ["dt"], [], [], []]
LOG_AT = 2
X3_EARLY = 1
assert len(UNITS) == HP + 1 + MT and sum(UNITS) == NS


def pool_adds(g):
    return FIRST_ADDS if isinstance(g, int) and g == 0 else POOL_ADDS


def states(step, ahead):
    first = sum(UNITS[:step])
    return range(first, first + UNITS[step]) if ahead else range(0)

LN_PARTS = (1, 1, 2)


def ln_var(k):
    return 2 * TT // LN_PARTS[k] + 2


def ln_out(k):
    return 3 * TT // LN_PARTS[k] + 6


CONV_N = KD * TAPS
SPLITS = HP + MT
SP_M, SP_DT, SP_N = 1, 12, 13
SMALL = 1 / 64
SPLIT_N = 4
UNIT_N = 4
TAIL_YT, TAIL_X1, TAIL_N = 2, 4, 4
KV_N = 5
PROD_N = 2 * QT
SM_MAX, SM_N = 1, 2
FOLDS = 4
SLOTS = 3
ADD_LAG = 2
FIRST_ADDS = (1, 3, 5, 7, 9, 11, 13)
POOL_ADDS = (1, 2)
DOWN_LAG = 7
GATE_N = 29
FFN_N = 2


def before(g, per, s, depth):
    return g * per + max(0, s + 1 - depth)


CREDIT = {"sync": {"out_done": 16},
          "tensor": dict.fromkeys(["pe_hu", "pe_ctx", "pe_sc", "pe_w2", "pe_qp", "pe_at", "pe_comb",
                                   "pe_qb"], 1),
          "scalar": dict.fromkeys(["act_g", "act_hq", "act_b", "act_c"], 1),
          "gpsimd": dict.fromkeys(["w_lo", "pool_at", "pool_act", "pool_hc", "kv"], 1),
          "vector": dict.fromkeys(["x2_ready", "ffn", "unit", "tail", "y_add"], 1)}
CREDIT_OF = {name: c for names in CREDIT.values() for name, c in names.items()}


class Sems(dict):

    def at(self, name, n):
        return self[name], n + CREDIT_OF.get(name, 0)


class Steps:

    def __init__(self, eng, s, name, per):
        self.eng, self.s, self.name, self.per, self.k, self.base = eng, s, name, per, 0, 0

    def start(self, round_):
        assert self.k in (0, self.per), (self.k, self.per)
        self.base, self.k = round_ * self.per, 0
        return self

    def mark(self, instruction):
        self.k += 1
        instruction.then_inc(self.s[self.name], 1)

    def at(self, k):
        return self.s.at(self.name, self.base + k)

    def link(self, instruction):
        self.mark(instruction)
        self.eng.wait_ge(*self.at(self.k))


def build(nc, a, out):
    f32, f32r, bf16 = mybir.dt.float32, mybir.dt.float32r, mybir.dt.bfloat16
    ALU, ACT, AX = mybir.AluOpType, mybir.ActivationFunctionType, mybir.AxisListType
    ctx = ExitStack()
    with ctx:
        def sb(name, shape, dt=f32):
            return ctx.enter_context(nc.sbuf_tensor(name, shape, dt))

        def sem(name):
            return ctx.enter_context(nc.semaphore(name))

        ident = sb("ident", [P, P])
        sel_bc = sb("sel_bc", [96, 2 * NS, P], bf16)
        sel_comb = sb("sel_comb", [96, MT, P], bf16)
        rope_q = sb("rope_q", [P, 2, QT, SEQ])
        rope_k = sb("rope_k", [P, 2, DC])
        conv_w = sb("conv_w", [P, KD, TAPS])
        vecs = sb("vecs", [P, 3, KD])
        conv_b, dt_b, d_par = vecs[:, 0, :], vecs[:, 1, :], vecs[:, 2, :]
        a_neg = sb("a_neg", [P, KD, NS])
        xp_dt = sb("xp_dt", [P, KD, RANK])
        xp_bc = sb("xp_bc", [P, KD, 96])
        dtw = sb("dtw", [RANK, D])
        gate_w = sb("gate_w", [P, KD, E])
        gate_hi, gate_lo = sb("gate_hi", [P, KD, E], f32r), sb("gate_lo", [P, KD, E], f32r)
        prio = sb("prio", [P, E])
        minus_half = sb("minus_half", [P, TT])
        wf = sb("wf", [P, KD, H * DQ])
        n_mat = sb("n_mat", [P, HP, 2, 4, DC])
        u_mat = sb("u_mat", [P, HP, D])
        w2 = sb("w2", [P, RING2, D])
        w13 = sb("w13", [P, RING, 2, KD, P])

        w_hi, w_lo = (sb(name, [P, 2, KD * QT * P], f32r) for name in ("w_hi", "w_lo"))

        x_raw = sb("x_raw", [P, TT, D])
        x1 = sb("x1", [P, TT, D])
        x2 = sb("x2", [P, TT, D])
        ln_stats = [sb(f"ln_stats{k}", [P, TT, 6]) for k in range(3)]
        ln_mv = [sb(f"ln_mv{k}", [P, TT, 2]) for k in range(3)]
        ln_s = [sb(f"ln_s{k}", [P, 3, TT]) for k in range(3)]

        conv_in = sb("conv_in", [P, KD, NB, SEQ + TAPS - 1])
        xc = sb("xc", [P, KD, GT])
        dt_ = sb("dt", [P, KD, GT])
        u = sb("u", [P, KD, GT])
        da = sb("da", [P, 2, KD, GT])
        v = sb("v", [P, KD, GT])
        h = sb("h", [P, SLOTS, KD, GT])
        y = sb("y", [P, KD, GT])
        b_sb = sb("b_sb", [P, 2, GT])
        c_sb = sb("c_sb", [P, 2, GT])
        bc_parts = sb("bc_parts", [96, GT], bf16)
        xn1 = v[:, :, :].rearrange("p k t -> p (k t)").rearrange("p (t d) -> p t d", t=TT)
        acc = v
        th_c = h[:, 1]
        dt_raw = b_sb[:, 0, :]
        bc_hi = c_sb[0:96, 0, 0:GT // 2].bitcast(bf16)
        bc_r = b_sb[0:96, 1, :]
        zs = y[:, :, :]
        sp_e = h[:, 0]
        sp_ln = v
        sp_c = h[:, 1]
        yt = v
        xn2 = h[:, 0].rearrange("p k t -> p (k t)").rearrange("p (t d) -> p t d", t=TT)

        x_hi, x_lo = sb("x_hi", [P, KD, GT], f32r), sb("x_lo", [P, KD, GT], f32r)
        kr = sb("kr", [P, NB, DC])
        bd = sb("bd", [P, NB, P])
        kb = sb("kb", [P, NB, P])

        region = sb("region", [P, REGION])
        at = [0]

        def part(n, start=None):
            if start is not None:
                at[0] = start
            s = region[:, at[0]:at[0] + n]
            at[0] += n
            assert at[0] <= REGION, at[0]
            return s

        wq_in = part(H * D, 0).rearrange("p (h d) -> p h d", h=H)
        wkq_in = part(H * DQ).rearrange("p (h d) -> p h d", h=H)
        wo_in = part(H * D, 0).rearrange("p (h d) -> p h d", h=H)
        wkv_in = part(H * DC).rearrange("p (h d) -> p h d", h=H)
        wkr_in = part(H * DC).rearrange("p (h d) -> p h d", h=H)
        wqr_in = part(H * DQ).rearrange("p (h d) -> p h d", h=H)
        prod = part(QT * 2 * GT, 0).rearrange("p (t c n) -> p t c n", t=QT, c=2)
        ctx_t = part(HP * GT).rearrange("p (h n) -> p h n", h=HP)
        qp = part(GT)
        sh = part(GT).rearrange("p (g l) -> p g l", l=SEQ)
        ex = part(GT).rearrange("p (g l) -> p g l", l=SEQ)
        at_t = part(GT).rearrange("p (b s) -> p b s", b=NBP)
        kr_t = part(NB * DC, REGION - NB * DC).rearrange("p (b c) -> p b c", c=DC)
        sm_s = sb("sm_s", [P, 3, NB])
        act_h = part(MT * GT, 0).rearrange("p (m n) -> p m n", m=MT)
        th_f = part(2 * GT).rearrange("p (k n) -> p k n", k=2)
        xn3 = region[:, 0:TT * D].rearrange("p (t d) -> p t d", t=TT)
        gw = part(2 * GT).rearrange("p (k n) -> p k n", k=2)
        gt = [sb(f"gt{k}", [P, TT, E]) for k in range(7)]
        g_s = sb("g_s", [P, 8, TT])
        g_bf = sb("g_bf", [P, 2, TT, E], bf16)
        comb = sb("comb", [P, TT, 96])
        comb_t = sb("comb_t", [96, GT], bf16)

        bank = [ctx.enter_context(nc.psum_tensor(f"bank{i}", [P, GT], f32)) for i in range(8)]
        dtc_ps, bc_ps = bank[0], bank[1]
        q_ps, r2, r3 = [bank[3], bank[4], bank[5]], bank[6], bank[7]
        x3_ps = [bank[5], bank[6]]
        w2_ps = [bank[2], bank[6]]
        x1_ps = tail_ps = [bank[0], bank[1]]
        z_ps = [bank[2], bank[0]]

        def hu_ps(use):
            return bank[(3, 4, 5, 6, 2)[use]] if use < 5 else bank[3 + (use - 5) % 3]

        names = """ld_ident ld_const ld_mix ld_prep1 ld_prep2 ld_x ld_c ld_w13_0 ld_w13_1 ld_w2_0 ld_w2_1 ld_w2_2 out_done
            gate_split w_hi w_lo hq_lo x3_lo
            mem_set a_ready conv_scaled ln1 ln2 ln3 pow1 pow2 pow3
            pe_x1t act_conv_in conv act_tanh xc_ready pe_proj act_dt_raw act_bc_hi act_bc_part bc_split
            pe_z act_z softplus act_e act_ln pe_b pe_c act_c act_b act_da unit pool_hc y_add
            tail pe_yt pe_x2t act_hq
            kv pe_kv act_kb pe_qb prod_done pe_qp act_qp pe_sc softmax act_ex pool_at pe_at act_at pe_ctx
            act_ctx pe_wo x2_ready pe_x3t act_x3t pe_logit act_ge gate pe_comb act_comb pe_hu pe_g act_tf
            ffn act_g pool_act pe_w2 pe_prep1 pe_prep2 pe_prep3 prep1_out prep2_out prep3_out""".split()
        s = Sems((n, sem(n)) for n in names)

        def split_of(n):
            if n < HP:
                wide = KD * QT * P
                views = [w[:, n % 2, 0:wide].rearrange("p (k c) -> p k c", k=KD) for w in (w_lo, w_hi)]
                return *views, wf[:, :, n * QT * P:(n + 1) * QT * P]
            wide = 2 * KD * P
            views = [w[:, n % 2, 0:wide].rearrange("p (w k c) -> p w k c", w=2, k=KD) for w in (w_lo, w_hi)]
            return *views, w13[:, (n - HP) % RING]

        block = ctx.enter_context(nc.Block())

        LN_SEM = [("ln1", "pow1"), ("ln2", "pow2"), ("ln3", "pow3")]

        @block.sync
        def _(sp):
            for name, c in CREDIT["sync"].items():
                sp.sem_inc(s[name], c)
            def load(name, dst, src):
                sp.dma_start(dst, src).then_inc(s[name], 16)

            def load_x(g):
                sp.wait_ge(*s.at("tail", g * TAIL_N))
                load("ld_x", x_raw[:, :, :], a["x"][bass.ds(g * GT, GT), :].rearrange("(n p) d -> p n d", p=P))

            def load_ctx(g):
                sp.wait_ge(*s.at("kv", g * KV_N))
                src = a["ctx"][bass.ds(g * GT, GT), :].rearrange("(b l) d -> l b d", l=SEQ)
                for dup in range(2):
                    load("ld_c", kr[dup * SEQ:(dup + 1) * SEQ, :, :], src)

            def load_w2(g, m):
                sp.wait_ge(*s.at("pe_w2", before(g, MT, m, RING2)))
                load(f"ld_w2_{m % RING2}", w2[:, m % RING2], a["w2"][m])

            def stream_ffn(g):
                for m in range(MT):
                    last = HP + m - RING + 1 if m >= RING else 0
                    sp.wait_ge(*s.at("w_lo", g * SPLITS + last))
                    load(f"ld_w13_{m % RING}", w13[:, m % RING], a["w13"][m])
                    if m >= DOWN_LAG:
                        load_w2(g, m - DOWN_LAG)
                for m in range(MT - DOWN_LAG, MT):
                    load_w2(g, m)

            load_x(0)
            load("ld_ident", ident[:, :], a["ident"])
            load("ld_mix", conv_w[:, :, :], a["conv_w"])
            load("ld_mix", vecs[:, :, :], a["vecs"])
            load("ld_mix", a_neg[:, :, :], a["a_log"])
            load("ld_mix", xp_dt[:, :, :], a["xp_dt"])
            load("ld_mix", xp_bc[:, :, :], a["xp_bc"])
            load("ld_mix", dtw[:, :], a["dtw"])
            load("ld_mix", sel_bc[:, :, :], a["sel_bc"])
            load("ld_const", rope_k[:, :, :], a["rope_k"])
            load("ld_const", rope_q[:, :, :, :], a["rope_q"])
            load("ld_const", sel_comb[:, :, :], a["sel_comb"])
            load("ld_const", gate_w[:, :, :], a["gate_w"])
            load("ld_const", prio[:, :], a["prio"])
            load_ctx(0)
            load("ld_prep1", wq_in, a["wq"])
            load("ld_prep1", wkq_in, a["wkq"])
            sp.wait_ge(*s.at("pe_prep1", H))
            sp.wait_ge(*s.at("kv", KV_N))
            load("ld_prep2", wo_in, a["wo"])
            load("ld_prep2", wkv_in, a["wkv"])
            load("ld_prep2", wkr_in[0:R], a["wkr"])
            load("ld_prep2", wkr_in[R:2 * R], a["wkr"])
            load("ld_prep2", wqr_in, a["wqr"])

            def store(g):
                sp.wait_ge(*s.at("x2_ready", (g + 1) * 4))
                sp.dma_start(out[bass.ds(g * GT, GT), :].rearrange("(n p) d -> p n d", p=P),
                             x2[:, :, :]).then_inc(s["out_done"], 16)

            load_x(1)
            with sp.Fori(0, NG - 2) as i:
                load_ctx(i + 1)
                stream_ffn(i)
                load_x(i + 2)
                store(i)
            load_ctx(NG - 1)
            stream_ffn(NG - 2)
            store(NG - 2)
            stream_ffn(NG - 1)
            store(NG - 1)
            sp.wait_ge(*s.at("out_done", 16 * NG))

        @block.gpsimd
        def _(pool):
            for name, c in CREDIT["gpsimd"].items():
                pool.sem_inc(s[name], c)
            for k, (t, val) in enumerate([
                    (conv_in[:, :, :, 0:TAPS - 1], 0.0),
                    (minus_half[:, :], -0.5),
                    (bd[0:SEQ, :, SEQ:], 0.0), (bd[SEQ:, :, 0:SEQ], 0.0),
                    (da[:, :, :, 0:GT:SEQ], 0.0),
                    (n_mat[:, :, :, 1:3, :], 0.0),
                    (comb[:, :, :], 0.0)]):
                nc.gpsimd.memset(t, val).then_inc(s["mem_set"], 1)
                pool.wait_ge(*s.at("mem_set", k + 1))
            nc.gpsimd.memset(comb[:, :, E:E + 1], 0.5).then_inc(s["mem_set"], 1)
            pool.wait_ge(*s.at("mem_set", 8))

            def rstd(k, g):
                dve_sem, pool_sem = LN_SEM[k]
                for part_ in range(LN_PARTS[k]):
                    ts = slice(part_ * TT // LN_PARTS[k], (part_ + 1) * TT // LN_PARTS[k])
                    pool.wait_ge(*s.at(dve_sem, (g * LN_PARTS[k] + part_) * ln_out(k) + ln_var(k)))
                    nc.gpsimd.tensor_tensor(ln_s[k][:, 1, ts], ln_s[k][:, 0, ts], minus_half[:, ts],
                                            ALU.pow).then_inc(s[pool_sem], 1)

            kv = Steps(pool, s, "kv", KV_N)

            def rope_keys(g):
                kv.start(g)
                pool.wait_ge(*s.at("ld_c", (g + 1) * 32))
                pool.wait_ge(*s.at("pe_ctx", g * HP))
                cos = rope_k[:, 0:1, :].to_broadcast([P, NB, DC])
                for lo in (0, DC // 2):
                    hi = DC // 2 - lo
                    kv.mark(nc.gpsimd.tensor_tensor(
                        kr_t[:, :, lo:lo + DC // 2], kr[:, :, hi:hi + DC // 2],
                        rope_k[:, 1:2, lo:lo + DC // 2].to_broadcast([P, NB, DC // 2]), ALU.mult))
                pool.wait_ge(*kv.at(2))
                kv.link(nc.gpsimd.tensor_tensor(kr[:, :, :], kr[:, :, :], cos, ALU.mult))
                for rows, cols in ((slice(0, SEQ), slice(0, DC)), (slice(SEQ, P), slice(DC, P))):
                    kv.link(nc.gpsimd.tensor_tensor(bd[rows, :, cols], kr[rows], kr_t[rows], ALU.add))

            def unit(g, n):
                last = n - ADD_LAG
                if last in pool_adds(g):
                    pool.wait_ge(*s.at("pool_hc", g * NS + last + 1))
                    pool.wait_ge(*s.at("y_add", g * (NS - 1) + last - 1))
                    nc.gpsimd.tensor_tensor(y[:, :, :], y[:, :, :], h[:, last % SLOTS],
                                            ALU.add).then_inc(s["y_add"], 1)
                pool.wait_ge(*s.at("unit", (g * NS + n) * UNIT_N + 4))
                pool.wait_ge(*s.at("act_c", g * NS + n + 1))
                if n == 0:
                    pool.wait_ge(*s.at("tail", g * TAIL_N))
                c = c_sb[:, n % 2:n % 2 + 1, :].to_broadcast([P, KD, GT])
                nc.gpsimd.tensor_tensor(h[:, n % SLOTS] if n else y[:, :, :], h[:, n % SLOTS], c,
                                        ALU.mult).then_inc(s["pool_hc"], 1)

            def norm(g, p):
                n = g * HP + p
                pool.wait_ge(*s.at("softmax", n * SM_N + SM_N))
                pool.wait_ge(*s.at("pe_at", n))
                inv = sm_s[:, 2, :].unsqueeze(2).to_broadcast([P, NB, SEQ])
                nc.gpsimd.tensor_tensor(sh, ex, inv, ALU.mult).then_inc(s["pool_at"], 1)

            def ffn_tile(g, m):
                n = g * MT + m
                pool.wait_ge(*s.at("ffn", (n + 1) * FFN_N))
                pool.wait_ge(*s.at("act_g", n + 1))
                nc.gpsimd.tensor_tensor(act_h[:, m, :], th_f[:, m % 2, :], gw[:, m % 2, :],
                                        ALU.mult).then_inc(s["pool_act"], 1)

            rstd(0, 0)
            def split_lo(g, n):
                pool.wait_ge(*s.at("w_hi", g * SPLITS + n + 1))
                lo, hi, src = split_of(n)
                nc.gpsimd.tensor_tensor(lo, src, hi.bitcast(f32), ALU.subtract).then_inc(s["w_lo"], 1)

            pool.wait_ge(*s.at("ld_const", 80))
            rope_keys(0)
            for n in range(NS):
                unit(0, n)
            rstd(1, 0)
            split_lo(0, 0)
            split_lo(0, 1)
            rstd(0, 1)

            def body(g, ahead, further):
                for p in range(HP):
                    norm(g, p)
                    split_lo(g, p + 2)
                    for n in states(p, ahead):
                        unit(g + 1, n)
                rstd(2, g)
                for n in states(HP, ahead):
                    unit(g + 1, n)
                if ahead:
                    rope_keys(g + 1)
                for m in range(MT):
                    if m + 2 < MT:
                        split_lo(g, HP + m + 2)
                    ffn_tile(g, m)
                    for n in states(HP + 1 + m, ahead):
                        unit(g + 1, n)
                if ahead:
                    rstd(1, g + 1)
                    split_lo(g + 1, 0)
                    split_lo(g + 1, 1)
                    if further:
                        rstd(0, g + 2)

            with pool.Fori(0, NG - 2) as i:
                body(i, True, True)
            body(NG - 2, True, False)
            body(NG - 1, False, False)

        @block.scalar
        def _(act):
            for name, c in CREDIT["scalar"].items():
                act.sem_inc(s[name], c)
            def evict(dst, src, name):
                nc.scalar.activation(dst, src, ACT.Copy).then_inc(s[name], 1)

            act.wait_ge(*s.at("ld_mix", 7 * 16))
            nc.scalar.activation(a_neg[:, :, :], a_neg[:, :, :], ACT.Exp).then_inc(s["a_ready"], 1)

            def front_conv_in(g):
                act.wait_ge(*s.at("pe_x1t", g + 1))
                for k in range(KD):
                    evict(conv_in[:, k, :, TAPS - 1:], x1_ps[k][:, :].rearrange("p (b t) -> p b t", b=NB),
                          "act_conv_in")

            def front_tanh(g):
                act.wait_ge(*s.at("conv", (g + 1) * CONV_N))
                nc.scalar.activation(th_c, acc[:, :, :], ACT.Tanh).then_inc(s["act_tanh"], 1)

            def front_proj(g):
                act.wait_ge(*s.at("pe_proj", 2 * g + 1))
                evict(dt_raw, dtc_ps[:, :], "act_dt_raw")
                act.wait_ge(*s.at("pe_proj", 2 * g + 2))
                evict(bc_hi, bc_ps[0:96, :], "act_bc_hi")
                evict(bc_parts[0:32, :], bc_ps[0:32, :], "act_bc_part")

            def front_z(g):
                act.wait_ge(*s.at("pe_z", g + 1))
                for k in range(KD):
                    nc.scalar.activation(zs[:, k, :], z_ps[k][:, :], ACT.Identity,
                                         bias=dt_b[:, k:k + 1]).then_inc(s["act_z"], 1)

            def front_log(g):
                act.wait_ge(*s.at("softplus", g * SP_N + SP_M))
                nc.scalar.activation(sp_e[:, :, :], sp_e[:, :, :], ACT.Exp).then_inc(s["act_e"], 1)
                act.wait_ge(*s.at("act_e", g + 1))
                nc.scalar.activation(sp_ln[:, :, :], sp_e[:, :, :], ACT.Ln, bias=1.0).then_inc(s["act_ln"], 1)

            def decay(g, n):
                act.wait_ge(*s.at("unit", before(g, NS, n, 2) * UNIT_N))
                act.wait_ge(*s.at("softplus", g * SP_N + SP_DT))
                for k in range(KD):
                    dst = da[:, n % 2, k, :].rearrange("p (b t) -> p b t", b=NB)[:, :, 1:]
                    src = dt_[:, k, :].rearrange("p (b t) -> p b t", b=NB)[:, :, 1:]
                    nc.scalar.activation(dst, src, ACT.Exp, scale=a_neg[:, k, n:n + 1]).then_inc(s["act_da"], 1)

            def take_b(g, n):
                act.wait_ge(*s.at("pe_b", g * NS + n + 1))
                act.wait_ge(*s.at("unit", before(g, NS, n, 2) * UNIT_N))
                evict(b_sb[:, n % 2, :], bc_ps[:, :], "act_b")

            def take_c(g, n):
                act.wait_ge(*s.at("pe_c", g * NS + n + 1))
                act.wait_ge(*s.at("pool_hc", before(g, NS, n, 2)))
                evict(c_sb[:, n % 2, :], dtc_ps[:, :], "act_c")

            def fetch(g, n):
                take_b(g, n)
                decay(g, n)
                take_c(g, n)

            def split_hi(g, n):
                if n >= HP:
                    m = n - HP
                    slot = m % RING
                    act.wait_ge(*s.at(f"ld_w13_{slot}", (g * len(range(slot, MT, RING)) + m // RING + 1) * 16))
                if n < 2:
                    act.wait_ge(*s.at("pe_hu", g * MT))
                elif n < HP + 2:
                    act.wait_ge(*s.at("pe_qb", (g * HP + n - 1) * QT))
                else:
                    act.wait_ge(*s.at("pe_hu", g * MT + n - HP - 1))
                _, hi, src = split_of(n)
                evict(hi, src, "w_hi")

            def tail_hq(g):
                act.wait_ge(*s.at("pe_x2t", g + 1))
                act.wait_ge(*s.at("pe_hu", g * MT))
                for k in range(KD):
                    evict(x_hi[:, k, :], tail_ps[k][:, :], "act_hq")

            def keys(g):
                act.wait_ge(*s.at("pe_kv", g + 1))
                act.wait_ge(*s.at("pe_sc", g * HP))
                for k, b in enumerate((q_ps[1], r3)):
                    evict(kb[:, 4 * k:4 * k + 4, :], b[:, :].rearrange("p (b c) -> p b c", c=P), "act_kb")

            def pair_qp(g, p):
                n = g * HP + p
                act.wait_ge(*s.at("pe_qp", n + 1))
                act.wait_ge(*s.at("pe_sc", n))
                evict(qp, r2[:, :], "act_qp")

            def pair_at(g, p):
                n = g * HP + p
                act.wait_ge(*s.at("pe_at", n + 1))
                act.wait_ge(*s.at("pe_ctx", n))
                evict(at_t, r3[:, :].rearrange("p (b s) -> p b s", b=NBP), "act_at")

            def pair_exp(g, p):
                n = g * HP + p
                act.wait_ge(*s.at("softmax", n * SM_N + SM_MAX))
                act.wait_ge(*s.at("pool_at", n))
                for b in range(NB):
                    nc.scalar.activation(ex[:, b, :], r2[:, b * SEQ:(b + 1) * SEQ], ACT.Exp,
                                         bias=sm_s[:, 0, b:b + 1],
                                         accum_out=sm_s[:, 1, b:b + 1]).then_inc(s["act_ex"], 1)

            def pair_ctx(g, p):
                n = g * HP + p
                act.wait_ge(*s.at("pe_ctx", n + 1))
                if p == 0:
                    act.wait_ge(*s.at("pe_w2", g * MT))
                evict(ctx_t[:, p, :], r3[:, :], "act_ctx")

            def ffn_tile(g, m):
                n = g * MT + m
                act.wait_ge(*s.at("pe_hu", n + 1))
                act.wait_ge(*s.at("pool_act", before(g, MT, m, 2)))
                nc.scalar.activation(th_f[:, m % 2, :], hu_ps(2 * m)[:, :], ACT.Tanh,
                                     scale=0.5).then_inc(s["act_tf"], 1)

            def ffn_gate(g, m):
                n = g * MT + m
                act.wait_ge(*s.at("pe_g", n + 1))
                act.wait_ge(*s.at("pool_act", before(g, MT, m, 2)))
                evict(gw[:, m % 2, :], r3[:, :], "act_g")

            act.wait_ge(*s.at("a_ready", 1))
            nc.scalar.mul(a_neg[:, :, :], a_neg[:, :, :], -1.0).then_inc(s["a_ready"], 1)
            act.wait_ge(*s.at("a_ready", 2))
            front_conv_in(0)
            front_tanh(0)
            front_proj(0)
            front_z(0)
            front_log(0)
            def fold_query(hd):
                act.wait_ge(*s.at("pe_prep1", hd + 1))
                for k in range(KD):
                    evict(wf[:, k, hd * DQ:(hd + 1) * DQ], bank[3 + hd % 2][:, k * DQ:(k + 1) * DQ], "prep1_out")

            def fold_pair(p):
                act.wait_ge(*s.at("pe_prep2", p + 1))
                for c in range(2):
                    src = bank[3 + 2 * c + p % 2][:, 0:4 * DC].rearrange("p (b d) -> p b d", b=4)
                    evict(n_mat[:, p, c, 0:4:3, :], src[:, 0:4:3, :], "prep2_out")
                    for b, rows in ((1, slice(0, SEQ)), (2, slice(SEQ, P))):
                        evict(n_mat[rows, p, c, b, :], src[rows, b, :], "prep2_out")
                act.wait_ge(*s.at("pe_prep3", p + 1))
                evict(u_mat[:, p, :], bank[7][:, 0:D], "prep3_out")

            act.wait_ge(*s.at("ld_const", 80))
            evict(gate_hi[:, :, :], gate_w[:, :, :], "gate_split")
            act.wait_ge(*s.at("mem_set", 8))
            fetch(0, 0)
            for n in range(NS):
                for hd in range(FOLDS * n, min(FOLDS * n + FOLDS, H)):
                    fold_query(hd)
                if n >= NS // 2:
                    fold_pair(n - NS // 2)
                if n + 1 < NS:
                    fetch(0, n + 1)
            split_hi(0, 0)
            split_hi(0, 1)
            tail_hq(0)
            keys(0)

            def body(g, ahead):
                if ahead:
                    front_conv_in(g + 1)
                for p in range(HP):
                    now = states(p, ahead)
                    pair_qp(g, p)
                    if ahead and p == 0:
                        front_tanh(g + 1)
                    if ahead and p == 1:
                        front_z(g + 1)
                    for n in now[:1]:
                        take_b(g + 1, n)
                    if p:
                        pair_at(g, p - 1)
                    for n in now[:1]:
                        take_c(g + 1, n)
                    pair_exp(g, p)
                    if ahead and p == LOG_AT:
                        front_log(g + 1)
                    split_hi(g, p + 2)
                    for n in now[:1]:
                        decay(g + 1, n)
                    for n in now[1:]:
                        take_b(g + 1, n)
                    if p:
                        pair_ctx(g, p - 1)
                    for n in now[1:]:
                        take_c(g + 1, n)
                        decay(g + 1, n)
                    if ahead and p == 0:
                        front_proj(g + 1)
                pair_at(g, HP - 1)
                pair_ctx(g, HP - 1)
                for n in states(HP, ahead):
                    fetch(g + 1, n)
                for j in range(2):
                    act.wait_ge(*s.at("pe_x3t", 2 * g + j + 1))
                    evict(x_hi[:, :, j * GT // 2:(j + 1) * GT // 2],
                          x3_ps[j][:, :].rearrange("p (k n) -> p k n", k=KD), "act_x3t")
                act.wait_ge(*s.at("pe_logit", g + 1))
                nc.scalar.activation(gt[0][:, :, :], r3[:, 0:TT * E].rearrange("p (t e) -> p t e", e=E),
                                     ACT.Exp, scale=-1.0).then_inc(s["act_ge"], 1)
                for m in range(MT):
                    now = states(HP + 1 + m, ahead)
                    if m == 1:
                        act.wait_ge(*s.at("pe_comb", g + 1))
                        evict(comb_t[:, :], r3[0:96, :], "act_comb")
                        ffn_gate(g, 0)
                    for n in now:
                        take_b(g + 1, n)
                    ffn_tile(g, m)
                    if m + 2 < MT:
                        split_hi(g, HP + m + 2)
                    if m >= 2:
                        ffn_gate(g, m - 1)
                    for n in now:
                        take_c(g + 1, n)
                        decay(g + 1, n)
                ffn_gate(g, MT - 1)
                if ahead:
                    split_hi(g + 1, 0)
                    split_hi(g + 1, 1)
                    tail_hq(g + 1)
                    keys(g + 1)

            with act.Fori(0, NG - 1) as i:
                body(i, True)
            body(NG - 1, False)

        @block.vector
        def _(dve):
            for name, c in CREDIT["vector"].items():
                dve.sem_inc(s[name], c)
            V = nc.vector


            ln = [Steps(dve, s, LN_SEM[k][0], ln_out(k)) for k in range(3)]

            def layernorm(k, g, x, xn, part_=0, meanwhile=None):
                st, mv, w = ln_stats[k], ln_mv[k], ln_s[k]
                n = g * LN_PARTS[k] + part_
                tiles = range(part_ * TT // LN_PARTS[k], (part_ + 1) * TT // LN_PARTS[k])
                ts = slice(tiles[0], tiles[-1] + 1)
                step = ln[k].start(n)
                for t in tiles:
                    step.mark(V.bn_stats(st[:, t, :], x[:, t, :]))
                dve.wait_ge(*step.at(len(tiles)))
                step.mark(V.memset(w[:, 2, ts], 0.0))
                for t in tiles:
                    step.mark(V.bn_aggr(mv[:, t, :], st[:, t, :]))
                dve.wait_ge(*step.at(2 * len(tiles) + 1))
                step.mark(V.tensor_scalar(w[:, 0, ts], mv[:, ts, 1], EPS, None, ALU.add))
                if meanwhile:
                    meanwhile()
                dve.wait_ge(*s.at(LN_SEM[k][1], n + 1))
                step.link(V.tensor_tensor(w[:, 2, ts], w[:, 1, ts], w[:, 1, ts], ALU.mult))
                step.link(V.tensor_tensor(w[:, 2, ts], w[:, 2, ts], w[:, 0, ts], ALU.mult))
                step.link(V.tensor_scalar(w[:, 2, ts], w[:, 2, ts], -0.5, 1.5, ALU.mult, ALU.add))
                step.link(V.tensor_tensor(w[:, 1, ts], w[:, 2, ts], w[:, 1, ts], ALU.mult))
                for t in tiles:
                    step.mark(V.tensor_scalar(xn[:, t, :], x[:, t, :], mv[:, t, 0:1], w[:, 1, t:t + 1],
                                              ALU.subtract, ALU.mult))

            def front_ln(g, meanwhile=None):
                dve.wait_ge(*s.at("ld_x", (g + 1) * 16))
                layernorm(0, g, x_raw, xn1, meanwhile=meanwhile)

            conv = Steps(dve, s, "conv", CONV_N)

            def front_conv(g):
                conv.start(g)
                dve.wait_ge(*s.at("act_conv_in", (g + 1) * KD))
                for j in range(TAPS):
                    for k in range(KD):
                        o = acc[:, k, :].rearrange("p (b t) -> p b t", b=NB)
                        i_ = conv_in[:, k, :, j:j + SEQ]
                        if j:
                            dve.wait_ge(*conv.at(KD * (j - 1) + k + 1))
                            conv.mark(V.scalar_tensor_tensor(out=o, in0=i_, scalar=conv_w[:, k, j:j + 1], in1=o,
                                                             op0=ALU.mult, op1=ALU.add))
                        else:
                            conv.mark(V.tensor_scalar(o, i_, conv_w[:, k, 0:1], conv_b[:, k:k + 1],
                                                      ALU.mult, ALU.add))

            def front_silu(g):
                dve.wait_ge(*s.at("act_tanh", g + 1))
                V.scalar_tensor_tensor(out=xc[:, :, :], in0=th_c, scalar=1.0, in1=acc[:, :, :],
                                       op0=ALU.add, op1=ALU.mult).then_inc(s["xc_ready"], 1)

            split = Steps(dve, s, "bc_split", SPLIT_N)
            soft = Steps(dve, s, "softplus", SP_N)

            def front_split(g):
                split.start(g)
                dve.wait_ge(*s.at("act_bc_hi", g + 1))
                dve.wait_ge(*s.at("act_bc_part", g + 1))
                split.link(V.tensor_tensor(bc_r, bc_ps[0:96, :], bc_hi, ALU.subtract))
                split.mark(V.tensor_copy(bc_parts[32:64, :], bc_r[32:64, :]))
                split.link(V.tensor_copy(bc_hi[64:96], bc_r[64:96, :]))
                split.mark(V.tensor_tensor(bc_parts[64:96, :], bc_r[64:96, :], bc_hi[64:96], ALU.subtract))

            def front_abs(g):
                soft.start(g)
                dve.wait_ge(*s.at("act_z", (g + 1) * KD))
                soft.mark(V.scalar_tensor_tensor(out=sp_e[:, :, :], in0=zs, scalar=-1.0, in1=zs,
                                                 op0=ALU.mult, op1=ALU.min))

            def front_log1p(g):
                dve.wait_ge(*s.at("act_e", g + 1))
                soft.link(V.tensor_scalar(sp_c, sp_e[:, :, :], 1.0, -1.0, ALU.add, ALU.add))
                soft.link(V.tensor_tensor(sp_c, sp_e[:, :, :], sp_c, ALU.subtract))
                dve.wait_ge(*s.at("act_ln", g + 1))
                soft.link(V.tensor_tensor(sp_c, sp_ln[:, :, :], sp_c, ALU.add))
                e, series = sp_e[:, :, :], u[:, :, :]
                soft.link(V.tensor_scalar(series, e, -1 / 4, 1 / 3, ALU.mult, ALU.add))
                soft.link(V.tensor_tensor(series, series, e, ALU.mult))

            def front_series(g):
                e, series = sp_e[:, :, :], u[:, :, :]
                for c in (-1 / 2, 1.0):
                    soft.link(V.scalar_tensor_tensor(out=series, in0=series, scalar=c, in1=e,
                                                     op0=ALU.add, op1=ALU.mult))
                soft.mark(V.scalar_tensor_tensor(out=series, in0=e, scalar=SMALL, in1=series,
                                                 op0=ALU.is_lt, op1=ALU.mult))

            def front_dt(g):
                e, series = sp_e[:, :, :], u[:, :, :]
                soft.link(V.scalar_tensor_tensor(out=sp_c, in0=e, scalar=SMALL, in1=sp_c,
                                                 op0=ALU.is_ge, op1=ALU.mult))
                soft.link(V.tensor_tensor(sp_c, sp_c, series, ALU.add))
                soft.link(V.scalar_tensor_tensor(out=dt_[:, :, :], in0=zs, scalar=0.0, in1=sp_c,
                                                 op0=ALU.max, op1=ALU.add))
                soft.link(V.tensor_tensor(u[:, :, :], dt_[:, :, :], xc[:, :, :], ALU.mult))

            steps = Steps(dve, s, "unit", UNIT_N)

            def add_y(g, n):
                if n > 0 and n not in pool_adds(g):
                    dve.wait_ge(*s.at("pool_hc", g * NS + n + 1))
                    dve.wait_ge(*s.at("y_add", g * (NS - 1) + n - 1))
                    V.tensor_tensor(y[:, :, :], y[:, :, :], h[:, n % SLOTS], ALU.add).then_inc(s["y_add"], 1)

            def unit(g, n):
                steps.start(g * NS + n)
                dve.wait_ge(*s.at("act_b", g * NS + n + 1))
                b = b_sb[:, n % 2:n % 2 + 1, :].to_broadcast([P, KD, GT])
                steps.mark(V.tensor_tensor(v[:, :, :], u[:, :, :], b, ALU.mult))
                dve.wait_ge(*s.at("act_da", (g * NS + n + 1) * KD))
                d3 = da[:, n % 2].rearrange("p k (b t) -> p (k b) t", b=NB)[:, :, 1:]
                steps.mark(V.tensor_scalar(d3, d3, LOG_FLOOR, None, ALU.max))
                dve.wait_ge(*steps.at(1))
                steps.mark(V.tensor_scalar(v[:, :, :], v[:, :, :], LOG_FLOOR, None, ALU.max))
                add_y(g, n - ADD_LAG)
                dve.wait_ge(*steps.at(3))
                dve.wait_ge(*s.at("y_add", g * (NS - 1) + max(0, n - SLOTS)))
                if n == SLOTS:
                    dve.wait_ge(*s.at("pool_hc", g * NS + 1))
                steps.link(V.tensor_tensor_scan(h[:, n % SLOTS].rearrange("p k t -> p (k t)"),
                                                da[:, n % 2].rearrange("p k t -> p (k t)"),
                                                v[:, :, :].rearrange("p k t -> p (k t)"),
                                                0.0, ALU.mult, ALU.add))

            tail_s = Steps(dve, s, "tail", TAIL_N)

            def tail(g):
                tail_s.start(g)
                for n in range(NS - ADD_LAG, NS):
                    add_y(g, n)
                dve.wait_ge(*s.at("y_add", (g + 1) * (NS - 1)))
                for k in range(KD):
                    tail_s.mark(V.scalar_tensor_tensor(out=yt[:, k, :], in0=xc[:, k, :], scalar=d_par[:, k:k + 1],
                                                       in1=y[:, k, :], op0=ALU.mult, op1=ALU.add))
                dve.wait_ge(*s.at("pe_yt", g + 1))
                for j in range(2):
                    tail_s.mark(V.tensor_tensor(x1[:, 2 * j:2 * j + 2, :], x_raw[:, 2 * j:2 * j + 2, :],
                                                tail_ps[j][:, :].rearrange("p (t d) -> p t d", t=2), ALU.add))
                dve.wait_ge(*tail_s.at(TAIL_X1))
                layernorm(1, g, x1, xn2)

            def hq_lo(g):
                dve.wait_ge(*s.at("act_hq", (g + 1) * KD))
                for k in range(KD):
                    V.tensor_tensor(x_lo[:, k, :], tail_ps[k][:, :], x_hi[:, k, :].bitcast(f32),
                                    ALU.subtract).then_inc(s["hq_lo"], 1)

            def x3_lo(g, j):
                dve.wait_ge(*s.at("act_x3t", 2 * g + j + 1))
                cols = slice(j * GT // 2, (j + 1) * GT // 2)
                V.tensor_tensor(x_lo[:, :, cols], x3_ps[j][:, :].rearrange("p (k n) -> p k n", k=KD),
                                x_hi[:, :, cols].bitcast(f32), ALU.subtract).then_inc(s["x3_lo"], 1)

            def products(g, p):
                n = g * HP + p
                if p == 0:
                    dve.wait_ge(*s.at("pe_w2", g * MT))
                dve.wait_ge(*s.at("pe_qp", n))
                for t in range(QT):
                    dve.wait_ge(*s.at("pe_qb", n * QT + t + 1))
                    for c in range(2):
                        tab = rope_q[:, c, t, :].unsqueeze(1).to_broadcast([P, NB, SEQ])
                        V.tensor_tensor(prod[:, t, c, :].rearrange("p (b s) -> p b s", b=NB),
                                        q_ps[t][:, :].rearrange("p (b s) -> p b s", b=NB), tab,
                                        ALU.mult).then_inc(s["prod_done"], 1)

            sm = Steps(dve, s, "softmax", SM_N)

            def softmax_max(g, p):
                n = g * HP + p
                sm.start(n)
                dve.wait_ge(*s.at("pe_sc", n + 1))
                sc = r2[:, :].rearrange("p (g l) -> p g l", l=SEQ)
                sm.mark(V.tensor_reduce(sm_s[:, 0, :], sc, axis=AX.X, op=ALU.max, negate=True))

            def softmax_inv(g, p):
                n = g * HP + p
                dve.wait_ge(*s.at("act_ex", (n + 1) * NB))
                dve.wait_ge(*s.at("pool_at", n))
                sm.mark(V.reciprocal(sm_s[:, 2, :], sm_s[:, 1, :]))

            f = Steps(dve, s, "ffn", FFN_N)

            def ffn_tile(g, m):
                f.start(g * MT + m)
                dve.wait_ge(*s.at("act_tf", g * MT + m + 1))
                hb, ub = hu_ps(2 * m), hu_ps(2 * m + 1)
                th = th_f[:, m % 2, :]
                f.link(V.scalar_tensor_tensor(out=th, in0=th, scalar=1.0, in1=hb[:, :], op0=ALU.add, op1=ALU.mult))
                f.mark(V.tensor_tensor(th, th, ub[:, :], ALU.mult))

            gate = Steps(dve, s, "gate", GATE_N)

            def route(g):
                gate.start(g)
                tiny = lambda k: g_s[:, k, :]
                wide = lambda k: g_s[:, k, :].unsqueeze(2).to_broadcast([P, TT, E])
                pr = prio[:, :].unsqueeze(1).to_broadcast([P, TT, E])
                step, tt = gate.link, V.tensor_tensor
                dve.wait_ge(*s.at("act_ge", g + 1))
                step(V.tensor_scalar(gt[1][:, :, :], gt[0][:, :, :], 1.0, None, ALU.add))
                step(V.reciprocal(gt[2][:, :, :], gt[1][:, :, :]))
                left = gt[2]
                for k, hot in ((0, gt[3]), (1, gt[4])):
                    step(V.tensor_reduce(tiny(k), left[:, :, :], axis=AX.X, op=ALU.max))
                    step(tt(hot[:, :, :], left[:, :, :], wide(k), ALU.is_equal))
                    step(tt(hot[:, :, :], hot[:, :, :], pr, ALU.mult))
                    step(V.tensor_reduce(tiny(2), hot[:, :, :], axis=AX.X, op=ALU.max))
                    step(tt(hot[:, :, :], hot[:, :, :], wide(2), ALU.is_equal))
                    if k == 0:
                        step(V.scalar_tensor_tensor(out=gt[5][:, :, :], in0=hot[:, :, :], scalar=-2.0,
                                                    in1=left[:, :, :], op0=ALU.mult, op1=ALU.add))
                        left = gt[5]
                step(tt(tiny(3), tiny(0), tiny(1), ALU.add))
                step(V.tensor_scalar(tiny(3), tiny(3), 1e-20, None, ALU.add))
                step(V.reciprocal(tiny(4), tiny(3)))
                for k in range(2):
                    step(tt(tiny(5 + k), tiny(k), tiny(4), ALU.mult))
                    step(V.tensor_scalar(tiny(5 + k), tiny(5 + k), 1.25, None, ALU.mult))
                    step(tt(gt[3 + k][:, :, :], gt[3 + k][:, :, :], wide(5 + k), ALU.mult))
                step(tt(gt[6][:, :, :], gt[3][:, :, :], gt[4][:, :, :], ALU.add))
                step(V.tensor_copy(g_bf[:, 0], gt[6][:, :, :]))
                step(tt(gt[1][:, :, :], gt[6][:, :, :], g_bf[:, 0], ALU.subtract))
                dve.wait_ge(*s.at("pe_comb", g))
                gate_hi = V.tensor_copy(comb[:, :, 0:E], g_bf[:, 0])
                gate.mark(gate_hi)
                gate.link(V.tensor_copy(g_bf[:, 1], gt[1][:, :, :]))
                return tt

            def route_parts(g):
                gate.mark(V.tensor_copy(comb[:, :, 32:32 + E], g_bf[:, 1]))
                gate.mark(V.tensor_tensor(comb[:, :, 64:64 + E], gt[1][:, :, :], g_bf[:, 1], ALU.subtract))

            front_ln(0)
            dve.wait_ge(*s.at("ld_mix", 7 * 16))
            V.tensor_scalar(conv_w[:, :, :], conv_w[:, :, :], 0.5, None, ALU.mult).then_inc(s["conv_scaled"], 1)
            V.tensor_scalar(conv_b, conv_b, 0.5, None, ALU.mult).then_inc(s["conv_scaled"], 1)
            dve.wait_ge(*s.at("conv_scaled", 2))
            dve.wait_ge(*s.at("mem_set", 8))
            front_conv(0)
            front_silu(0)
            front_split(0)
            front_abs(0)
            front_log1p(0)
            front_series(0)
            front_dt(0)
            for n in range(NS):
                unit(0, n)
            dve.wait_ge(*s.at("gate_split", 1))
            V.tensor_tensor(gate_lo[:, :, :], gate_w[:, :, :], gate_hi[:, :, :].bitcast(f32),
                            ALU.subtract).then_inc(s["gate_split"], 1)
            tail(0)
            front_ln(1, lambda: hq_lo(0))

            front = {"split": front_split, "abs": front_abs, "log1p": front_log1p,
                     "series": front_series, "dt": front_dt}

            def body(g, ahead, further):
                products(g, 0)
                if ahead:
                    front_conv(g + 1)
                for p in range(HP):
                    softmax_max(g, p)
                    if ahead and p == 0:
                        front_silu(g + 1)
                    if p + 1 < HP:
                        products(g, p + 1)
                    softmax_inv(g, p)
                    for step in FRONT[p] if ahead else ():
                        front[step](g + 1)
                    for n in states(p, ahead):
                        unit(g + 1, n)
                dve.wait_ge(*s.at("out_done", g * 16))
                for j in range(2):
                    dve.wait_ge(*s.at("pe_wo", 2 * g + j + 1))
                    V.tensor_tensor(x2[:, 2 * j:2 * j + 2, :], x1[:, 2 * j:2 * j + 2, :],
                                    q_ps[j][:, :].rearrange("p (t d) -> p t d", t=2),
                                    ALU.add).then_inc(s["x2_ready"], 1)
                    dve.wait_ge(*s.at("x2_ready", g * 4 + j + 1))
                    layernorm(2, g, x2, xn3, j, (lambda: x3_lo(g, 0)) if j else None)
                for n in states(HP, ahead):
                    unit(g + 1, n)
                x3_lo(g, 1)
                route(g)
                route_parts(g)
                ffn_tile(g, 0)
                for m in range(MT):
                    if m:
                        ffn_tile(g, m)
                    for n in states(HP + 1 + m, ahead):
                        unit(g + 1, n)
                if ahead:
                    tail(g + 1)
                    if further:
                        front_ln(g + 2, lambda: hq_lo(g + 1))
                    else:
                        hq_lo(g + 1)
                dve.wait_ge(*s.at("pe_w2", (g + 1) * MT))
                for j, b in enumerate(w2_ps):
                    V.tensor_tensor(x2[:, 2 * j:2 * j + 2, :], x2[:, 2 * j:2 * j + 2, :],
                                    b[:, :].rearrange("p (t d) -> p t d", t=2), ALU.add).then_inc(s["x2_ready"], 1)

            with dve.Fori(0, NG - 2) as i:
                body(i, True, True)
            body(NG - 2, True, False)
            body(NG - 1, False, False)

        @block.tensor
        def _(pe):
            for name, c in CREDIT["tensor"].items():
                pe.sem_inc(s[name], c)
            mm = nc.tensor.matmul

            def group(b, pairs, name=None):
                for i_, (l, r) in enumerate(pairs):
                    last = mm(b, l, r, start=i_ == 0, stop=i_ == len(pairs) - 1)
                if name:
                    last.then_inc(s[name], 1)

            def passes(hi, lo, k, cols=slice(0, GT)):
                return [(hi, x_hi[:, k, cols]), (hi, x_lo[:, k, cols]), (lo, x_hi[:, k, cols])]

            def to_channels(xn, banks, name, tiles=range(TT)):
                for k in range(KD):
                    for t in tiles:
                        last = nc.tensor.transpose(banks[k][:, t * P:(t + 1) * P], xn[:, t, k * P:(k + 1) * P],
                                                   ident[:, :])
                last.then_inc(s[name], 1)

            def front_x1t(g, wait_lo):
                pe.wait_ge(*s.at("ln1", (g + 1) * ln_out(0)))
                pe.wait_ge(*s.at("act_hq", g * KD))
                if wait_lo:
                    pe.wait_ge(*s.at("hq_lo", g * KD))
                to_channels(xn1, x1_ps, "pe_x1t")

            def front_proj(g):
                pe.wait_ge(*s.at("xc_ready", g + 1))
                pe.wait_ge(*s.at("act_conv_in", (g + 1) * KD))
                pe.wait_ge(*s.at("act_c", g * NS))
                group(dtc_ps[:, :], [(xp_dt[:, k, :], xc[:, k, :]) for k in range(KD)], "pe_proj")
                group(bc_ps[0:96, :], [(xp_bc[:, k, :], xc[:, k, :]) for k in range(KD)], "pe_proj")

            def front_z(g):
                pe.wait_ge(*s.at("act_dt_raw", g + 1))
                for k in range(KD):
                    group(z_ps[k][:, :], [(dtw[:, k * P:(k + 1) * P], dt_raw)], "pe_z" if k == KD - 1 else None)

            def send_b(g, n):
                if n == 0:
                    pe.wait_ge(*s.at("bc_split", (g + 1) * SPLIT_N))
                pe.wait_ge(*s.at("act_b", g * NS + n))
                group(bc_ps[:, :], [(sel_bc[:, n, :], bc_parts[:, :])], "pe_b")

            def send_c(g, n):
                if n == 0:
                    pe.wait_ge(*s.at("act_z", (g + 1) * KD))
                pe.wait_ge(*s.at("act_c", g * NS + n))
                group(dtc_ps[:, :], [(sel_bc[:, NS + n, :], bc_parts[:, :])], "pe_c")

            def tail_yt(g):
                pe.wait_ge(*s.at("tail", g * TAIL_N + TAIL_YT))
                for t in range(TT):
                    for k in range(KD):
                        at_ = (t % 2) * D + k * P
                        last = nc.tensor.transpose(tail_ps[t // 2][:, at_:at_ + P], yt[:, k, t * P:(t + 1) * P],
                                                   ident[:, :])
                last.then_inc(s["pe_yt"], 1)

            def tail_x2t(g):
                pe.wait_ge(*s.at("ln2", (g + 1) * ln_out(1)))
                to_channels(xn2, tail_ps, "pe_x2t")

            def keys(g):
                pe.wait_ge(*s.at("kv", (g + 1) * KV_N))
                pe.wait_ge(*s.at("ffn", g * MT * FFN_N))
                pe.wait_ge(*s.at("act_g", g * MT))
                for b in range(NB):
                    last = nc.tensor.transpose((q_ps[1], r3)[b // 4][:, (b % 4) * P:(b % 4 + 1) * P], bd[:, b, :],
                                               ident[:, :])
                last.then_inc(s["pe_kv"], 1)

            def query(g, p):
                n = g * HP + p
                if p == 0:
                    pe.wait_ge(*s.at("hq_lo", (g + 1) * KD))
                pe.wait_ge(*s.at("w_lo", g * SPLITS + p + 1))
                lo, hi, _ = split_of(p)
                for t in range(QT):
                    if p == 0 and t == 1:
                        pe.wait_ge(*s.at("act_kb", 2 * g + 1))
                    if p:
                        pe.wait_ge(*s.at("prod_done", (n - 1) * PROD_N + 2 * t + 2))
                    c = slice(t * P, (t + 1) * P)
                    group(q_ps[t][:, :], [pair for k in range(KD) for pair in passes(hi[:, k, c], lo[:, k, c], k)],
                          "pe_qb")

            def latent_query(g, p):
                n = g * HP + p
                pe.wait_ge(*s.at("prod_done", (n + 1) * PROD_N))
                if p:
                    pe.wait_ge(*s.at("act_ex", n * NB))
                else:
                    pe.wait_ge(*s.at("x2_ready", g * 4))
                todo = [(t, c) for t in range(2) for c in range(2)]
                for i_, (t, c) in enumerate(todo):
                    for hd in range(2):
                        blk, tile = (t, t) if hd == 0 else (2 + t, 1 + t)
                        last = mm(r2[hd * DC:(hd + 1) * DC, :], n_mat[:, p, c, blk, :], prod[:, tile, c, :],
                                  start=i_ == 0, stop=i_ == len(todo) - 1)
                last.then_inc(s["pe_qp"], 1)

            def scores(g, p):
                n = g * HP + p
                pe.wait_ge(*s.at("act_qp", n + 1))
                if p == 0:
                    pe.wait_ge(*s.at("act_kb", (g + 1) * 2))
                for bp in range(NBP):
                    for o in range(2):
                        b = 2 * bp + o
                        last = mm(r2[o * SEQ:(o + 1) * SEQ, bp * P:(bp + 1) * P], qp[:, b * SEQ:(b + 1) * SEQ],
                                  kb[:, b, :], start=bp == 0, stop=bp == NBP - 1, skip_group_check=True)
                last.then_inc(s["pe_sc"], 1)

            def weights_t(g, p):
                n = g * HP + p
                pe.wait_ge(*s.at("pool_at", n + 1))
                if p:
                    pe.wait_ge(*s.at("act_ctx", n))
                w = sh.rearrange("p (b h) l -> p b (h l)", b=NBP)
                for bp in range(NBP):
                    last = nc.tensor.transpose(r3[:, bp * P:(bp + 1) * P], w[:, bp, :], ident[:, :])
                last.then_inc(s["pe_at"], 1)

            def context(g, p):
                n = g * HP + p
                pe.wait_ge(*s.at("act_at", n + 1))
                for b in range(NB):
                    last = mm(r3[:, b * SEQ:(b + 1) * SEQ], bd[:, b, :],
                              at_t[:, b // 2, (b % 2) * SEQ:(b % 2 + 1) * SEQ],
                              start=b == 0, stop=b == NB - 1, skip_group_check=True)
                last.then_inc(s["pe_ctx"], 1)

            def project(g, p, j):
                pe.wait_ge(*s.at("act_ctx", g * HP + p + 1))
                if p == 0:
                    pe.wait_ge(*s.at("prod_done", (g + 1) * HP * PROD_N))
                for t in (2 * j, 2 * j + 1):
                    last = mm(q_ps[j][:, (t % 2) * D:(t % 2 + 1) * D], ctx_t[:, p, t * P:(t + 1) * P],
                              u_mat[:, p, :], start=p == 0 and t % 2 == 0, stop=p == HP - 1,
                              skip_group_check=True)
                if p == HP - 1:
                    last.then_inc(s["pe_wo"], 1)

            def half_up(g, m, w, j):
                use = 2 * m + w
                pe.wait_ge(*s.at("w_lo", g * SPLITS + HP + m + 1))
                lo, hi, _ = split_of(HP + m)
                pe.wait_ge(*s.at("x3_lo", 2 * g + j + 1))
                if use < 2:
                    pe.wait_ge(*s.at("x2_ready", g * 4 + use + 1))
                cols = slice(j * GT // 2, (j + 1) * GT // 2)
                pairs = [pair for k in range(KD) for pair in passes(hi[:, w, k, :], lo[:, w, k, :], k, cols)]
                for i_, (l, x) in enumerate(pairs):
                    last = mm(hu_ps(use)[:, cols], l, x, start=(j, i_) == (0, 0),
                              stop=(j, i_) == (1, len(pairs) - 1), skip_group_check=True)
                if w and j:
                    last.then_inc(s["pe_hu"], 1)

            def ffn_up(g, m, w, ahead):
                use = 2 * m + w
                pe.wait_ge(*s.at("w_lo", g * SPLITS + HP + m + 1))
                lo, hi, _ = split_of(HP + m)
                if use < 5:
                    pe.wait_ge(*s.at("x3_lo", 2 * g + 2))
                    if ahead:
                        pe.wait_ge(*s.at("act_z", (g + 2) * KD))
                else:
                    last_m, last_w = divmod(use - (5 if use < 8 else 3), 2)
                    pe.wait_ge(*s.at("ffn", (g * MT + last_m) * FFN_N + last_w + 1))
                group(hu_ps(use)[:, :], [pair for k in range(KD) for pair in passes(hi[:, w, k, :], lo[:, w, k, :], k)],
                      "pe_hu" if w else None)

            def x3_rows(g, j):
                pe.wait_ge(*s.at("ln3", (g * 2 + j + 1) * ln_out(2)))
                for k in range(KD):
                    for t in range(2):
                        at_ = (2 * k + t) * P
                        last = nc.tensor.transpose(x3_ps[j][:, at_:at_ + P], xn3[:, 2 * j + t, k * P:(k + 1) * P],
                                                   ident[:, :])
                last.then_inc(s["pe_x3t"], 1)

            def logits(g, j):
                pe.wait_ge(*s.at("x3_lo", 2 * g + j + 1))
                pe.wait_ge(*s.at("act_ctx", (g + 1) * HP))
                for t in (2 * j, 2 * j + 1):
                    pairs = [pair for k in range(KD)
                             for pair in passes(gate_hi[:, k, :], gate_lo[:, k, :], k, slice(t * P, (t + 1) * P))]
                    for i_, (w, x) in enumerate(pairs):
                        last = mm(r3[:, t * E:(t + 1) * E], x, w, start=(t, i_) == (0, 0),
                                  stop=(t, i_) == (TT - 1, len(pairs) - 1), skip_group_check=True)
                if j:
                    last.then_inc(s["pe_logit"], 1)

            def ffn_gate(g, m):
                n = g * MT + m
                if m:
                    pe.wait_ge(*s.at("act_g", n))
                else:
                    pe.wait_ge(*s.at("act_comb", g + 1))
                group(r3[:, :], [(sel_comb[:, m, :], comb_t[:, :])], "pe_g")

            def ffn_down(g, m, ahead):
                n = g * MT + m
                pe.wait_ge(*s.at("pool_act", n + 1))
                slot = m % RING2
                pe.wait_ge(*s.at(f"ld_w2_{slot}", (g * len(range(slot, MT, RING2)) + m // RING2 + 1) * 16))
                if m == 0:
                    pe.wait_ge(*s.at("ffn", (g * MT + 2) * FFN_N + 1))
                for t in range(TT):
                    last = mm(w2_ps[t // 2][:, (t % 2) * D:(t % 2 + 1) * D], act_h[:, m, t * P:(t + 1) * P],
                              w2[:, slot, :], start=m == 0 and t % 2 == 0, stop=m == MT - 1, skip_group_check=True)
                last.then_inc(s["pe_w2"], 1)

            pe.wait_ge(*s.at("ld_ident", 16))
            front_x1t(0, False)
            pe.wait_ge(*s.at("ld_const", 80))
            pe.wait_ge(*s.at("ld_mix", 7 * 16))
            front_proj(0)
            front_z(0)

            def fold_query(hd):
                if hd >= 2:
                    pe.wait_ge(*s.at("prep1_out", (hd - 1) * KD))
                for k in range(KD):
                    last = mm(bank[3 + hd % 2][:, k * DQ:(k + 1) * DQ], wq_in[:, hd, k * P:(k + 1) * P],
                              wkq_in[:, hd, :], start=k == 0, stop=k == KD - 1, skip_group_check=True)
                last.then_inc(s["pe_prep1"], 1)

            def fold_pair(p):
                pe.wait_ge(*s.at("prep1_out", H * KD))
                if p >= 2:
                    pe.wait_ge(*s.at("prep2_out", (p - 1) * 6))
                for c in range(2):
                    rows = slice(c * R, (c + 1) * R)
                    wqr = wqr_in[rows, 2 * p:2 * p + 2, :].rearrange("p h q -> p (h q)")
                    for blk, (tile, hd) in enumerate(((0, 0), (1, 0), (1, 1), (2, 1))):
                        last = mm(bank[3 + 2 * c + p % 2][:, blk * DC:(blk + 1) * DC],
                                  wqr[:, tile * P:(tile + 1) * P], wkr_in[rows, 2 * p + hd, :],
                                  start=blk == 0, stop=blk == 3, skip_group_check=True)
                last.then_inc(s["pe_prep2"], 1)
                if p >= 1:
                    pe.wait_ge(*s.at("prep3_out", p))
                for hd in range(2):
                    last = mm(bank[7][hd * DC:(hd + 1) * DC, 0:D], wkv_in[:, 2 * p + hd, :],
                              wo_in[:, 2 * p + hd, :], start=True, stop=True)
                last.then_inc(s["pe_prep3"], 1)

            send_b(0, 0)
            send_c(0, 0)
            pe.wait_ge(*s.at("ld_prep1", 32))
            for n in range(NS):
                for hd in range(FOLDS * n, min(FOLDS * n + FOLDS, H)):
                    fold_query(hd)
                if n == NS // 2:
                    pe.wait_ge(*s.at("ld_prep2", 5 * 16))
                if n >= NS // 2:
                    fold_pair(n - NS // 2)
                if n + 1 < NS:
                    send_b(0, n + 1)
                    send_c(0, n + 1)
            tail_yt(0)
            tail_x2t(0)
            pe.wait_ge(*s.at("gate_split", 2))
            pe.wait_ge(*s.at("prep2_out", HP * 6))
            pe.wait_ge(*s.at("prep3_out", HP))
            keys(0)

            def body(g, ahead):
                query(g, 0)
                if ahead:
                    front_x1t(g + 1, True)
                for p in range(HP):
                    now = states(p, ahead)
                    latent_query(g, p)
                    if ahead and p == 1:
                        front_z(g + 1)
                    for n in now[:1]:
                        send_b(g + 1, n)
                    if p:
                        weights_t(g, p - 1)
                    scores(g, p)
                    for n in now[:1]:
                        send_c(g + 1, n)
                    if p + 1 < HP:
                        query(g, p + 1)
                    for n in now[1:]:
                        send_b(g + 1, n)
                    if p:
                        context(g, p - 1)
                    for n in now[1:]:
                        send_c(g + 1, n)
                    if ahead and p == 0:
                        front_proj(g + 1)
                for p in range(HP - 1):
                    project(g, p, 0)
                weights_t(g, HP - 1)
                project(g, 0, 1)
                context(g, HP - 1)
                project(g, 1, 1)
                project(g, HP - 1, 0)
                for n in states(HP, ahead):
                    send_b(g + 1, n)
                    send_c(g + 1, n)
                for p in range(2, HP):
                    if p == HP - X3_EARLY:
                        x3_rows(g, 0)
                    project(g, p, 1)
                logits(g, 0)
                first = ((0, 0), (0, 1), (1, 0))
                for m, w in first:
                    half_up(g, m, w, 0)
                x3_rows(g, 1)
                logits(g, 1)
                for m, w in first:
                    half_up(g, m, w, 1)
                for m in range(MT):
                    now = states(HP + 1 + m, ahead)
                    if m >= 2:
                        ffn_up(g, m, 0, ahead)
                    if m == 1:
                        ffn_up(g, 1, 1, ahead)
                        pe.wait_ge(*s.at("gate", (g + 1) * GATE_N))
                        for t in range(TT):
                            last = nc.tensor.transpose(r3[0:96, t * P:(t + 1) * P], comb[:, t, :], ident[:, :])
                        last.then_inc(s["pe_comb"], 1)
                        ffn_gate(g, 0)
                    for n in now:
                        send_b(g + 1, n)
                    if m >= 2:
                        ffn_up(g, m, 1, ahead)
                    if m >= 2:
                        ffn_gate(g, m - 1)
                    for n in now:
                        send_c(g + 1, n)
                    if m >= DOWN_LAG:
                        ffn_down(g, m - DOWN_LAG, ahead)
                ffn_gate(g, MT - 1)
                for m in range(MT - DOWN_LAG, MT):
                    if ahead and m == MT - DOWN_LAG + TAIL_AT[0]:
                        tail_yt(g + 1)
                    if ahead and m == MT - DOWN_LAG + TAIL_AT[1]:
                        tail_x2t(g + 1)
                    ffn_down(g, m, ahead)
                if ahead:
                    keys(g + 1)

            with pe.Fori(0, NG - 1) as i:
                body(i, True)
            body(NG - 1, False)


def rope_table(length, dim):
    inv = (1.0 / 10000.0 ** (np.arange(0, dim, 2, dtype=np.float32) / dim)).astype(np.float32)
    f = np.arange(length, dtype=np.float32)[:, None] * inv[None, :]
    return np.repeat(np.sin(f), 2, axis=-1), np.repeat(np.cos(f), 2, axis=-1)


def constants():
    sin_q, cos_q = rope_table(SEQ, DQ)
    sin_k, cos_k = rope_table(SEQ, DC)
    j = np.arange(QT * P) % DQ
    half = DQ // 2
    sin_t = (sin_q[:, (j + half) % DQ] * np.where(j < half, 1.0, -1.0)).T
    rope_q = np.stack([cos_q[:, j].T, sin_t]).reshape(2, QT, P, SEQ).transpose(2, 0, 1, 3)
    sign = np.where(np.arange(DC) < DC // 2, -1.0, 1.0)
    rope_k = np.tile(np.stack([cos_k, sin_k * sign], axis=1), (2, 1, 1))
    sel_bc = np.zeros((96, 2 * NS, P))
    sel_comb = np.zeros((96, MT * P))
    for part in range(3):
        for r in range(2 * NS):
            sel_bc[32 * part + r, r, :] = 1
        for e in range(E + 1):
            sel_comb[32 * part + e, e * HID:(e + 1) * HID] = 1
    f32 = np.float32
    return {"ident": np.eye(P, dtype=f32), "rope_q": rope_q.astype(f32), "rope_k": rope_k.astype(f32),
            "sel_bc": sel_bc.astype(np.dtype("bfloat16")),
            "sel_comb": sel_comb.reshape(96, MT, P).astype(np.dtype("bfloat16")),
            "prio": np.tile(np.arange(E, 0, -1, dtype=f32), (P, 1))}


def laid_out(x, ctx_512, L0_attn_conv_w, L0_attn_conv_b, L0_attn_x_proj_w, L0_attn_dt_proj_w, L0_attn_dt_proj_b,
             L0_attn_A_log, L0_attn_D_param, L0_xattn_Wq, L0_xattn_w_kc_q, L0_xattn_w_kc_kv, L0_xattn_W_qr,
             L0_xattn_W_kr, L0_xattn_Wo, L0_ffn_gate_w, L0_ffn_w1, L0_ffn_w2, L0_ffn_w3, L0_ffn_sw1, L0_ffn_sw2,
             L0_ffn_sw3):
    n = np.asarray

    def halves(w):
        return n(w).reshape(KD, P, -1).transpose(1, 0, 2)

    xp = halves(n(L0_attn_x_proj_w).T)
    bc = xp[:, :, RANK:]
    pad = MT * P - (E + 1) * HID

    def packed(w, sw):
        cols = np.concatenate([n(w).transpose(1, 0, 2).reshape(D, E * HID), n(sw),
                               np.zeros((D, pad), np.float32)], axis=1)
        return cols.reshape(KD, P, MT, P).transpose(2, 1, 0, 3)

    w2 = np.concatenate([n(L0_ffn_w2).reshape(E * HID, D), n(L0_ffn_sw2), np.zeros((pad, D), np.float32)])
    qr = n(L0_xattn_W_qr).transpose(2, 0, 1)
    return {
        "x": n(x).reshape(T_ALL, D), "ctx": n(ctx_512).reshape(T_ALL, DC),
        "conv_w": halves(n(L0_attn_conv_w).reshape(D, TAPS)),
        "vecs": np.stack([halves(L0_attn_conv_b)[:, :, 0], halves(L0_attn_dt_proj_b)[:, :, 0],
                          halves(L0_attn_D_param)[:, :, 0]], axis=1),
        "a_log": halves(L0_attn_A_log), "xp_dt": xp[:, :, :RANK], "xp_bc": np.concatenate([bc, bc, bc], axis=2),
        "dtw": n(L0_attn_dt_proj_w).T,
        "wq": n(L0_xattn_Wq).reshape(H, P, D).transpose(1, 0, 2), "wkq": n(L0_xattn_w_kc_q).transpose(1, 0, 2),
        "wo": n(L0_xattn_Wo).reshape(D, H, P).transpose(2, 1, 0), "wkv": n(L0_xattn_w_kc_kv).transpose(1, 0, 2),
        "wkr": n(L0_xattn_W_kr).transpose(2, 0, 1),
        "wqr": np.concatenate([qr, np.roll(qr, -(DQ // 2), axis=2)]),
        "gate_w": halves(n(L0_ffn_gate_w).T), "w2": w2.reshape(MT, P, D),
        "w13": np.stack([packed(L0_ffn_w1, L0_ffn_sw1), packed(L0_ffn_w3, L0_ffn_sw3)], axis=2),
    }


def kernel(**inputs):
    import concourse.bacc as bacc
    from concourse.bass_utils import run_bass_kernel_spmd

    arrays = {f"in_{k}": np.ascontiguousarray(v) for k, v in {**constants(), **laid_out(**inputs)}.items()}
    nc = bacc.Bacc("TRN2", target_bir_lowering=False, num_devices=1)
    aps = {k[3:]: nc.dram_tensor(k, v.shape, mybir.dt.from_np(v.dtype), kind="ExternalInput").ap()
           for k, v in arrays.items()}
    out = nc.dram_tensor("out", (T_ALL, D), mybir.dt.float32, kind="ExternalOutput").ap()
    build(nc, aps, out)
    r = run_bass_kernel_spmd(nc, [arrays], core_ids=[0])
    return r.results[0]["out"].reshape(T_ALL // SEQ, SEQ, D)
```
